# Optimizing a Trainium2 kernel written in Bass

```python
import numpy as np
import jax
import jax.numpy as jnp

def _softmax(x, axis=-1):
    return jax.nn.softmax(x, axis=axis)

def _gelu(x):
    return jax.nn.gelu(x, approximate=True)

def _silu(x):
    return jax.nn.silu(x)

def _sigmoid(x):
    return jax.nn.sigmoid(x)

def _layernorm(x, axis=-1, eps=1e-05):
    m = jnp.mean(x, axis=axis, keepdims=True)
    v = jnp.var(x, axis=axis, keepdims=True)
    return (x - m) / jnp.sqrt(v + eps)

def _scatter_add(tgt, idx, src, axis=0):
    return tgt.at[idx].add(src)

def _segment_sum(src, seg, n):
    return jax.ops.segment_sum(src, seg, n)
kernel_name = 'mk_gnn_ffn_d1_gnn_r8_590f86'

def setup_inputs(seed: int=0):
    np.random.seed(seed)
    _w = jnp.asarray

    def _rec_inputs():
        import jax
        import jax.numpy as jnp
        _gk = jax.random.key(seed)
        x = -0.0001126 + 1 * jax.random.normal(jax.random.fold_in(_gk, 1), (1250, 768), jnp.float32)
        _s = jax.random.randint(jax.random.fold_in(_gk, 2), (10000,), 0, 1250, jnp.int32)
        _d = jax.random.randint(jax.random.fold_in(_gk, 3), (10000,), 0, 1250, jnp.int32)
        _loop = jnp.arange(1250, dtype=jnp.int32)
        src = jnp.concatenate([_s, _d, _loop])
        dst = jnp.concatenate([_d, _s, _loop])
        _o = jnp.argsort(dst, stable=True)
        src = src[_o]
        dst = dst[_o]
        return (x, src, dst)
    x, src, dst = _rec_inputs()

    def _L0_gnn_setup():
        import jax, jax.numpy as jnp
        import numpy as np
        N, E, DM, H, L = (1250, 20000, 768, 8, 2)
        HD = DM // H
        LN_EPS = 1e-05
        SLOPE = 0.2

        def layer_norm(x, w, b):
            mu = jnp.mean(x, axis=-1, keepdims=True)
            var = jnp.mean(jnp.square(x - mu), axis=-1, keepdims=True)
            return (x - mu) * jax.lax.rsqrt(var + LN_EPS) * w + b

        def gatv2_layer(x, Ws, bs, Wd, bd, attn, src, dst):
            hs = (x @ Ws + bs).reshape(N, H, HD)
            hd = (x @ Wd + bd).reshape(N, H, HD)
            hs_e = hs[src]
            e = jax.nn.leaky_relu(hs_e + hd[dst], SLOPE)
            logits = jnp.einsum('ehd,hd->eh', e, attn)
            m = jax.ops.segment_max(logits, dst, num_segments=N)
            ex = jnp.exp(logits - m[dst])
            s = jax.ops.segment_sum(ex, dst, num_segments=N)
            alpha = ex / s[dst]
            out = jax.ops.segment_sum(alpha[..., None] * hs_e, dst, num_segments=N)
            return jax.nn.elu(out).reshape(N, DM)
        key = jax.random.key(seed)
        ks = jax.random.split(key, 12)
        xav = 1.0 / np.sqrt(DM)
        return {'x': jax.random.normal(ks[0], (N, DM), jnp.float32), 'Wsrc': jax.random.uniform(ks[1], (L, DM, DM), jnp.float32, -xav, xav), 'bsrc': jnp.zeros((L, DM), jnp.float32), 'Wdst': jax.random.uniform(ks[2], (L, DM, DM), jnp.float32, -xav, xav), 'bdst': jnp.zeros((L, DM), jnp.float32), 'attn': jax.random.normal(ks[3], (L, H, HD), jnp.float32) * (1.0 / np.sqrt(HD)), 'ln_w': jnp.ones((L, DM), jnp.float32), 'ln_b': jnp.zeros((L, DM), jnp.float32), 'on_w': jnp.ones((DM,), jnp.float32), 'on_b': jnp.zeros((DM,), jnp.float32), 'src': jax.random.randint(ks[4], (E,), 0, N, jnp.int32), 'dst': jax.random.randint(ks[5], (E,), 0, N, jnp.int32)}
    _L0_gnn_all = _L0_gnn_setup()
    _L0_gnn_in = {k: v for k, v in _L0_gnn_all.items() if k in ('Wsrc', 'bsrc', 'Wdst', 'bdst', 'attn', 'ln_w', 'ln_b', 'on_w', 'on_b')}
    del _L0_gnn_all

    def _L0_ffn_setup():
        import jax, jax.numpy as jnp
        import numpy as np
        DIM = 768
        HID = 512
        E = 16
        G = 8
        TOPK_G = 4
        TOPK_E = 4
        SCALE = 2.5
        B, S = (2, 256)
        key = jax.random.key(seed)
        ks = jax.random.split(key, 9)
        init = lambda k, shape: jax.random.normal(k, shape, dtype=jnp.float32) * 0.02
        z = lambda shape: jnp.zeros(shape, jnp.float32)
        return {'x': jax.random.normal(ks[0], (B, S, DIM), dtype=jnp.float32), 'gate_w': init(ks[1], (DIM, E)), 'gate_b': z((E,)), 'bias': z((E,)), 'Wu': init(ks[2], (E, DIM, HID)), 'bu': z((E, HID)), 'Wg': init(ks[3], (E, DIM, HID)), 'bg': z((E, HID)), 'Wd': init(ks[4], (E, HID, DIM)), 'bd': z((E, DIM)), 'sWu': init(ks[5], (DIM, HID)), 'sbu': z((HID,)), 'sWg': init(ks[6], (DIM, HID)), 'sbg': z((HID,)), 'sWd': init(ks[7], (HID, DIM)), 'sbd': z((DIM,))}
    _L0_ffn_all = _L0_ffn_setup()
    _L0_ffn_in = {k: v for k, v in _L0_ffn_all.items() if k in ('gate_w', 'gate_b', 'bias', 'Wu', 'bu', 'Wg', 'bg', 'Wd', 'bd', 'sWu', 'sbu', 'sWg', 'sbg', 'sWd', 'sbd')}
    del _L0_ffn_all
    return {'x': x, 'src': src, 'dst': dst, 'L0_gnn_Wsrc': _L0_gnn_in['Wsrc'], 'L0_gnn_bsrc': _L0_gnn_in['bsrc'], 'L0_gnn_Wdst': _L0_gnn_in['Wdst'], 'L0_gnn_bdst': _L0_gnn_in['bdst'], 'L0_gnn_attn': _L0_gnn_in['attn'], 'L0_gnn_ln_w': _L0_gnn_in['ln_w'], 'L0_gnn_ln_b': _L0_gnn_in['ln_b'], 'L0_gnn_on_w': _L0_gnn_in['on_w'], 'L0_gnn_on_b': _L0_gnn_in['on_b'], 'L0_ffn_gate_w': _L0_ffn_in['gate_w'], 'L0_ffn_gate_b': _L0_ffn_in['gate_b'], 'L0_ffn_bias': _L0_ffn_in['bias'], 'L0_ffn_Wu': _L0_ffn_in['Wu'], 'L0_ffn_bu': _L0_ffn_in['bu'], 'L0_ffn_Wg': _L0_ffn_in['Wg'], 'L0_ffn_bg': _L0_ffn_in['bg'], 'L0_ffn_Wd': _L0_ffn_in['Wd'], 'L0_ffn_bd': _L0_ffn_in['bd'], 'L0_ffn_sWu': _L0_ffn_in['sWu'], 'L0_ffn_sbu': _L0_ffn_in['sbu'], 'L0_ffn_sWg': _L0_ffn_in['sWg'], 'L0_ffn_sbg': _L0_ffn_in['sbg'], 'L0_ffn_sWd': _L0_ffn_in['sWd'], 'L0_ffn_sbd': _L0_ffn_in['sbd']}

def reference(x, src, dst, L0_gnn_Wsrc, L0_gnn_bsrc, L0_gnn_Wdst, L0_gnn_bdst, L0_gnn_attn, L0_gnn_ln_w, L0_gnn_ln_b, L0_gnn_on_w, L0_gnn_on_b, L0_ffn_gate_w, L0_ffn_gate_b, L0_ffn_bias, L0_ffn_Wu, L0_ffn_bu, L0_ffn_Wg, L0_ffn_bg, L0_ffn_Wd, L0_ffn_bd, L0_ffn_sWu, L0_ffn_sbu, L0_ffn_sWg, L0_ffn_sbg, L0_ffn_sWd, L0_ffn_sbd):
    import jax
    import jax.numpy as jnp

    def _L0_gnn_ref(x, Wsrc, bsrc, Wdst, bdst, attn, ln_w, ln_b, on_w, on_b, src, dst):
        import jax, jax.numpy as jnp
        import numpy as np
        N, E, DM, H, L = (1250, 20000, 768, 8, 2)
        HD = DM // H
        LN_EPS = 1e-05
        SLOPE = 0.2

        def layer_norm(x, w, b):
            mu = jnp.mean(x, axis=-1, keepdims=True)
            var = jnp.mean(jnp.square(x - mu), axis=-1, keepdims=True)
            return (x - mu) * jax.lax.rsqrt(var + LN_EPS) * w + b

        def gatv2_layer(x, Ws, bs, Wd, bd, attn, src, dst):
            hs = (x @ Ws + bs).reshape(N, H, HD)
            hd = (x @ Wd + bd).reshape(N, H, HD)
            hs_e = hs[src]
            e = jax.nn.leaky_relu(hs_e + hd[dst], SLOPE)
            logits = jnp.einsum('ehd,hd->eh', e, attn)
            m = jax.ops.segment_max(logits, dst, num_segments=N)
            ex = jnp.exp(logits - m[dst])
            s = jax.ops.segment_sum(ex, dst, num_segments=N)
            alpha = ex / s[dst]
            out = jax.ops.segment_sum(alpha[..., None] * hs_e, dst, num_segments=N)
            return jax.nn.elu(out).reshape(N, DM)
        h = x
        for l in range(L):
            h_new = gatv2_layer(h, Wsrc[l], bsrc[l], Wdst[l], bdst[l], attn[l], src, dst)
            h = layer_norm(h_new + h, ln_w[l], ln_b[l])
        return layer_norm(h, on_w, on_b)

    def _L0_ffn_ref(x, gate_w, gate_b, bias, Wu, bu, Wg, bg, Wd, bd, sWu, sbu, sWg, sbg, sWd, sbd):
        import jax, jax.numpy as jnp
        import numpy as np
        DIM = 768
        HID = 512
        E = 16
        G = 8
        TOPK_G = 4
        TOPK_E = 4
        SCALE = 2.5
        B, S = (2, 256)
        orig_shape = x.shape
        xt = x.reshape(-1, DIM)
        T = xt.shape[0]
        scores = jax.nn.softmax(xt @ gate_w + gate_b, axis=-1)
        orig_scores = jax.lax.stop_gradient(scores)
        s = scores + bias[None, :]
        s3 = s.reshape(T, G, E // G)
        group_scores = jax.lax.top_k(s3, 2)[0].sum(-1)
        gidx = jax.lax.top_k(group_scores, TOPK_G)[1]
        gmask = jnp.any(jnp.arange(G)[None, None, :] == gidx[:, :, None], axis=1)
        s_masked = jnp.where(gmask[:, :, None], s3, -jnp.inf).reshape(T, E)
        _, idx = jax.lax.top_k(s_masked, TOPK_E)
        w = jnp.take_along_axis(orig_scores, idx, axis=1) * SCALE
        w_full = jnp.zeros((T, E), xt.dtype).at[jnp.arange(T)[:, None], idx].add(w)
        up = jax.nn.silu(jnp.einsum('td,edh->teh', xt, Wu) + bu)
        gt = jnp.einsum('td,edh->teh', xt, Wg) + bg
        act = up * gt * w_full[:, :, None]
        y = jnp.einsum('teh,ehd->td', act, Wd) + w_full @ bd
        sh = jax.nn.silu(xt @ sWu + sbu) * (xt @ sWg + sbg)
        y = y + sh @ sWd + sbd
        return y.reshape(orig_shape)
    x = x + _L0_gnn_ref(_layernorm(x, axis=-1), L0_gnn_Wsrc, L0_gnn_bsrc, L0_gnn_Wdst, L0_gnn_bdst, L0_gnn_attn, L0_gnn_ln_w, L0_gnn_ln_b, L0_gnn_on_w, L0_gnn_on_b, src, dst)
    x = x + _L0_ffn_ref(_layernorm(x, axis=-1)[None], L0_ffn_gate_w, L0_ffn_gate_b, L0_ffn_bias, L0_ffn_Wu, L0_ffn_bu, L0_ffn_Wg, L0_ffn_bg, L0_ffn_Wd, L0_ffn_bd, L0_ffn_sWu, L0_ffn_sbu, L0_ffn_sWg, L0_ffn_sbg, L0_ffn_sWd, L0_ffn_sbd)[0]
    return x

_drawn_inputs = setup_inputs


def setup_inputs(seed=0):
    import zlib

    import numpy as np

    out = dict(_drawn_inputs(seed))
    spreads = {'L0_gnn_bsrc': (0.0, 0.1),
     'L0_gnn_bdst': (0.0, 0.8),
     'L0_gnn_ln_w': (1.0, 0.2),
     'L0_gnn_ln_b': (0.0, 0.1),
     'L0_gnn_on_w': (1.0, 0.2),
     'L0_gnn_on_b': (0.0, 0.1),
     'L0_ffn_gate_b': (0.0, 0.763),
     'L0_ffn_bias': (0.0, 0.275),
     'L0_ffn_bu': (0.0, 0.8),
     'L0_ffn_bg': (0.0, 0.8),
     'L0_ffn_bd': (0.0, 0.348),
     'L0_ffn_sbu': (0.0, 0.8),
     'L0_ffn_sbg': (0.0, 0.8),
     'L0_ffn_sbd': (0.0, 0.1)}
    factors = {'L0_gnn_Wdst': 3.761, 'L0_ffn_Wu': 3.278, 'L0_ffn_Wg': 3.178, 'L0_ffn_Wd': 3.13}
    for name, (base, spread) in spreads.items():
        noise = np.random.default_rng([zlib.crc32(name.encode()), seed]).standard_normal(out[name].shape)
        drawn = base * np.exp(spread * noise) if base else spread * noise
        out[name] = jnp.asarray(drawn.astype(out[name].dtype))
    for name, factor in factors.items():
        out[name] = (out[name] * factor).astype(out[name].dtype)
    return out
```

```python
from contextlib import ExitStack, contextmanager

import concourse.bass as bass
from concourse import mybir

P = 128
N = 1250
E = 21250
DM = 768
H = 8
HD = DM // H
L = 2
NT = (N + P - 1) // P
NLAST = N - (NT - 1) * P
NP = NT * P
KC = DM // P
HALF = DM // 2
HH = H // 2
HW = HALF + HH
ROW = 2 * HW
GE = 2 * P
NG = (E + NT * (GE - 1)) // GE
NG += NG % 2
NTILE = 2 * NG
TPC = P // H
NC = (NTILE + TPC - 1) // TPC
NTP = NC * TPC
SENTINEL = 4095
BIG = 1.0e30
EL = 125
EC = E // EL
SLOPE = 0.2
LN_EPS = 1e-5

F32 = mybir.dt.float32
I32 = mybir.dt.int32
BF16 = mybir.dt.bfloat16
ALU = mybir.AluOpType
ACT = mybir.ActivationFunctionType
AX = mybir.AxisListType


@contextmanager
def stage_semaphore(nc, name):
    handle = nc.alloc_semaphore(name)
    yield handle
    RETIRED.append(handle)


RETIRED = []


def recycle(nc):
    nc.clear_and_free_semaphores(list(RETIRED))
    RETIRED.clear()
    nc.all_engine_barrier()


class Chain:

    def __init__(self, eng, sem):
        self.eng, self.sem, self.n = eng, sem, 0

    def __call__(self, instruction):
        self.n += 1
        instruction.then_inc(self.sem, 1)
        self.eng.wait_ge(self.sem, self.n)


def bcast(row, parts):
    return row.rearrange("(a n) -> a n", a=1).broadcast_to([parts, row.shape[0]])


def constants(nc, K):
    with ExitStack() as ctx:
        s_zero = ctx.enter_context(stage_semaphore(nc, "identity_zeroed"))
        s_all = ctx.enter_context(stage_semaphore(nc, "constants_made"))
        block = ctx.enter_context(nc.Block())

        @block.gpsimd
        def _(pool):
            pool.memset(K.ident[:, :], 0.0).then_inc(s_zero, 1)
            pool.memset(K.ones[:, :], 1.0).then_inc(s_all, 1)
            pool.wait_ge(s_zero, 1)
            pool.affine_select(out=K.ident[:, :], in_=K.ident[:, :], compare_op=ALU.not_equal, fill=1.0,
                               base=0, pattern=[[-1, P]], channel_multiplier=1).then_inc(s_all, 1)
            pool.iota(K.iota_free[:, :], [[1, P]], base=0, channel_multiplier=0,
                      allow_small_or_imprecise_dtypes=True).then_inc(s_all, 1)
            pool.iota(K.iota_part[:, :], [[0, 1]], base=0, channel_multiplier=1,
                      allow_small_or_imprecise_dtypes=True).then_inc(s_all, 1)
            pool.wait_ge(s_all, 4)


def norm_block(nc, K, name, src, dst, weight=None, bias=None, also=None, load=None, load_to=None):
    load_to = src if load_to is None else load_to
    """dst = layernorm(src) * weight + bias over [P, NT, DM]; weight and bias are rows in every partition.

    load: DRAM [N, DM] read into src first. also: (weight2, bias2, other): dst = dst normalised once more
    with weight2/bias2 plus other."""
    with ExitStack() as ctx:
        def sem(n):
            return ctx.enter_context(stage_semaphore(nc, f"{name}_{n}"))
        loaded, stepped, dev_made, root_made = sem("loaded"), sem("stepped"), sem("deviation_made"), sem("root_made")
        stats = ctx.enter_context(nc.sbuf_tensor(f"{name}_stats", [P, NT, 2, 6], F32))
        mv = ctx.enter_context(nc.sbuf_tensor(f"{name}_mv", [P, NT, 2], F32))
        var = ctx.enter_context(nc.sbuf_tensor(f"{name}_var", [P, NT], F32))
        std = ctx.enter_context(nc.sbuf_tensor(f"{name}_std", [P, NT], F32))
        rstd = ctx.enter_context(nc.sbuf_tensor(f"{name}_rstd", [P, NT], F32))
        block = ctx.enter_context(nc.Block())

        if load is not None:
            @block.sync
            def _(sp):
                sp.wait_ge(stepped, 1)
                sp.dma_start(load_to[:, 0:NT - 1, :], load[0:(NT - 1) * P, :].rearrange("(t p) d -> p t d", p=P))\
                  .then_inc(loaded, 16)
                sp.dma_start(load_to[0:NLAST, NT - 1, :], load[(NT - 1) * P:N, :]).then_inc(loaded, 16)

        @block.vector
        def _(dve):
            step = Chain(dve, stepped)
            if load is not None:
                step(dve.memset(load_to[:, NT - 1, :], 0.0))
                dve.wait_ge(loaded, 32)

            def stats_of(x):
                for t in range(NT):
                    for h in range(2):
                        last = dve.bn_stats(stats[:, t, h, :], x[:, t, h * HALF:(h + 1) * HALF])
                step(last)
                for t in range(NT):
                    last = dve.bn_aggr(mv[:, t, :], stats[:, t, :, :].rearrange("p a b -> p (a b)"))
                step(last)

            def normalise(x, y, n):
                dve.tensor_scalar(var[:, :], mv[:, :, 1], LN_EPS, None, ALU.add).then_inc(dev_made, 1)
                dve.wait_ge(root_made, n)
                step(dve.reciprocal(rstd[:, :], std[:, :]))
                for t in range(NT):
                    last = dve.tensor_scalar(y[:, t, :], x[:, t, :], mv[:, t, 0:1], rstd[:, t:t + 1],
                                             ALU.subtract, ALU.mult)
                step(last)

            def affine(y, w, b):
                for t in range(NT):
                    last = dve.tensor_tensor(y[:, t, :], y[:, t, :], w[:, :], ALU.mult)
                step(last)
                for t in range(NT):
                    last = dve.tensor_tensor(y[:, t, :], y[:, t, :], b[:, :], ALU.add)
                step(last)

            stats_of(src)
            normalise(src, dst, 1)
            if weight is not None:
                affine(dst, weight, bias)
            if also is not None:
                w2, b2, other = also
                stats_of(dst)
                normalise(dst, dst, 2)
                affine(dst, w2, b2)
                for t in range(NT):
                    last = dve.tensor_tensor(dst[:, t, :], dst[:, t, :], other[:, t, :], ALU.add)
                step(last)

        @block.scalar
        def _(act):
            for n in range(1 if also is None else 2):
                act.wait_ge(dev_made, n + 1)
                act.activation(std[:, :], var[:, :], ACT.Sqrt).then_inc(root_made, 1)


def edge_tables(nc, K, src, dst):
    NB = NT
    with ExitStack() as ctx:
        def sem(n):
            return ctx.enter_context(stage_semaphore(nc, f"edges_{n}"))

        def sb(n, shape, dt):
            return ctx.enter_context(nc.sbuf_tensor(f"edges_{n}", shape, dt))
        dst_in, sorted_out, stepped, counted, tail = sem("dst_in"), sem("sorted_out"), sem("stepped"), sem("counted"), sem("tail")
        columns_in, tables_made, pads_set = sem("columns_in"), sem("tables_made"), sem("pads_set")
        dall = sb("dall", [EL, EC], I32)
        dallf = sb("dallf", [EL, EC], F32)
        junk = sb("junk", [EL, EC], F32)
        cnt = sb("cnt", [EL, NB + 1], F32)
        st = sb("st", [P, NB + 1], F32)
        sz = sb("sz", [P, NB], F32)
        szi = sb("szi", [P, NB], I32)
        zer = sb("zer", [P, NB], F32)
        ginc = sb("ginc", [P, NB], F32)
        cbase = sb("cbase", [P, NB + 1], F32)
        ig = sb("ig", [P, NG], F32)
        blk = sb("blk", [P, NG], F32)
        offf = sb("offf", [P, NG], F32)
        tmp = sb("tmp", [P, NG], F32)
        tails = sb("tails", [1, 2, GE], I32)
        dcol = sb("dcol", [P, NTP], I32)
        iota_made = sem("iota_made")
        ps = ctx.enter_context(nc.psum_tensor("edges_ps", [P, 512], F32))
        block = ctx.enter_context(nc.Block())

        @block.sync
        def _(sp):
            sp.dma_start(dall[:, :], dst.rearrange("(p c) -> p c", p=EL)).then_inc(dst_in, 16)
            sp.dma_start(K.srt_src[0:1, 0:E], src.rearrange("(a n) -> a n", a=1)).then_inc(sorted_out, 16)
            sp.dma_start(K.srt_dst[0:1, 0:E], dst.rearrange("(a n) -> a n", a=1)).then_inc(sorted_out, 16)
            sp.wait_ge(tail, 2)
            sp.dma_start(K.srt_src[0:1, E:E + GE], tails[:, 0, :]).then_inc(sorted_out, 16)
            sp.dma_start(K.srt_dst[0:1, E:E + GE], tails[:, 1, :]).then_inc(sorted_out, 16)
            sp.wait_ge(sorted_out, 64)
            sp.wait_ge(tables_made, 1)
            sp.wait_ge(pads_set, 1)
            with sp.Fori(0, NG) as g:
                off = sp.value_load(K.off_i[0:1, bass.ds(g, 1)], min_val=0, max_val=E)
                for arr, col in ((K.srt_src, K.srccol), (K.srt_dst, dcol)):
                    sp.dma_start(col[:, bass.ds(2 * g, 2)],
                                 arr[0:1, bass.ds(off, GE)].rearrange("a (j p) -> p (a j)", p=P),
                                 allow_slow_non_contiguous=True).then_inc(columns_in, 16)

        @block.gpsimd
        def _(pool):
            pool.memset(tails[:, 0, :], 0).then_inc(tail, 1)
            pool.memset(tails[:, 1, :], SENTINEL).then_inc(tail, 1)
            pool.iota(ig[:, :], [[1, NG]], base=0, channel_multiplier=0,
                      allow_small_or_imprecise_dtypes=True).then_inc(iota_made, 1)

        @block.vector
        def _(dve):
            step = Chain(dve, stepped)
            dve.memset(dcol[:, NTILE:NTP], SENTINEL).then_inc(pads_set, 1)
            dve.wait_ge(dst_in, 16)
            step(dve.tensor_copy(dallf[:, :], dall[:, :]))
            for b in range(NB + 1):
                step(dve.tensor_scalar(junk[:, :], dallf[:, :], float(P * b), 0.0, ALU.is_lt, ALU.add,
                                       accum_out=cnt[:, b:b + 1]))
            dve.engine_nop().then_inc(counted, 1)
            dve.wait_ge(counted, 2)
            step(dve.tensor_copy(st[:, :], ps[:, 0:NB + 1]))
            step(dve.tensor_tensor(sz[:, :], st[:, 1:NB + 1], st[:, 0:NB], ALU.subtract))
            step(dve.tensor_scalar(szi[:, :], sz[:, :], float(GE - 1), None, ALU.add))
            step(dve.tensor_scalar(szi[:, :], szi[:, :], GE.bit_length() - 1, None, ALU.arith_shift_right))
            step(dve.tensor_copy(sz[:, :], szi[:, :]))
            step(dve.memset(zer[:, :], 0.0))
            step(dve.tensor_tensor_scan(ginc[:, :], sz[:, :], zer[:, :], 0.0, ALU.add, ALU.add))
            step(dve.tensor_tensor(sz[:, :], ginc[:, :], sz[:, :], ALU.subtract))
            step(dve.memset(cbase[:, NB:NB + 1], float(E)))
            step(dve.scalar_tensor_tensor(out=cbase[:, 0:NB], in0=sz[:, :], scalar=-float(GE), in1=st[:, 0:NB],
                                          op0=ALU.mult, op1=ALU.add))
            dve.wait_ge(iota_made, 1)
            step(dve.memset(blk[:, :], 0.0))
            for b in range(NB):
                step(dve.scalar_tensor_tensor(out=blk[:, :], in0=ig[:, :], scalar=ginc[:, b:b + 1], in1=blk[:, :],
                                              op0=ALU.is_ge, op1=ALU.add))
            step(dve.tensor_scalar(offf[:, :], ig[:, :], float(GE), None, ALU.mult))
            for b in range(NB + 1):
                step(dve.tensor_scalar(tmp[:, :], blk[:, :], float(b), cbase[:, b:b + 1], ALU.is_equal, ALU.mult))
                step(dve.tensor_tensor(offf[:, :], offf[:, :], tmp[:, :], ALU.add))
            step(dve.tensor_scalar(offf[:, :], offf[:, :], float(E), 0.0, ALU.min, ALU.max))
            step(dve.tensor_scalar(blk[:, :], blk[:, :], float(NB - 1), None, ALU.min))
            step(dve.tensor_copy(K.off_i[:, :], offf[:, :]))
            step(dve.tensor_copy(K.blk_i[:, :], blk[:, :]))
            step(dve.tensor_scalar(K.blkiota[:, :], blk[:, :], float(P), K.iota_part[:, 0:1], ALU.mult, ALU.add))
            step(dve.tensor_scalar(tmp[:, :], blk[:, :], float(P), None, ALU.mult))
            dve.engine_nop().then_inc(tables_made, 1)
            dve.wait_ge(columns_in, 32 * NG)
            step(dve.tensor_copy(K.dcolf[:, :], dcol[:, :]))
            step(dve.tensor_tensor(K.drel[:, :].rearrange("p (g j) -> p g j", j=2),
                                   K.dcolf[:, 0:NTILE].rearrange("p (g j) -> p g j", j=2),
                                   tmp[:, :].rearrange("p (g j) -> p g j", j=1).broadcast_to([P, NG, 2]),
                                   ALU.subtract))

        @block.tensor
        def _(pe):
            pe.wait_ge(counted, 1)
            pe.matmul(ps[:, 0:NB + 1], K.ones[0:EL, :], cnt[:, :], start=True, stop=True).then_inc(counted, 1)


def segment_tables(nc, K):
    with ExitStack() as ctx:
        def sem(n):
            return ctx.enter_context(stage_semaphore(nc, f"seg_{n}"))

        def sb(n, shape, dt):
            return ctx.enter_context(nc.sbuf_tensor(f"seg_{n}", shape, dt))
        stepped, turned, ends_out, rows_in, links_out, links_in = (
            sem("stepped"), sem("turned"), sem("ends_out"), sem("rows_in"), sem("links_out"), sem("links_in"))
        drep = sb("drep", [P, NTP, H], F32)
        dT = sb("dT", [P, NC, P], F32)
        ends = sb("ends", [P, 2, NC], F32)
        rows = sb("rows", [H, 2, NC, TPC], F32)
        link = sb("link", [H, 2, NC * TPC], F32)
        whole = sb("whole", [H, NC * TPC], F32)
        linkT = sb("linkT", [P, 2, NC], F32)
        ps = [ctx.enter_context(nc.psum_tensor(f"seg_ps{i}", [P, 512], F32)) for i in range(3)]
        made = sem("made")
        block = ctx.enter_context(nc.Block())

        @block.tensor
        def _(pe):
            pe.wait_ge(made, 1)
            for c in range(NC):
                last = pe.transpose(ps[c // 4][:, (c % 4) * P:(c % 4 + 1) * P],
                                    drep[:, c * TPC:(c + 1) * TPC, :].rearrange("p t h -> p (t h)"), K.ident[:, :])
            last.then_inc(turned, 1)

        @block.sync
        def _(sp):
            sp.wait_ge(made, 2)
            sp.dma_start(K.bounce[0], ends[:, :, :].rearrange("p a c -> p (a c)")).then_inc(ends_out, 16)
            sp.wait_ge(ends_out, 16)
            for a in range(2):
                for c in range(NC):
                    sp.dma_start(rows[:, a, c, :], K.bounce[0].rearrange("(t h) n -> h t n", h=H)[:, :, a * NC + c],
                             allow_slow_non_contiguous=True).then_inc(rows_in, 16)
            sp.wait_ge(made, 3)
            sp.dma_start(K.bounce[1].rearrange("(h a) n -> h (a n)", h=H)[:, 0:2 * NTP],
                         link[:, :, :].rearrange("h a n -> h (a n)")).then_inc(links_out, 16)
            sp.wait_ge(links_out, 16)
            for h in range(H):
                for t in range(1):
                    pass
            lv = K.bounce[1].rearrange("(h a) n -> h (a n)", h=H)[:, 0:2 * NTP]\
                  .rearrange("h (a c t) -> t h a c", a=2, t=TPC)
            for t in range(TPC):
                sp.dma_start(linkT[t * H:(t + 1) * H, :, :], lv[t], allow_slow_non_contiguous=True)\
                  .then_inc(links_in, 16)

        @block.vector
        def _(dve):
            step = Chain(dve, stepped)
            dve.tensor_copy(drep[:, :, :], K.dcolf[:, :].rearrange("p (t h) -> p t h", h=1)
                            .broadcast_to([P, NTP, H])).then_inc(made, 1)
            dve.wait_ge(turned, 1)
            for i in range(3):
                last = dve.tensor_copy(dT[:, 4 * i:4 * i + 4, :].rearrange("p c l -> p (c l)"), ps[i][:, :])
            step(last)
            step(dve.tensor_copy(ends[:, 0, :], dT[:, :, 0]))
            dve.tensor_copy(ends[:, 1, :], dT[:, :, P - 1]).then_inc(made, 1)

            def penalty(out, mask):
                return dve.tensor_scalar(out, mask, 1.0, BIG, ALU.subtract, ALU.mult)

            same = K.pen_start
            step(dve.memset(K.pen_start[:, :, 0:1], -BIG))
            step(dve.memset(K.pen_end[:, :, P - 1:P], -BIG))
            step(dve.tensor_tensor(K.pen_start[:, :, 1:P], dT[:, :, 1:P], dT[:, :, 0:P - 1], ALU.is_equal))
            step(penalty(K.pen_start[:, :, 1:P], K.pen_start[:, :, 1:P]))
            step(dve.tensor_copy(K.pen_end[:, :, 0:P - 1], K.pen_start[:, :, 1:P]))
            dve.wait_ge(rows_in, 16 * 2 * NC)
            first = rows[:, 0, :, :].rearrange("h c t -> h (c t)")
            last_ = rows[:, 1, :, :].rearrange("h c t -> h (c t)")
            step(dve.memset(link[:, :, :], 0.0))
            step(dve.tensor_tensor(link[:, 0, 1:NTP], first[:, 1:NTP], last_[:, 0:NTP - 1], ALU.is_equal))
            step(dve.tensor_copy(link[:, 1, 0:NTP - 1], link[:, 0, 1:NTP]))
            step(dve.tensor_tensor(whole[:, :], first, last_, ALU.is_equal))
            for a in range(2):
                step(dve.tensor_tensor(K.pen_carry[:, a, :], whole[:, :], link[:, a, :], ALU.mult))
                step(penalty(K.pen_carry[:, a, :], K.pen_carry[:, a, :]))
            dve.engine_nop().then_inc(made, 1)
            dve.wait_ge(links_in, 16 * TPC)
            for a, pen in ((0, K.pen_first), (1, K.pen_last)):
                e = ends[:, a, :].rearrange("p (c l) -> p c l", l=1).broadcast_to([P, NC, P])
                lk = linkT[:, a, :].rearrange("p (c l) -> p c l", l=1).broadcast_to([P, NC, P])
                step(dve.tensor_tensor(pen[:, :, :], dT[:, :, :], e, ALU.is_equal))
                step(dve.tensor_tensor(pen[:, :, :], pen[:, :, :], lk, ALU.mult))
                step(penalty(pen[:, :, :], pen[:, :, :]))


def project(nc, K, l, A):
    with ExitStack() as ctx:
        def sem(n):
            return ctx.enter_context(stage_semaphore(nc, f"proj{l}_{n}"))

        def sb(n, shape, dt):
            return ctx.enter_context(nc.sbuf_tensor(f"proj{l}_{n}", shape, dt))
        weights_in, rows_in, turned, hT_made, proj_made, out_made, table_out, parts = (
            sem("weights_in"), sem("rows_in"), sem("turned"), sem("hT_made"), sem("proj_made"), sem("out_made"),
            sem("table_out"), sem("parts"))
        stepped = sem("stepped")
        Ws = sb("Ws", [P, KC, DM], F32)
        Wd = sb("Wd", [P, KC, DM], F32)
        brow = sb("brow", [P, 2, DM], F32)
        arow = sb("arow", [P, DM], F32)
        hT = sb("hT", [P, 2, KC, P], F32)
        row = sb("row", [P, 2, 2, HW], F32)
        prod = sb("prod", [P, DM], F32)
        rest = sb("rest", [P, ROW], F32)
        psT = ctx.enter_context(nc.psum_tensor(f"proj{l}_psT", [P, 2, 512], F32))
        psP = [ctx.enter_context(nc.psum_tensor(f"proj{l}_psP{i}", [P, 2, 512], F32)) for i in range(2)]
        block = ctx.enter_context(nc.Block())

        @block.sync
        def _(sp):
            sp.dma_start(Ws[:, :, :], A["L0_gnn_Wsrc"][l].rearrange("(k p) n -> p k n", p=P)).then_inc(weights_in, 16)
            sp.dma_start(Wd[:, :, :], A["L0_gnn_Wdst"][l].rearrange("(k p) n -> p k n", p=P)).then_inc(weights_in, 16)
            sp.dma_start(brow[:, 0, :], bcast(A["L0_gnn_bsrc"][l], P)).then_inc(rows_in, 16)
            sp.dma_start(brow[:, 1, :], bcast(A["L0_gnn_bdst"][l], P)).then_inc(rows_in, 16)
            sp.dma_start(arow[:, :], bcast(A["L0_gnn_attn"][l].rearrange("h d -> (h d)"), P)).then_inc(rows_in, 16)
            for t in range(NT):
                sp.wait_ge(out_made, 2 * t + 1)
                sp.dma_start(K.hs_tab[t * P:(t + 1) * P, :], row[:, 0, :, :].rearrange("p a n -> p (a n)"))\
                  .then_inc(table_out, 16)
            sp.wait_ge(table_out, 16 * NT)

        @block.tensor
        def _(pe):
            def turn(t):
                if t >= 1:
                    pe.wait_ge(hT_made, t)
                for k in range(KC):
                    last = pe.transpose(psT[:, k // 3, (k % 3) * P:(k % 3 + 1) * P],
                                        K.h[:, t, k * P:(k + 1) * P], K.ident[:, :])
                last.then_inc(turned, 1)
            turn(0)
            pe.wait_ge(weights_in, 32)
            for t in range(NT):
                pe.wait_ge(hT_made, t + 1)
                for s, W in ((0, Ws), (1, Wd)):
                    if t >= 1:
                        pe.wait_ge(out_made, 2 * (t - 1) + s + 1)
                    for n in range(2):
                        for k in range(KC):
                            last = pe.matmul(psP[s][:, n, 0:HALF], hT[:, t % 2, k, :],
                                             W[:, k, n * HALF:(n + 1) * HALF], start=(k == 0), stop=(k == KC - 1))
                    last.then_inc(proj_made, 1)
                    if s == 0 and t + 1 < NT:
                        turn(t + 1)

        @block.scalar
        def _(act):
            for t in range(NT):
                act.wait_ge(turned, t + 1)
                if t >= 2:
                    act.wait_ge(proj_made, 2 * (t - 1))
                for c in range(2):
                    last = act.activation(hT[:, t % 2, 3 * c:3 * c + 3, :].rearrange("p k n -> p (k n)"),
                                          psT[:, c, 0:3 * P], ACT.Copy)
                last.then_inc(hT_made, 1)

        @block.vector
        def _(dve):
            step = Chain(dve, stepped)
            dve.wait_ge(rows_in, 48)
            for t in range(NT):
                for s in range(2):
                    dve.wait_ge(proj_made, 2 * t + s + 1)
                    if s == 0 and t >= 1:
                        dve.wait_ge(table_out, 16 * t)
                    step(dve.tensor_tensor(row[:, s, :, 0:HALF], psP[s][:, :, 0:HALF],
                                           brow[:, s, :].rearrange("p (a n) -> p a n", a=2), ALU.add))
                    step(dve.tensor_tensor(prod[:, :].rearrange("p (a n) -> p a n", a=2), row[:, s, :, 0:HALF],
                                           arow[:, :].rearrange("p (a n) -> p a n", a=2), ALU.mult))
                    step(dve.tensor_reduce(rest[:, 0:H], prod[:, :].rearrange("p (h d) -> p h d", h=H), AX.X, ALU.add))
                    if s == 0:
                        dve.tensor_scalar(row[:, s, :, HALF:HW], rest[:, 0:H].rearrange("p (a h) -> p a h", a=2),
                                          (1 + SLOPE) / 2, None, ALU.mult).then_inc(out_made, 1)
                        continue
                    step(dve.tensor_scalar(row[:, s, :, HALF:HW], rest[:, 0:H].rearrange("p (a h) -> p a h", a=2),
                                           (1 + SLOPE) / 2, None, ALU.mult))
                    full = row[:, 1, :, :].rearrange("p a n -> p (a n)")
                    step(dve.tensor_copy(K.hdp[:, t, 0, :], full))
                    step(dve.tensor_tensor(rest[:, :], full, K.hdp[:, t, 0, :], ALU.subtract))
                    step(dve.tensor_copy(K.hdp[:, t, 1, :], rest[:, :]))
                    step(dve.tensor_tensor(rest[:, :], rest[:, :], K.hdp[:, t, 1, :], ALU.subtract))
                    dve.tensor_copy(K.hdp[:, t, 2, :], rest[:, :]).then_inc(out_made, 1)


def edge_logits(nc, K, l, A):
    CREDIT = 2
    with ExitStack() as ctx:
        def sem(n):
            return ctx.enter_context(stage_semaphore(nc, f"lg{l}_{n}"))

        def sb(n, shape, dt):
            return ctx.enter_context(nc.sbuf_tensor(f"lg{l}_{n}", shape, dt))
        row_in = [sem(f"row_in{k}") for k in range(2)]
        gathered = [sem(f"gathered{k}") for k in range(2)]
        attn_in, attn_made, index_set, onehot_made, hd_made, summed, weighed, reduced, logit_made, abs_made = (
            sem("attn_in"), sem("attn_made"), sem("index_set"), sem("onehot_made"), sem("hd_made"), sem("summed"),
            sem("weighed"), sem("reduced"), sem("logit_made"), sem("abs_made"))
        dstrow = sb("dstrow", [P, 2, GE], I32)
        ix = [[sb(f"ix{k}{j}", [P, 1], I32) for j in range(2)] for k in range(2)]
        hse = sb("hse", [P, 2, 2, 2, HW], F32)
        tt = sb("tt", [P, 2, 2, 2, HW], F32)
        prod = sb("prod", [P, 4, HALF], F32)
        arow = sb("arow", [P, 4, HALF], F32)
        ohT = sb("ohT", [P, 2, GE], BF16)
        ps = [ctx.enter_context(nc.psum_tensor(f"lg{l}_ps{j}", [P, 2, 512], F32)) for j in range(2)]
        block = ctx.enter_context(nc.Block())

        @block.sync
        def _(sp):
            for j in range(2):
                sp.dma_start(arow[:, 2 * j:2 * j + 2, :].rearrange("p a n -> p (a n)"),
                             bcast(A["L0_gnn_attn"][l].rearrange("h d -> (h d)"), P)).then_inc(attn_in, 16)
            with sp.Fori(0, NG // 2) as i:
                for k in range(2):
                    off = sp.value_load(K.off_i[0:1, bass.ds(2 * i + k, 1)], min_val=0, max_val=E)
                    sp.wait_ge(onehot_made, 2 * i + k - 1 + CREDIT)
                    sp.nop(nofuse=True)
                    sp.dma_start(dstrow[:, k, :], K.srt_dst[0:1, bass.ds(off, GE)].broadcast_to([P, GE]))\
                      .then_inc(row_in[k], 16)

        @block.gpsimd
        def _(pool):
            with pool.Fori(0, NG // 2) as i:
                for k in range(2):
                    n = 2 * i + k
                    pool.wait_ge(summed, 2 * n - 2 + 2 * CREDIT)
                    pool.nop(nofuse=True)
                    for j in range(2):
                        pool.tensor_copy(ix[k][j][:, :], K.srccol[:, bass.ds(2 * n + j, 1)]).then_inc(index_set, 1)
                    pool.wait_ge(index_set, 2 * n + 2)
                    pool.nop(nofuse=True)
                    for j in range(2):
                        pool.indirect_dma_start(hse[:, k, j, :, :].rearrange("p a n -> p (a n)"), None, K.hs_tab,
                                                bass.IndirectOffsetOnAxis(ap=ix[k][j][:, :], axis=0))\
                            .then_inc(gathered[k], 16)

        @block.tensor
        def _(pe):
            with pe.Fori(0, NG // 2) as i:
                for k in range(2):
                    n = 2 * i + k
                    b = pe.value_load(K.blk_i[0:1, bass.ds(n, 1)], min_val=0, max_val=NT - 1)
                    pe.wait_ge(onehot_made, n + 1 + CREDIT)
                    pe.nop(nofuse=True)
                    for j in range(2):
                        pe.wait_ge(summed, 2 * (n - 1) + j + 1 + 2 * CREDIT)
                        pe.nop(nofuse=True)
                        for a in range(2):
                            for part in range(3):
                                last = pe.matmul(ps[j][:, a, 0:HW], ohT[:, k, j * P:(j + 1) * P],
                                                 K.hdp[:, bass.ds(b, 1), part, a * HW:(a + 1) * HW],
                                                 start=(part == 0), stop=(part == 2))
                        last.then_inc(hd_made, 1)

        @block.scalar
        def _(act):
            with act.Fori(0, NG // 2) as i:
                for k in range(2):
                    n = 2 * i + k
                    act.wait_ge(summed, 2 * n + 2 + 2 * CREDIT)
                    act.nop(nofuse=True)
                    t4 = tt[:, k, :, :, :].rearrange("p j a n -> p (j a) n")
                    act.activation(t4[:, :, 0:HALF], t4[:, :, 0:HALF], ACT.Abs).then_inc(abs_made, 1)

        @block.vector
        def _(dve):
            dve.sem_inc(onehot_made, CREDIT)
            dve.sem_inc(summed, 2 * CREDIT)
            dve.sem_inc(hd_made, 2 * CREDIT)
            dve.wait_ge(attn_in, 32)
            dve.tensor_scalar(arow[:, :, :], arow[:, :, :], (1 - SLOPE) / 2, None, ALU.mult).then_inc(attn_made, 1)
            dve.wait_ge(attn_made, 1)

            def onehot(n, k, it):
                dve.wait_ge(row_in[k], 16 * it + 16)
                dve.wait_ge(hd_made, 2 * (n - 2) + 2 + 2 * CREDIT)
                dve.nop(nofuse=True)
                dve.tensor_scalar(ohT[:, k, :], dstrow[:, k, :], K.blkiota[:, bass.ds(n, 1)], None, ALU.is_equal)\
                   .then_inc(onehot_made, 1)

            def add(n, k, it):
                dve.wait_ge(gathered[k], 32 * it + 32)
                dve.nop(nofuse=True)
                for j in range(2):
                    dve.wait_ge(hd_made, 2 * n + j + 1 + 2 * CREDIT)
                    dve.nop(nofuse=True)
                    dve.tensor_tensor(tt[:, k, j, :, :], ps[j][:, :, 0:HW], hse[:, k, j, :, :], ALU.add)\
                       .then_inc(summed, 1)

            def weigh(n, k):
                dve.wait_ge(abs_made, n + 1)
                dve.nop(nofuse=True)
                t4 = tt[:, k, :, :, :].rearrange("p j a n -> p (j a) n")
                dve.tensor_tensor(prod[:, :, :], t4[:, :, 0:HALF], arow[:, :, :], ALU.mult).then_inc(weighed, 1)
                dve.wait_ge(weighed, n + 1)
                dve.nop(nofuse=True)
                lg = K.lg[:, bass.ds(n, 1), :]
                dve.tensor_reduce(lg, prod[:, :, :].rearrange("p a (h d) -> p (a h) d", d=HD), AX.X, ALU.add)\
                   .then_inc(reduced, 1)
                dve.wait_ge(reduced, n + 1)
                dve.nop(nofuse=True)
                dve.tensor_tensor(K.lg[:, bass.ds(n, 1), :].rearrange("p g (a h) -> p (g a) h", a=4),
                                  K.lg[:, bass.ds(n, 1), :].rearrange("p g (a h) -> p (g a) h", a=4),
                                  t4[:, :, HALF:HW], ALU.add).then_inc(logit_made, 1)
                dve.wait_ge(logit_made, n + 1)
                dve.nop(nofuse=True)

            onehot(0, 0, 0)
            onehot(1, 1, 0)
            add(0, 0, 0)
            with dve.Fori(0, NG // 2 - 1) as i:
                onehot(2 * i + 2, 0, i + 1)
                add(2 * i + 1, 1, i)
                weigh(2 * i, 0)
                onehot(2 * i + 3, 1, i + 1)
                add(2 * i + 2, 0, i + 1)
                weigh(2 * i + 1, 1)
            add(NG - 1, 1, NG // 2 - 1)
            weigh(NG - 2, 0)
            weigh(NG - 1, 1)


def segment_softmax(nc, K, l):
    with ExitStack() as ctx:
        def sem(n):
            return ctx.enter_context(stage_semaphore(nc, f"sm{l}_{n}"))

        def sb(n, shape, dt):
            return ctx.enter_context(nc.sbuf_tensor(f"sm{l}_{n}", shape, dt))
        stepped, pads_set, turned, made, ends_out, rows_in, carry_out, carry_in, back = (
            sem("stepped"), sem("pads_set"), sem("turned"), sem("made"), sem("ends_out"), sem("rows_in"),
            sem("carry_out"), sem("carry_in"), sem("back"))
        lgT = sb("lgT", [P, NC, P], F32)
        fw = sb("fw", [P, NC, P], F32)
        bw = sb("bw", [P, NC, P], F32)
        ends = sb("ends", [P, 2, NC], F32)
        rows = sb("rows", [H, 2, NC * TPC], F32)
        run = sb("run", [H, 2, NC * TPC], F32)
        carry = sb("carry", [H, 2, NC * TPC], F32)
        carryT = sb("carryT", [P, 2, NC], F32)
        ps = [ctx.enter_context(nc.psum_tensor(f"sm{l}_ps{i}", [P, 512], F32)) for i in range(3)]
        block = ctx.enter_context(nc.Block())
        lg3 = K.lg[:, :, :].rearrange("p g x -> p (g x)")

        @block.tensor
        def _(pe):
            pe.wait_ge(pads_set, 1)
            for c in range(NC):
                last = pe.transpose(ps[c // 4][:, (c % 4) * P:(c % 4 + 1) * P], lg3[:, c * P:(c + 1) * P],
                                    K.ident[:, :])
            last.then_inc(turned, 1)
            pe.wait_ge(made, 3)
            for c in range(NC):
                last = pe.transpose(ps[c // 4][:, (c % 4) * P:(c % 4 + 1) * P], lgT[:, c, :], K.ident[:, :])
            last.then_inc(turned, 1)

        @block.sync
        def _(sp):
            sp.wait_ge(made, 1)
            sp.dma_start(K.bounce[2], ends[:, :, :].rearrange("p a c -> p (a c)")).then_inc(ends_out, 16)
            sp.wait_ge(ends_out, 16)
            for a in range(2):
                for c in range(NC):
                    sp.dma_start(rows[:, a, c * TPC:(c + 1) * TPC],
                                 K.bounce[2].rearrange("(t h) n -> h t n", h=H)[:, :, a * NC + c],
                             allow_slow_non_contiguous=True).then_inc(rows_in, 16)
            sp.wait_ge(made, 2)
            sp.dma_start(K.bounce[3].rearrange("(h a) n -> h (a n)", h=H)[:, 0:2 * NTP],
                         carry[:, :, :].rearrange("h a n -> h (a n)")).then_inc(carry_out, 16)
            sp.wait_ge(carry_out, 16)
            cv = K.bounce[3].rearrange("(h a) n -> h (a n)", h=H)[:, 0:2 * NTP]\
                  .rearrange("h (a c t) -> t h a c", a=2, t=TPC)
            for t in range(TPC):
                sp.dma_start(carryT[t * H:(t + 1) * H, :, :], cv[t], allow_slow_non_contiguous=True)\
                  .then_inc(carry_in, 16)

        @block.vector
        def _(dve):
            step = Chain(dve, stepped)
            dve.memset(lg3[:, NTILE * H:NTP * H], 0.0).then_inc(pads_set, 1)
            dve.wait_ge(turned, 1)
            for i in range(3):
                last = dve.tensor_copy(lgT[:, 4 * i:4 * i + 4, :].rearrange("p c l -> p (c l)"), ps[i][:, :])
            step(last)

            def flat(x):
                return x[:, :, :].rearrange("p c l -> p (c l)")
            step(dve.tensor_tensor_scan(flat(fw), flat(K.pen_start), flat(lgT), -BIG, ALU.add, ALU.max))
            step(dve.tensor_tensor_scan(flat(bw)[:, ::-1], flat(K.pen_end)[:, ::-1], flat(lgT)[:, ::-1], -BIG,
                                        ALU.add, ALU.max))
            step(dve.tensor_copy(ends[:, 0, :], fw[:, :, P - 1]))
            dve.tensor_copy(ends[:, 1, :], bw[:, :, 0]).then_inc(made, 1)
            step(dve.tensor_tensor(flat(fw), flat(fw), flat(bw), ALU.max))
            dve.wait_ge(rows_in, 16 * 2 * NC)
            step(dve.memset(carry[:, :, :], -BIG))
            step(dve.tensor_tensor_scan(run[:, 0, :], K.pen_carry[:, 0, :], rows[:, 0, :], -BIG, ALU.add, ALU.max))
            step(dve.tensor_tensor_scan(run[:, 1, ::-1], K.pen_carry[:, 1, ::-1], rows[:, 1, ::-1], -BIG,
                                        ALU.add, ALU.max))
            step(dve.tensor_copy(carry[:, 0, 1:NTP], run[:, 0, 0:NTP - 1]))
            dve.tensor_copy(carry[:, 1, 0:NTP - 1], run[:, 1, 1:NTP]).then_inc(made, 1)
            dve.wait_ge(carry_in, 16 * TPC)
            for a, pen in ((0, K.pen_first), (1, K.pen_last)):
                cb = carryT[:, a, :].rearrange("p (c l) -> p c l", l=1).broadcast_to([P, NC, P])
                step(dve.tensor_tensor(bw[:, :, :], pen[:, :, :], cb, ALU.add))
                step(dve.tensor_tensor(fw[:, :, :], fw[:, :, :], bw[:, :, :], ALU.max))
            dve.tensor_tensor(bw[:, :, :], lgT[:, :, :], fw[:, :, :], ALU.subtract).then_inc(back, 1)
            dve.wait_ge(turned, 2)
            for i in range(3):
                last = dve.tensor_copy(lg3[:, i * 512:(i + 1) * 512], ps[i][:, :])
            step(last)

        @block.scalar
        def _(act):
            act.wait_ge(back, 1)
            act.activation(lgT[:, :, :].rearrange("p c l -> p (c l)"), bw[:, :, :].rearrange("p c l -> p (c l)"),
                           ACT.Exp).then_inc(made, 1)


def aggregate(nc, K, l):
    CREDIT = 2
    with ExitStack() as ctx:
        def sem(n):
            return ctx.enter_context(stage_semaphore(nc, f"ag{l}_{n}"))

        def sb(n, shape, dt):
            return ctx.enter_context(nc.sbuf_tensor(f"ag{l}_{n}", shape, dt))
        gathered = [sem(f"gathered{k}") for k in range(2)]
        index_set, onehot_made, scaled, message_made, summed, added, zeroed = (
            sem("index_set"), sem("onehot_made"), sem("scaled"), sem("message_made"), sem("summed"), sem("added"),
            sem("zeroed"))
        ix = [[sb(f"ix{k}{j}", [P, 1], I32) for j in range(2)] for k in range(2)]
        hse = sb("hse", [P, 2, 2, ROW], F32)
        msg = sb("msg", [P, 2, 2, ROW], F32)
        oh = sb("oh", [P, 2, 2, P], F32)
        ps = [ctx.enter_context(nc.psum_tensor(f"ag{l}_ps{k}", [P, 2, 512], F32)) for k in range(2)]
        block = ctx.enter_context(nc.Block())

        @block.gpsimd
        def _(pool):
            with pool.Fori(0, NG // 2) as i:
                for k in range(2):
                    n = 2 * i + k
                    pool.wait_ge(message_made, n - 1 + CREDIT)
                    pool.nop(nofuse=True)
                    for j in range(2):
                        pool.tensor_copy(ix[k][j][:, :], K.srccol[:, bass.ds(2 * n + j, 1)]).then_inc(index_set, 1)
                    pool.wait_ge(index_set, 2 * n + 2)
                    pool.nop(nofuse=True)
                    for j in range(2):
                        pool.indirect_dma_start(hse[:, k, j, :], None, K.hs_tab,
                                                bass.IndirectOffsetOnAxis(ap=ix[k][j][:, :], axis=0))\
                            .then_inc(gathered[k], 16)

        @block.tensor
        def _(pe):
            with pe.Fori(0, NG // 2) as i:
                for k in range(2):
                    n = 2 * i + k
                    pe.wait_ge(message_made, n + 1 + CREDIT)
                    pe.nop(nofuse=True)
                    pe.wait_ge(added, n - 1 + CREDIT)
                    pe.nop(nofuse=True)
                    for a in range(2):
                        for j in range(2):
                            last = pe.matmul(ps[k][:, a, 0:HW], oh[:, k, j, :], msg[:, k, j, a * HW:(a + 1) * HW],
                                             start=(j == 0), stop=(j == 1))
                    last.then_inc(summed, 1)

        @block.vector
        def _(dve):
            dve.sem_inc(message_made, CREDIT)
            dve.sem_inc(added, CREDIT)
            dve.sem_inc(summed, CREDIT)
            dve.memset(K.acc[:, :, :], 0.0).then_inc(zeroed, 1)
            dve.wait_ge(zeroed, 1)

            def message(n, k, it):
                dve.wait_ge(gathered[k], 32 * it + 32)
                dve.wait_ge(summed, n - 1 + CREDIT)
                dve.nop(nofuse=True)
                for j in range(2):
                    dve.tensor_scalar(oh[:, k, j, :], K.iota_free[:, :], K.drel[:, bass.ds(2 * n + j, 1)], None,
                                      ALU.is_equal)
                ex = K.lg[:, bass.ds(n, 1), :].rearrange("p g (a h) -> p (g a) h", a=4)
                m4 = msg[:, k, :, :].rearrange("p j (a n) -> p (j a) n", a=2)
                h4 = hse[:, k, :, :].rearrange("p j (a n) -> p (j a) n", a=2)
                dve.tensor_copy(m4[:, :, HALF:HW], ex)
                for j in range(2):
                    for a in range(2):
                        exh = K.lg[:, bass.ds(n, 1), (2 * j + a) * HH:(2 * j + a + 1) * HH]\
                            .rearrange("p g (h d) -> p (g h) d", d=1).broadcast_to([P, HH, HD])
                        last = dve.tensor_tensor(
                            m4[:, 2 * j + a, 0:HALF].rearrange("p (h d) -> p h d", d=HD),
                            h4[:, 2 * j + a, 0:HALF].rearrange("p (h d) -> p h d", d=HD), exh, ALU.mult)
                last.then_inc(message_made, 1)

            def add(n, k):
                b = dve.value_load(K.blk_i[0:1, bass.ds(n, 1)], min_val=0, max_val=NT - 1)
                dve.wait_ge(summed, n + 1 + CREDIT)
                dve.nop(nofuse=True)
                dve.wait_ge(added, n + CREDIT)
                dve.nop(nofuse=True)
                a = K.acc[:, bass.ds(b, 1), :].rearrange("p b (a n) -> p (b a) n", a=2)
                dve.tensor_tensor(a, a, ps[k][:, :, 0:HW], ALU.add).then_inc(added, 1)

            message(0, 0, 0)
            with dve.Fori(0, NG // 2 - 1) as i:
                message(2 * i + 1, 1, i)
                add(2 * i, 0)
                message(2 * i + 2, 0, i + 1)
                add(2 * i + 1, 1)
            message(NG - 1, 1, NG // 2 - 1)
            add(NG - 2, 0)
            add(NG - 1, 1)


def node_update(nc, K, l, A):
    with ExitStack() as ctx:
        def sem(n):
            return ctx.enter_context(stage_semaphore(nc, f"up{l}_{n}"))

        def sb(n, shape, dt):
            return ctx.enter_context(nc.sbuf_tensor(f"up{l}_{n}", shape, dt))
        stepped, low_made, exp_made, rows_in = sem("stepped"), sem("low_made"), sem("exp_made"), sem("rows_in")
        rs = sb("rs", [P, NT, H], F32)
        o = sb("o", [P, 2, DM], F32)
        m = sb("m", [P, 2, DM], F32)
        block = ctx.enter_context(nc.Block())

        @block.sync
        def _(sp):
            sp.dma_start(K.lnw[:, :], bcast(A["L0_gnn_ln_w"][l], P)).then_inc(rows_in, 16)
            sp.dma_start(K.lnb[:, :], bcast(A["L0_gnn_ln_b"][l], P)).then_inc(rows_in, 16)
            if l == L - 1:
                sp.dma_start(K.onw[:, :], bcast(A["L0_gnn_on_w"], P)).then_inc(rows_in, 16)
                sp.dma_start(K.onb[:, :], bcast(A["L0_gnn_on_b"], P)).then_inc(rows_in, 16)
            sp.wait_ge(rows_in, 64 if l == L - 1 else 32)

        @block.vector
        def _(dve):
            step = Chain(dve, stepped)
            acc4 = K.acc[:, :, :].rearrange("p t (a n) -> p t a n", a=2)
            for a in range(2):
                step(dve.tensor_scalar(rs[:, :, a * HH:(a + 1) * HH], acc4[:, :, a, HALF:HW], 1e-30, None, ALU.max))
            step(dve.reciprocal(rs[:, :, :], rs[:, :, :]))

            def first(t):
                for a in range(2):
                    r = rs[:, t, a * HH:(a + 1) * HH].rearrange("p (h d) -> p h d", d=1).broadcast_to([P, HH, HD])
                    last = dve.tensor_tensor(o[:, t % 2, a * HALF:(a + 1) * HALF].rearrange("p (h d) -> p h d", d=HD),
                                             acc4[:, t, a, 0:HALF].rearrange("p (h d) -> p h d", d=HD), r, ALU.mult)
                step(last)
                dve.tensor_scalar(m[:, t % 2, :], o[:, t % 2, :], 0.0, None, ALU.min).then_inc(low_made, 1)

            def second(t):
                dve.wait_ge(exp_made, t + 1)
                step(dve.scalar_tensor_tensor(out=o[:, t % 2, :], in0=o[:, t % 2, :], scalar=0.0, in1=m[:, t % 2, :],
                                              op0=ALU.max, op1=ALU.add))
                step(dve.scalar_tensor_tensor(out=K.h[:, t, :], in0=o[:, t % 2, :], scalar=-1.0, in1=K.h[:, t, :],
                                              op0=ALU.add, op1=ALU.add))
            first(0)
            for t in range(NT):
                if t + 1 < NT:
                    first(t + 1)
                second(t)

        @block.scalar
        def _(act):
            for t in range(NT):
                act.wait_ge(low_made, t + 1)
                act.activation(m[:, t % 2, :], m[:, t % 2, :], ACT.Exp).then_inc(exp_made, 1)


class Keep:
    pass


def gnn(nc, K, A):
    with ExitStack() as ctx:
        def sb(n, shape, dt):
            return ctx.enter_context(nc.sbuf_tensor(n, shape, dt))
        K.hdp = sb("hd_parts", [P, NT, 3, ROW], BF16)
        K.lg = sb("logits", [P, NTP // 2, 2 * H], F32)
        K.srccol = sb("src_columns", [P, NTILE], I32)
        K.dcolf = sb("dst_columns", [P, NTP], F32)
        K.drel = sb("dst_in_block", [P, NTILE], F32)
        K.off_i = sb("group_offset", [P, NG], I32)
        K.blk_i = sb("group_block", [P, NG], I32)
        K.blkiota = sb("block_members", [P, NG], F32)
        K.pen_start = sb("pen_start", [P, NC, P], F32)
        K.pen_end = sb("pen_end", [P, NC, P], F32)
        K.pen_first = sb("pen_first", [P, NC, P], F32)
        K.pen_last = sb("pen_last", [P, NC, P], F32)
        K.pen_carry = sb("pen_carry", [H, 2, NTP], F32)
        edge_tables(nc, K, A["src"], A["dst"])
        segment_tables(nc, K)
        for l in range(L):
            if l > 0:
                recycle(nc)
            project(nc, K, l, A)
            edge_logits(nc, K, l, A)
            segment_softmax(nc, K, l)
            with ExitStack() as c2:
                K.acc = c2.enter_context(nc.sbuf_tensor(f"acc{l}", [P, NT, ROW], F32))
                aggregate(nc, K, l)
                node_update(nc, K, l, A)
            if l < L - 1:
                norm_block(nc, K, f"ln{l}", K.h, K.h, K.lnw, K.lnb)


NE = 16
NGRP = 8
PER = NE // NGRP
TOPG = 4
TOPE = 4
SCALE = 2.5
HID = 512
KH = HID // P
TM = (N * TOPE + NE * (P - 1)) // P
TM -= 0 if TM % 2 == 0 else -1
BW = 2 * HID + DM


def bias_parts(nc, K, A):
    with ExitStack() as ctx:
        def sem(n):
            return ctx.enter_context(stage_semaphore(nc, f"bias_{n}"))

        def sb(n, shape, dt):
            return ctx.enter_context(nc.sbuf_tensor(f"bias_{n}", shape, dt))
        rows_in, stepped, parts_made, parts_out = sem("rows_in"), sem("stepped"), sem("parts_made"), sem("parts_out")
        full = sb("full", [NE + 1, BW], F32)
        parts = sb("parts", [NE + 1, 3, BW], BF16)
        block = ctx.enter_context(nc.Block())

        @block.sync
        def _(sp):
            for name, at, w in (("bu", 0, HID), ("bg", HID, HID), ("bd", 2 * HID, DM)):
                sp.dma_start(full[0:NE, at:at + w], A["L0_ffn_" + name]).then_inc(rows_in, 16)
                sp.dma_start(full[NE:NE + 1, at:at + w], A["L0_ffn_s" + name].rearrange("(a n) -> a n", a=1))\
                  .then_inc(rows_in, 16)
            sp.wait_ge(parts_made, 1)
            sp.dma_start(K.bias_tab, parts[:, :, :]).then_inc(parts_out, 16)
            sp.wait_ge(parts_out, 16)

        @block.vector
        def _(dve):
            step = Chain(dve, stepped)
            dve.wait_ge(rows_in, 96)
            step(dve.tensor_copy(parts[:, 0, :], full[:, :]))
            step(dve.tensor_tensor(full[:, :], full[:, :], parts[:, 0, :], ALU.subtract))
            step(dve.tensor_copy(parts[:, 1, :], full[:, :]))
            step(dve.tensor_tensor(full[:, :], full[:, :], parts[:, 1, :], ALU.subtract))
            dve.tensor_copy(parts[:, 2, :], full[:, :]).then_inc(parts_made, 1)


def route(nc, K, A):
    with ExitStack() as ctx:
        def sem(n):
            return ctx.enter_context(stage_semaphore(nc, f"route_{n}"))

        def sb(n, shape, dt):
            return ctx.enter_context(nc.sbuf_tensor(f"route_{n}", shape, dt))
        weights_in, rows_out, turned, xT_made, logits_made, exp_ready, exp_made = (
            sem("weights_in"), sem("rows_out"), sem("turned"), sem("xT_made"), sem("logits_made"), sem("exp_ready"),
            sem("exp_made"))
        stepped, iotas, chosen, counted, zeroed = sem("stepped"), sem("iotas"), sem("chosen"), sem("counted"), sem("zeroed")
        gw = sb("gw", [P, KC, NE], F32)
        rows = sb("rows", [P, 2, NE], F32)
        xT = sb("xT", [P, 2, KC, P], F32)
        lo = sb("lo", [P, NT, NE], F32)
        sc = sb("sc", [P, NT, NE], F32)
        s = sb("s", [P, NT, NE], F32)
        mx = sb("mx", [P, NT], F32)
        g = sb("g", [P, NT, NGRP], F32)
        cmp_ = sb("cmp", [P, NT, NE, NE], F32)
        eq = sb("eq", [P, NT, NE, NE], F32)
        rank = sb("rank", [P, NT, NE], F32)
        tri = sb("tri", [P, NE, NE], F32)
        tri8 = sb("tri8", [P, NGRP, NGRP], F32)
        upper = sb("upper", [P, P], F32)
        tok = sb("tok", [P, NT], F32)
        valid = sb("valid", [P, NT], F32)
        sel = sb("sel", [P, NT, NE], F32)
        c1 = sb("c1", [P, NT, NE], F32)
        c2 = sb("c2", [P, NT, NE], F32)
        pos = sb("pos", [P, NT, NE], F32)
        tot = sb("tot", [P, NT, NE], F32)
        run = sb("run", [P, NE], F32)
        nt = sb("nt", [P, NE], F32)
        nti = sb("nti", [P, NE], I32)
        zer = sb("zer", [P, NE], F32)
        cum = sb("cum", [P, NE], F32)
        base = sb("base", [P, NE], F32)
        it = sb("it", [P, TM], F32)
        te = sb("te", [P, TM], F32)
        pk = sb("pk", [P, TOPE, NT], F32)
        lane = sb("lane", [P, TOPE, NT], I32)
        none = sb("none", [P, TM], I32)
        psT = ctx.enter_context(nc.psum_tensor("route_psT", [P, 2, 512], F32))
        psL = ctx.enter_context(nc.psum_tensor("route_psL", [P, NT * NE], F32))
        psC = [ctx.enter_context(nc.psum_tensor(f"route_psC{i}", [P, NT * NE], F32)) for i in range(2)]
        block = ctx.enter_context(nc.Block())

        @block.sync
        def _(sp):
            sp.dma_start(gw[:, :, :], A["L0_ffn_gate_w"].rearrange("(k p) n -> p k n", p=P)).then_inc(weights_in, 16)
            sp.dma_start(rows[:, 0, :], bcast(A["L0_ffn_gate_b"], P)).then_inc(weights_in, 16)
            sp.dma_start(rows[:, 1, :], bcast(A["L0_ffn_bias"], P)).then_inc(weights_in, 16)
            sp.dma_start(K.xn_tab.rearrange("(t p) d -> p t d", p=P), K.xn[:, :, :]).then_inc(rows_out, 16)
            sp.wait_ge(zeroed, 1)
            sp.dma_start(K.pair_tab.rearrange("(p k) a -> p (k a)", p=P), none[:, :]).then_inc(rows_out, 16)
            sp.wait_ge(rows_out, 32)

        @block.gpsimd
        def _(pool):
            pool.memset(none[:, :], 0).then_inc(zeroed, 1)
            pool.memset(upper[:, :], 1.0).then_inc(iotas, 1)
            pool.memset(tri[:, :, :], 1.0).then_inc(iotas, 1)
            pool.memset(tri8[:, :, :], 1.0).then_inc(iotas, 1)
            pool.wait_ge(iotas, 3)
            pool.affine_select(out=upper[:, :], in_=upper[:, :], compare_op=ALU.is_gt, fill=0.0, base=0,
                               pattern=[[1, P]], channel_multiplier=-1).then_inc(iotas, 1)
            pool.affine_select(out=tri[:, :, :], in_=tri[:, :, :], compare_op=ALU.is_gt, fill=0.0, base=0,
                               pattern=[[1, NE], [-1, NE]], channel_multiplier=0).then_inc(iotas, 1)
            pool.affine_select(out=tri8[:, :, :], in_=tri8[:, :, :], compare_op=ALU.is_gt, fill=0.0, base=0,
                               pattern=[[1, NGRP], [-1, NGRP]], channel_multiplier=0).then_inc(iotas, 1)
            pool.iota(tok[:, :], [[P, NT]], base=0, channel_multiplier=1,
                      allow_small_or_imprecise_dtypes=True).then_inc(iotas, 1)
            pool.iota(it[:, :], [[1, TM]], base=0, channel_multiplier=0,
                      allow_small_or_imprecise_dtypes=True).then_inc(iotas, 1)

        @block.tensor
        def _(pe):
            pe.wait_ge(weights_in, 48)
            for t in range(NT):
                if t >= 1:
                    pe.wait_ge(xT_made, t)
                for k in range(KC):
                    last = pe.transpose(psT[:, k // 3, (k % 3) * P:(k % 3 + 1) * P], K.xn[:, t, k * P:(k + 1) * P],
                                        K.ident[:, :])
                last.then_inc(turned, 1)
                pe.wait_ge(xT_made, t + 1)
                for k in range(KC):
                    last = pe.matmul(psL[:, t * NE:(t + 1) * NE], xT[:, t % 2, k, :], gw[:, k, :], start=(k == 0),
                                     stop=(k == KC - 1))
                last.then_inc(logits_made, 1)
            pe.wait_ge(chosen, 1)
            selv = sel[:, :, :].rearrange("p t e -> p (t e)")
            pe.matmul(psC[0][:, :], upper[:, :], selv, start=True, stop=True)
            pe.matmul(psC[1][:, :], K.ones[:, :], selv, start=True, stop=True).then_inc(counted, 1)

        @block.scalar
        def _(act):
            for t in range(NT):
                act.wait_ge(turned, t + 1)
                if t >= 2:
                    act.wait_ge(logits_made, t - 1)
                for c in range(2):
                    last = act.activation(xT[:, t % 2, 3 * c:3 * c + 3, :].rearrange("p k n -> p (k n)"),
                                          psT[:, c, 0:3 * P], ACT.Copy)
                last.then_inc(xT_made, 1)
            act.wait_ge(exp_ready, 1)
            act.activation(sc[:, :, :], lo[:, :, :], ACT.Exp).then_inc(exp_made, 1)

        @block.vector
        def _(dve):
            step = Chain(dve, stepped)

            def over(x, n):
                return x.rearrange("p (t e) -> p t e", e=1).broadcast_to([P, NT, n])

            dve.wait_ge(logits_made, NT)
            gb = rows[:, 0:1, :].broadcast_to([P, NT, NE])
            step(dve.tensor_tensor(lo[:, :, :], psL[:, :].rearrange("p (t e) -> p t e", e=NE), gb, ALU.add))
            step(dve.tensor_reduce(mx[:, :], lo[:, :, :], AX.X, ALU.max))
            dve.tensor_tensor(lo[:, :, :], lo[:, :, :], over(mx[:, :], NE), ALU.subtract).then_inc(exp_ready, 1)
            dve.wait_ge(exp_made, 1)
            step(dve.tensor_reduce(mx[:, :], sc[:, :, :], AX.X, ALU.add))
            step(dve.reciprocal(mx[:, :], mx[:, :]))
            step(dve.tensor_tensor(sc[:, :, :], sc[:, :, :], over(mx[:, :], NE), ALU.mult))
            step(dve.tensor_tensor(s[:, :, :], sc[:, :, :], rows[:, 1:2, :].broadcast_to([P, NT, NE]), ALU.add))
            s4 = s[:, :, :].rearrange("p t (g a) -> p t g a", a=PER)
            step(dve.tensor_tensor(g[:, :, :], s4[:, :, :, 0], s4[:, :, :, 1], ALU.add))
            dve.wait_ge(iotas, 8)

            def top(x, n, k, low, out):
                for t in range(NT):
                    xj = x[:, t:t + 1, :].broadcast_to([P, n, n])
                    xi = x[:, t, :].rearrange("p (i j) -> p i j", j=1).broadcast_to([P, n, n])
                    dve.tensor_tensor(cmp_[:, t, 0:n, 0:n], xj, xi, ALU.is_gt)
                    last = dve.tensor_tensor(eq[:, t, 0:n, 0:n], xj, xi, ALU.is_equal)
                step(last)
                for t in range(NT):
                    last = dve.tensor_tensor(eq[:, t, 0:n, 0:n], eq[:, t, 0:n, 0:n], low[:, :, :], ALU.mult)
                step(last)
                for t in range(NT):
                    last = dve.tensor_tensor(cmp_[:, t, 0:n, 0:n], cmp_[:, t, 0:n, 0:n], eq[:, t, 0:n, 0:n], ALU.add)
                step(last)
                for t in range(NT):
                    last = dve.tensor_reduce(rank[:, t, 0:n], cmp_[:, t, 0:n, 0:n], AX.X, ALU.add)
                step(last)
                step(dve.tensor_scalar(out, rank[:, :, 0:n], float(k), None, ALU.is_lt))

            top(g, NGRP, TOPG, tri8, c1[:, :, 0:NGRP])
            for a in range(PER):
                step(dve.tensor_scalar(c2[:, :, 0:NGRP], c1[:, :, 0:NGRP], 1.0, BIG, ALU.subtract, ALU.mult))
                step(dve.tensor_tensor(s4[:, :, :, a], s4[:, :, :, a], c1[:, :, 0:NGRP], ALU.mult))
                step(dve.tensor_tensor(s4[:, :, :, a], s4[:, :, :, a], c2[:, :, 0:NGRP], ALU.add))
            top(s, NE, TOPE, tri, sel[:, :, :])
            step(dve.tensor_scalar(valid[:, :], tok[:, :], float(N), None, ALU.is_lt))
            dve.tensor_tensor(sel[:, :, :], sel[:, :, :], over(valid[:, :], NE), ALU.mult).then_inc(chosen, 1)
            dve.wait_ge(chosen, 1)
            src_, n = sel, 1
            for dst_ in (c1, c2, c1, c2):
                dve.tensor_copy(dst_[:, :, 0:n], src_[:, :, 0:n])
                step(dve.tensor_tensor(dst_[:, :, n:NE], src_[:, :, n:NE], src_[:, :, 0:NE - n], ALU.add))
                src_, n = dst_, 2 * n
            dve.wait_ge(counted, 1)
            step(dve.tensor_copy(pos[:, :, :], psC[0][:, :].rearrange("p (t e) -> p t e", e=NE)))
            step(dve.tensor_copy(tot[:, :, :], psC[1][:, :].rearrange("p (t e) -> p t e", e=NE)))
            step(dve.memset(run[:, :], 0.0))
            for t in range(NT):
                step(dve.tensor_tensor(pos[:, t, :], pos[:, t, :], run[:, :], ALU.add))
                step(dve.tensor_tensor(run[:, :], run[:, :], tot[:, t, :], ALU.add))
            step(dve.tensor_scalar(nti[:, :], run[:, :], float(P - 1), None, ALU.add))
            step(dve.tensor_scalar(nti[:, :], nti[:, :], P.bit_length() - 1, None, ALU.arith_shift_right))
            step(dve.tensor_copy(nt[:, :], nti[:, :]))
            step(dve.memset(zer[:, :], 0.0))
            step(dve.tensor_tensor_scan(cum[:, :], nt[:, :], zer[:, :], 0.0, ALU.add, ALU.add))
            step(dve.tensor_tensor(base[:, :], cum[:, :], nt[:, :], ALU.subtract))
            step(dve.tensor_scalar(base[:, :], base[:, :], float(P), None, ALU.mult))
            step(dve.tensor_tensor(pos[:, :, :], pos[:, :, :],
                                   base[:, :].rearrange("p (a e) -> p a e", a=1).broadcast_to([P, NT, NE]), ALU.add))
            step(dve.memset(te[:, :], 0.0))
            for e in range(NE):
                step(dve.scalar_tensor_tensor(out=te[:, :], in0=it[:, :], scalar=cum[:, e:e + 1], in1=te[:, :],
                                              op0=ALU.is_ge, op1=ALU.add))
            step(dve.tensor_scalar(te[:, :], te[:, :], float(NE - 1), None, ALU.min))
            step(dve.tensor_copy(K.tile_expert[:, :], te[:, :]))
            for q in range(TOPE):
                step(dve.tensor_scalar(c1[:, :, :], c2[:, :, :], float(q + 1), None, ALU.is_equal))
                step(dve.tensor_tensor(c1[:, :, :], c1[:, :, :], sel[:, :, :], ALU.mult))
                step(dve.tensor_tensor(s[:, :, :], c1[:, :, :], pos[:, :, :], ALU.mult))
                step(dve.tensor_reduce(pk[:, q, :], s[:, :, :], AX.X, ALU.add))
                step(dve.tensor_tensor(s[:, :, :], c1[:, :, :], sc[:, :, :], ALU.mult))
                step(dve.tensor_reduce(K.pair_w[:, q, :], s[:, :, :], AX.X, ALU.add))
            step(dve.tensor_scalar(K.pair_w[:, :, :], K.pair_w[:, :, :], SCALE, None, ALU.mult))
            step(dve.tensor_copy(K.pair_row[:, :, :], pk[:, :, :]))
            step(dve.tensor_scalar(lane[:, :, :], K.pair_row[:, :, :], P - 1, None, ALU.bitwise_and))
            step(dve.tensor_scalar(K.pair_at[:, :, :], K.pair_row[:, :, :], P.bit_length() - 1, None,
                                   ALU.arith_shift_right))
            step(dve.scalar_tensor_tensor(out=K.pair_at[:, :, :], in0=lane[:, :, :], scalar=float(TM),
                                          in1=K.pair_at[:, :, :], op0=ALU.mult, op1=ALU.add))
            step(dve.tensor_copy(K.token_id[:, :], tok[:, :]))


def expert_tiles(nc, K, A, name, count, routed):
    C = 2
    with ExitStack() as ctx:
        def sem(n):
            return ctx.enter_context(stage_semaphore(nc, f"{name}_{n}"))

        def sb(n, shape, dt):
            return ctx.enter_context(nc.sbuf_tensor(f"{name}_{n}", shape, dt))
        slots = 2 if routed else 1
        weights_in = [sem(f"weights_in{k}") for k in range(slots)]
        x_in = [sem(f"x_in{k}") for k in range(2)]
        y_out = [sem(f"y_out{k}") for k in range(2)]
        x_turned, xT_made, up_made, silu_made, act_made, act_turned, actT_made, y_made, y_taken = (
            sem("x_turned"), sem("xT_made"), sem("up_made"), sem("silu_made"), sem("act_made"), sem("act_turned"),
            sem("actT_made"), sem("y_made"), sem("y_taken"))
        scattered, pairs_in, index_set = sem("scattered"), sem("pairs_in"), sem("index_set")
        Wu = sb("Wu", [P, slots, KC, HID], F32)
        Wg = sb("Wg", [P, slots, KC, HID], F32)
        Wd = sb("Wd", [P, slots, KH, DM], F32)
        br = sb("br", [3, slots, BW], BF16)
        xe = sb("xe", [P, 2, DM], F32)
        ix = [sb(f"ix{k}", [P, 1], I32) for k in range(2)]
        xT = sb("xT", [P, 2, KC, P], F32)
        su = sb("su", [P, 2, HID], F32)
        aa = sb("aa", [P, 2, HID], F32)
        aT = sb("aT", [P, 2, KH, P], F32)
        y = sb("y", [P, 2, DM], F32)
        psG = [ctx.enter_context(nc.psum_tensor(f"{name}_psG{k}", [P, 512], F32)) for k in range(2)]
        psU = [ctx.enter_context(nc.psum_tensor(f"{name}_psU{k}", [P, 512], F32)) for k in range(2)]
        psX = ctx.enter_context(nc.psum_tensor(f"{name}_psX", [P, 2, 512], F32))
        psY = ctx.enter_context(nc.psum_tensor(f"{name}_psY", [P, 2, 512], F32))
        block = ctx.enter_context(nc.Block())
        half = count // 2
        yrows = K.pair_y if routed else K.shared_y

        @block.sync
        def _(sp):
            if not routed:
                sp.dma_start(Wu[:, 0, :, :], A["L0_ffn_sWu"].rearrange("(k p) n -> p k n", p=P)).then_inc(weights_in[0], 16)
                sp.dma_start(Wg[:, 0, :, :], A["L0_ffn_sWg"].rearrange("(k p) n -> p k n", p=P)).then_inc(weights_in[0], 16)
                sp.dma_start(Wd[:, 0, :, :], A["L0_ffn_sWd"].rearrange("(k p) n -> p k n", p=P)).then_inc(weights_in[0], 16)
                sp.dma_start(br[:, 0, :], K.bias_tab[NE]).then_inc(weights_in[0], 16)
            with sp.Fori(0, half) as i:
                for k in range(2):
                    n = 2 * i + k
                    if routed:
                        e = sp.value_load(K.tile_expert[0:1, bass.ds(n, 1)], min_val=0, max_val=NE - 1)
                        sp.wait_ge(y_made, n - 1 + C)
                        sp.nop(nofuse=True)
                        for w, dram in ((Wu, "Wu"), (Wg, "Wg"), (Wd, "Wd")):
                            sp.dma_start(w[:, k, :, :], A["L0_ffn_" + dram][bass.ds(e, 1)]
                                         .rearrange("e (k p) n -> p (e k) n", p=P)).then_inc(weights_in[k], 16)
                        sp.dma_start(br[:, k, :], K.bias_tab[bass.ds(e, 1)].rearrange("e c n -> c (e n)"))\
                          .then_inc(weights_in[k], 16)
                    else:
                        sp.wait_ge(x_turned, n - 1 + C)
                        sp.nop(nofuse=True)
                        sp.dma_start(xe[:, k, :], K.xn_tab[bass.ds(n * P, P), :]).then_inc(x_in[k], 16)

        @block.gpsimd
        def _(pool):
            if not routed:
                for t in range(NT):
                    m = P if t < NT - 1 else NLAST
                    for q in range(TOPE):
                        pool.indirect_dma_start(K.pair_tab, bass.IndirectOffsetOnAxis(ap=K.pair_at[0:m, q, t:t + 1], axis=0),
                                                K.token_id[0:m, t:t + 1], None).then_inc(scattered, 16)
                pool.wait_ge(scattered, 16 * NT * TOPE)
                pool.dma_start(K.pairs[:, :], K.pair_tab.rearrange("(p k) a -> p (k a)", p=P)).then_inc(pairs_in, 16)
                pool.wait_ge(pairs_in, 16)
                return
            with pool.Fori(0, half) as i:
                for k in range(2):
                    n = 2 * i + k
                    pool.wait_ge(x_turned, n - 1 + C)
                    pool.nop(nofuse=True)
                    pool.tensor_copy(ix[k][:, :], K.pairs[:, bass.ds(n, 1)]).then_inc(index_set, 1)
                    pool.wait_ge(index_set, n + 1)
                    pool.nop(nofuse=True)
                    pool.indirect_dma_start(xe[:, k, :], None, K.xn_tab,
                                            bass.IndirectOffsetOnAxis(ap=ix[k][:, :], axis=0)).then_inc(x_in[k], 16)

        def in_pairs(eng, first, step, last):
            first()
            with eng.Fori(0, half - 1) as i:
                step(2 * i + 1, 1, i)
                step(2 * i + 2, 0, i + 1)
            last()

        @block.tensor
        def _(pe):
            def turn_x(n, k, it):
                pe.wait_ge(x_in[k], 16 * it + 16)
                pe.nop(nofuse=True)
                for c in range(KC):
                    last = pe.transpose(psX[:, c // 4, (c % 4) * P:(c % 4 + 1) * P], xe[:, k, c * P:(c + 1) * P],
                                        K.ident[:, :])
                last.then_inc(x_turned, 1)

            def product(ps, W, at, k):
                s = k if routed else 0
                pe.matmul(ps[:, :], K.ones3[:, :], br[:, s, at:at + HID], start=True, stop=False)
                for c in range(KC):
                    last = pe.matmul(ps[:, :], xT[:, k, c, :], W[:, s, c, :], start=False, stop=(c == KC - 1))
                return last

            def gate(n, k, it):
                pe.wait_ge(xT_made, n + 1)
                pe.wait_ge(act_made, n - 1 + C)
                if routed:
                    pe.wait_ge(weights_in[k], 64 * it + 64)
                    pe.nop(nofuse=True)
                product(psG[k], Wg, HID, k)

            def up(n, k):
                product(psU[k], Wu, 0, k).then_inc(up_made, 1)

            def turn_act(n, k):
                pe.wait_ge(act_made, n + 1 + C)
                pe.nop(nofuse=True)
                for c in range(KH):
                    last = pe.transpose(psX[:, 0, c * P:(c + 1) * P], aa[:, k, c * P:(c + 1) * P], K.ident[:, :])
                last.then_inc(act_turned, 1)

            def down(n, k):
                s = k if routed else 0
                pe.wait_ge(actT_made, n + 1)
                pe.wait_ge(y_taken, n + 1)
                pe.nop(nofuse=True)
                for a in range(2):
                    cols = slice(a * HALF, (a + 1) * HALF)
                    pe.matmul(psY[:, a, 0:HALF], K.ones3[:, :], br[:, s, 2 * HID + a * HALF:2 * HID + (a + 1) * HALF],
                              start=True, stop=False)
                    for c in range(KH):
                        last = pe.matmul(psY[:, a, 0:HALF], aT[:, k, c, :], Wd[:, s, c, cols], start=False,
                                         stop=(c == KH - 1))
                last.then_inc(y_made, 1)

            def first():
                turn_x(0, 0, 0)
                if not routed:
                    pe.wait_ge(weights_in[0], 64)
                gate(0, 0, 0)
                up(0, 0)
                turn_x(1, 1, 0)

            def step(n, k, it):
                gate(n, k, it)
                turn_act(n - 1, 1 - k)
                up(n, k)
                pe.wait_ge(actT_made, n)
                pe.nop(nofuse=True)
                turn_x(n + 1, 1 - k, it + (1 if k else 0))
                down(n - 1, 1 - k)

            def last():
                n = count - 1
                gate(n, 1, half - 1)
                turn_act(n - 1, 0)
                up(n, 1)
                down(n - 1, 0)
                turn_act(n, 1)
                down(n, 1)
            in_pairs(pe, first, step, last)

        @block.scalar
        def _(act):
            for k in range(2):
                act.sem_inc(y_out[k], 16)
            act.sem_inc(y_taken, 1)

            def take_x(n, k):
                act.wait_ge(x_turned, n + 1 + C)
                act.nop(nofuse=True)
                act.activation(xT[:, k, 0:4, :].rearrange("p c n -> p (c n)"), psX[:, 0, :], ACT.Copy)
                act.activation(xT[:, k, 4:KC, :].rearrange("p c n -> p (c n)"), psX[:, 1, 0:2 * P], ACT.Copy)\
                   .then_inc(xT_made, 1)

            def silu(n, k):
                act.wait_ge(up_made, n + 1)
                act.nop(nofuse=True)
                act.activation(su[:, k, :], psU[k][:, :], ACT.Silu).then_inc(silu_made, 1)

            def take_y(n, k, it):
                act.wait_ge(y_made, n + 1 + C)
                act.wait_ge(y_out[k], 16 * it + 16)
                act.nop(nofuse=True)
                act.activation(y[:, k, :].rearrange("p (a n) -> p a n", a=2), psY[:, :, 0:HALF], ACT.Copy)\
                   .then_inc(y_taken, 1)
                act.wait_ge(y_taken, n + 2)
                act.nop(nofuse=True)
                act.dma_start(yrows[bass.ds(n * P, P), :], y[:, k, :]).then_inc(y_out[k], 16)

            def first():
                take_x(0, 0)
                silu(0, 0)
                take_x(1, 1)

            def step(n, k, it):
                silu(n, k)
                take_x(n + 1, 1 - k)
                take_y(n - 1, 1 - k, it if k else it - 1)

            def last():
                silu(count - 1, 1)
                take_y(count - 2, 0, half - 1)
                take_y(count - 1, 1, half - 1)
                for k in range(2):
                    act.wait_ge(y_out[k], 16 * (half + 1))
            in_pairs(act, first, step, last)

        @block.vector
        def _(dve):
            dve.sem_inc(x_turned, C)
            dve.sem_inc(act_made, C)
            dve.sem_inc(y_made, C)

            def multiply(n, k):
                dve.wait_ge(silu_made, n + 1)
                dve.nop(nofuse=True)
                dve.tensor_tensor(aa[:, k, :], psG[k][:, :], su[:, k, :], ALU.mult).then_inc(act_made, 1)

            def take_act(n, k):
                dve.wait_ge(act_turned, n + 1)
                dve.nop(nofuse=True)
                dve.tensor_copy(aT[:, k, :, :].rearrange("p c n -> p (c n)"), psX[:, 0, :]).then_inc(actT_made, 1)

            def first():
                multiply(0, 0)

            def step(n, k, it):
                take_act(n - 1, 1 - k)
                multiply(n, k)

            def last():
                take_act(count - 2, 0)
                multiply(count - 1, 1)
                take_act(count - 1, 1)
            in_pairs(dve, first, step, last)


def combine(nc, K, A, out):
    with ExitStack() as ctx:
        def sem(n):
            return ctx.enter_context(stage_semaphore(nc, f"comb_{n}"))

        def sb(n, shape, dt):
            return ctx.enter_context(nc.sbuf_tensor(f"comb_{n}", shape, dt))
        gathered = [sem(f"gathered{k}") for k in range(2)]
        shared_in = [sem(f"shared_in{k}") for k in range(2)]
        stepped, tile_made, out_written = sem("stepped"), sem("tile_made"), sem("out_written")
        yq = sb("yq", [P, 2, TOPE, DM], F32)
        ys = sb("ys", [P, 2, DM], F32)
        block = ctx.enter_context(nc.Block())

        @block.gpsimd
        def _(pool):
            for t in range(NT):
                m = P if t < NT - 1 else NLAST
                if t >= 2:
                    pool.wait_ge(tile_made, t - 1)
                for q in range(TOPE):
                    pool.indirect_dma_start(yq[0:m, t % 2, q, :], None, K.pair_y,
                                            bass.IndirectOffsetOnAxis(ap=K.pair_row[0:m, q, t:t + 1], axis=0))\
                        .then_inc(gathered[t % 2], 16)

        @block.sync
        def _(sp):
            for t in range(NT):
                if t >= 2:
                    sp.wait_ge(tile_made, t - 1)
                sp.dma_start(ys[:, t % 2, :], K.shared_y[t * P:(t + 1) * P, :]).then_inc(shared_in[t % 2], 16)

        @block.scalar
        def _(act):
            for t in range(NT):
                m = P if t < NT - 1 else NLAST
                act.wait_ge(tile_made, t + 1)
                act.dma_start(out[t * P:t * P + m, :], K.h[0:m, t, :]).then_inc(out_written, 16)
            act.wait_ge(out_written, 16 * NT)

        @block.vector
        def _(dve):
            step = Chain(dve, stepped)
            for t in range(NT):
                m = P if t < NT - 1 else NLAST
                dve.wait_ge(shared_in[t % 2], 16 * (t // 2 + 1))
                dve.wait_ge(gathered[t % 2], 16 * TOPE * (t // 2 + 1))
                acc = ys[0:m, t % 2, :]
                for q in range(TOPE):
                    step(dve.scalar_tensor_tensor(out=acc, in0=yq[0:m, t % 2, q, :], scalar=K.pair_w[0:m, q, t:t + 1],
                                                  in1=acc, op0=ALU.mult, op1=ALU.add))
                dve.tensor_tensor(K.h[0:m, t, :], K.h[0:m, t, :], acc, ALU.add).then_inc(tile_made, 1)


def ffn(nc, K, A, out):
    K.xn_tab = nc.dram_tensor("xn_table", (NP, DM), F32).ap()
    K.pair_tab = nc.dram_tensor("pair_table", (P * TM, 1), I32).ap()
    K.bias_tab = nc.dram_tensor("bias_table", (NE + 1, 3, BW), BF16).ap()
    K.pair_y = nc.dram_tensor("pair_rows", (TM * P, DM), F32).ap()
    K.shared_y = nc.dram_tensor("shared_rows", (NP, DM), F32).ap()
    with ExitStack() as ctx:
        def sb(n, shape, dt):
            return ctx.enter_context(nc.sbuf_tensor(n, shape, dt))
        K.ones3 = sb("ones3", [3, P], BF16)
        K.tile_expert = sb("tile_expert", [P, TM], I32)
        K.pair_w = sb("pair_w", [P, TOPE, NT], F32)
        K.pair_row = sb("pair_row", [P, TOPE, NT], I32)
        K.pair_at = sb("pair_at", [P, TOPE, NT], I32)
        K.token_id = sb("token_id", [P, NT], I32)
        K.pairs = sb("pairs", [P, TM], I32)
        with ExitStack() as c2:
            made = c2.enter_context(stage_semaphore(nc, "ones3_made"))
            block = c2.enter_context(nc.Block())

            @block.vector
            def _(dve):
                dve.memset(K.ones3[:, :], 1.0).then_inc(made, 1)
                dve.wait_ge(made, 1)
        bias_parts(nc, K, A)
        with ExitStack() as c2:
            K.xn = c2.enter_context(nc.sbuf_tensor("xn", [P, NT, DM], F32))
            norm_block(nc, K, "ln_ffn", K.h, K.xn)
            route(nc, K, A)
        expert_tiles(nc, K, A, "shared", NT, False)
        expert_tiles(nc, K, A, "routed", TM, True)
        combine(nc, K, A, out)


def build(nc, A, out):
    RETIRED.clear()
    K = Keep()
    K.srt_src = nc.dram_tensor("sorted_src", (1, E + GE), I32).ap()
    K.srt_dst = nc.dram_tensor("sorted_dst", (1, E + GE), I32).ap()
    K.hs_tab = nc.dram_tensor("hs_table", (NP, ROW), F32).ap()
    K.bounce = [nc.dram_tensor(f"bounce{i}", (P, 2 * NC), F32).ap() for i in range(4)]
    with ExitStack() as ctx:
        def sb(n, shape, dt):
            return ctx.enter_context(nc.sbuf_tensor(n, shape, dt))
        K.ident = sb("ident", [P, P], F32)
        K.ones = sb("ones", [P, P], F32)
        K.iota_free = sb("iota_free", [P, P], F32)
        K.iota_part = sb("iota_part", [P, 1], F32)
        K.h = sb("h", [P, NT, DM], F32)
        constants(nc, K)
        with ExitStack() as c2:
            x_in = c2.enter_context(nc.sbuf_tensor("x_in", [P, NT, DM], F32))
            norm_block(nc, K, "ln_in", x_in, K.h, load=A["x"])
        with ExitStack() as c2:
            K.lnw, K.lnb, K.onw, K.onb = (c2.enter_context(nc.sbuf_tensor(n, [P, DM], F32))
                                          for n in ("ln_w", "ln_b", "on_w", "on_b"))
            gnn(nc, K, A)
            x_again = c2.enter_context(nc.sbuf_tensor("x_again", [P, NT, DM], F32))
            norm_block(nc, K, f"ln{L - 1}", K.h, K.h, K.lnw, K.lnb, also=(K.onw, K.onb, x_again), load=A["x"],
                       load_to=x_again)
        recycle(nc)
        ffn(nc, K, A, out)


_INS = ['x', 'src', 'dst', 'L0_gnn_Wsrc', 'L0_gnn_bsrc', 'L0_gnn_Wdst', 'L0_gnn_bdst', 'L0_gnn_attn', 'L0_gnn_ln_w',
        'L0_gnn_ln_b', 'L0_gnn_on_w', 'L0_gnn_on_b', 'L0_ffn_gate_w', 'L0_ffn_gate_b', 'L0_ffn_bias', 'L0_ffn_Wu',
        'L0_ffn_bu', 'L0_ffn_Wg', 'L0_ffn_bg', 'L0_ffn_Wd', 'L0_ffn_bd', 'L0_ffn_sWu', 'L0_ffn_sbu', 'L0_ffn_sWg',
        'L0_ffn_sbg', 'L0_ffn_sWd', 'L0_ffn_sbd']
_OUTS = [((N, DM), 'float32')]


def kernel(**inputs):
    import numpy as _np
    import concourse.bacc as _bacc
    from concourse import mybir as _mybir
    from concourse.bass_utils import run_bass_kernel_spmd as _run

    nc = _bacc.Bacc("TRN2", target_bir_lowering=False, num_devices=1)
    arrays, args = {}, {}
    for name in _INS:
        a = _np.ascontiguousarray(inputs[name])
        arrays[f"in_{name}_dram"] = a
        args[name] = nc.dram_tensor(f"in_{name}_dram", a.shape, _mybir.dt.from_np(a.dtype), kind="ExternalInput").ap()
    out = nc.dram_tensor("out_0_dram", _OUTS[0][0], _mybir.dt.from_np(_np.dtype(_OUTS[0][1])),
                         kind="ExternalOutput").ap()
    build(nc, args, out)
    r = _run(nc, [arrays], core_ids=[0])
    return r.results[0]["out_0_dram"]
```

```python
from contextlib import ExitStack, contextmanager

import concourse.bass as bass
from concourse import mybir

P = 128
N = 1250
E = 21250
DM = 768
H = 8
HD = DM // H
L = 2
NT = (N + P - 1) // P
NLAST = N - (NT - 1) * P
NP = NT * P
KC = DM // P
HALF = DM // 2
HH = H // 2
HW = HALF + HH
ROW = 2 * HW
GE = 2 * P
NG = (E + NT * (GE - 1)) // GE
NG += NG % 2
NTILE = 2 * NG
RING_LOGITS = 6
LAG = 5
RING_SUMS = 4
TPC = P // H
NC = (NTILE + TPC - 1) // TPC
NTP = NC * TPC
SENTINEL = 4095
UNIT = 64
UNITS = GE // UNIT + 1
ES = (E + GE + UNIT) // UNIT * UNIT
BIG = 1.0e30
EL = 125
EC = E // EL
SLOPE = 0.2
LN_EPS = 1e-5

F32 = mybir.dt.float32
I32 = mybir.dt.int32
BF16 = mybir.dt.bfloat16
ALU = mybir.AluOpType
ACT = mybir.ActivationFunctionType
AX = mybir.AxisListType


@contextmanager
def stage_semaphore(nc, name):
    handle = nc.alloc_semaphore(name)
    yield handle
    RETIRED.append(handle)


RETIRED = []


def recycle(nc):
    nc.clear_and_free_semaphores(list(RETIRED))
    RETIRED.clear()
    nc.all_engine_barrier()


class Chain:

    def __init__(self, eng, sem):
        self.eng, self.sem, self.n = eng, sem, 0

    def __call__(self, instruction):
        self.n += 1
        instruction.then_inc(self.sem, 1)
        self.eng.wait_ge(self.sem, self.n)


def bcast(row, parts):
    return row.rearrange("(a n) -> a n", a=1).broadcast_to([parts, row.shape[0]])


def constants(nc, K):
    with ExitStack() as ctx:
        s_zero = ctx.enter_context(stage_semaphore(nc, "identity_zeroed"))
        s_all = ctx.enter_context(stage_semaphore(nc, "constants_made"))
        block = ctx.enter_context(nc.Block())

        @block.gpsimd
        def _(pool):
            pool.memset(K.ident[:, :], 0.0).then_inc(s_zero, 1)
            pool.memset(K.ones[:, :], 1.0).then_inc(s_all, 1)
            pool.wait_ge(s_zero, 1)
            pool.affine_select(out=K.ident[:, :], in_=K.ident[:, :], compare_op=ALU.not_equal, fill=1.0,
                               base=0, pattern=[[-1, P]], channel_multiplier=1).then_inc(s_all, 1)
            pool.iota(K.iota_free[:, :], [[1, P]], base=0, channel_multiplier=0,
                      allow_small_or_imprecise_dtypes=True).then_inc(s_all, 1)
            pool.iota(K.iota_part[:, :], [[0, 1]], base=0, channel_multiplier=1,
                      allow_small_or_imprecise_dtypes=True).then_inc(s_all, 1)
            pool.wait_ge(s_all, 4)


def norm_block(nc, K, name, src, dst, weight=None, bias=None, also=None, load=None, load_to=None):
    load_to = src if load_to is None else load_to
    """dst = layernorm(src) * weight + bias over [P, NT, DM]; weight and bias are rows in every partition.

    load: DRAM [N, DM] read into src first. also: (weight2, bias2, other): dst = dst normalised once more
    with weight2/bias2 plus other."""
    with ExitStack() as ctx:
        def sem(n):
            return ctx.enter_context(stage_semaphore(nc, f"{name}_{n}"))
        loaded, stepped, dev_made, root_made = sem("loaded"), sem("stepped"), sem("deviation_made"), sem("root_made")
        stats = ctx.enter_context(nc.sbuf_tensor(f"{name}_stats", [P, NT, 2, 6], F32))
        mv = ctx.enter_context(nc.sbuf_tensor(f"{name}_mv", [P, NT, 2], F32))
        var = ctx.enter_context(nc.sbuf_tensor(f"{name}_var", [P, NT], F32))
        std = ctx.enter_context(nc.sbuf_tensor(f"{name}_std", [P, NT], F32))
        rstd = ctx.enter_context(nc.sbuf_tensor(f"{name}_rstd", [P, NT], F32))
        block = ctx.enter_context(nc.Block())

        if load is not None:
            @block.sync
            def _(sp):
                sp.wait_ge(stepped, 1)
                sp.dma_start(load_to[:, 0:NT - 1, :], load[0:(NT - 1) * P, :].rearrange("(t p) d -> p t d", p=P))\
                  .then_inc(loaded, 16)
                sp.dma_start(load_to[0:NLAST, NT - 1, :], load[(NT - 1) * P:N, :]).then_inc(loaded, 16)

        @block.vector
        def _(dve):
            step = Chain(dve, stepped)
            if load is not None:
                step(dve.memset(load_to[:, NT - 1, :], 0.0))
                dve.wait_ge(loaded, 32)

            def stats_of(x):
                for t in range(NT):
                    for h in range(2):
                        last = dve.bn_stats(stats[:, t, h, :], x[:, t, h * HALF:(h + 1) * HALF])
                step(last)
                for t in range(NT):
                    last = dve.bn_aggr(mv[:, t, :], stats[:, t, :, :].rearrange("p a b -> p (a b)"))
                step(last)

            def normalise(x, y, n):
                dve.tensor_scalar(var[:, :], mv[:, :, 1], LN_EPS, None, ALU.add).then_inc(dev_made, 1)
                dve.wait_ge(root_made, n)
                step(dve.reciprocal(rstd[:, :], std[:, :]))
                for t in range(NT):
                    last = dve.tensor_scalar(y[:, t, :], x[:, t, :], mv[:, t, 0:1], rstd[:, t:t + 1],
                                             ALU.subtract, ALU.mult)
                step(last)

            def affine(y, w, b):
                for t in range(NT):
                    last = dve.tensor_tensor(y[:, t, :], y[:, t, :], w[:, :], ALU.mult)
                step(last)
                for t in range(NT):
                    last = dve.tensor_tensor(y[:, t, :], y[:, t, :], b[:, :], ALU.add)
                step(last)

            stats_of(src)
            normalise(src, dst, 1)
            if weight is not None:
                affine(dst, weight, bias)
            if also is not None:
                w2, b2, other = also
                stats_of(dst)
                normalise(dst, dst, 2)
                affine(dst, w2, b2)
                for t in range(NT):
                    last = dve.tensor_tensor(dst[:, t, :], dst[:, t, :], other[:, t, :], ALU.add)
                step(last)

        @block.scalar
        def _(act):
            for n in range(1 if also is None else 2):
                act.wait_ge(dev_made, n + 1)
                act.activation(std[:, :], var[:, :], ACT.Sqrt).then_inc(root_made, 1)


def order_edges(nc, K, src, dst):
    with ExitStack() as ctx:
        def sem(n):
            return ctx.enter_context(stage_semaphore(nc, f"order_{n}"))

        def sb(n, shape, dt):
            return ctx.enter_context(nc.sbuf_tensor(f"order_{n}", shape, dt))
        tails_set, tails_out, last_set, edges_in, compared, counted, stepped = (
            sem("tails_set"), sem("tails_out"), sem("last_set"), sem("edges_in"), sem("compared"), sem("counted"),
            sem("stepped"))
        tails = sb("tails", [1, 2, ES - E], I32)
        nxt = sb("nxt", [EL, EC], I32)
        junk = sb("junk", [EL, EC], F32)
        falls = sb("falls", [EL, 1], F32)
        some = sb("some", [P, 1], F32)
        flags = sb("flags", [P, 2], I32)
        ps = ctx.enter_context(nc.psum_tensor("order_ps", [P, 1], F32))
        with nc.Block() as block:
            @block.sync
            def _(sp):
                sp.dma_start(K.dall[:, :], dst.rearrange("(p c) -> p c", p=EL)).then_inc(edges_in, 16)
                sp.dma_start(K.sall[:, :], src.rearrange("(p c) -> p c", p=EL)).then_inc(edges_in, 16)
                sp.wait_ge(last_set, 1)
                sp.dma_start(nxt[0:EL - 1, :], dst[1:1 + (EL - 1) * EC].rearrange("(p c) -> p c", p=EL - 1))\
                  .then_inc(edges_in, 16)
                sp.dma_start(nxt[EL - 1:EL, 0:EC - 1], dst[1 + (EL - 1) * EC:E].rearrange("(a n) -> a n", a=1))\
                  .then_inc(edges_in, 16)
                sp.wait_ge(tails_set, 2)
                sp.dma_start(K.srt_src[0:1, E:ES], tails[:, 0, :]).then_inc(tails_out, 16)
                sp.dma_start(K.srt_dst[0:1, E:ES], tails[:, 1, :]).then_inc(tails_out, 16)
                sp.wait_ge(tails_out, 32)

            @block.gpsimd
            def _(pool):
                pool.memset(nxt[:, EC - 1:EC], SENTINEL).then_inc(last_set, 1)
                pool.memset(tails[:, 0, :], 0).then_inc(tails_set, 1)
                pool.memset(tails[:, 1, :], SENTINEL).then_inc(tails_set, 1)

            @block.vector
            def _(dve):
                step = Chain(dve, stepped)
                dve.wait_ge(edges_in, 64)
                step(dve.tensor_copy(K.dallf[:, :], K.dall[:, :]))
                step(dve.tensor_tensor(junk[:, :], K.dallf[:, :], nxt[:, :], ALU.is_gt))
                dve.tensor_reduce(falls[:, :], junk[:, :], AX.X, ALU.add).then_inc(compared, 1)
                dve.wait_ge(counted, 1)
                step(dve.tensor_scalar(some[:, :], ps[:, :], 1.0, None, ALU.min))
                step(dve.tensor_copy(flags[:, 0:1], some[:, :]))
                step(dve.tensor_scalar(flags[:, 1:2], some[:, :], -1.0, 1.0, ALU.mult, ALU.add))

            @block.tensor
            def _(pe):
                pe.wait_ge(compared, 1)
                pe.matmul(ps[:, :], K.ones[0:EL, :], falls[:, :], start=True, stop=True).then_inc(counted, 1)

        counting_sort(nc, ctx, K, src, dst, flags)


def counting_sort(nc, ctx, K, src, dst, flags):
    BINS = NP

    def sem(n):
        return ctx.enter_context(stage_semaphore(nc, f"sort_{n}"))

    def sb(n, shape, dt):
        return ctx.enter_context(nc.sbuf_tensor(f"sort_{n}", shape, dt))
    copied, tables, onehot_made, counted, stepped, placed, before_made, after_made, column_set, scattered, places_free = (
        sem("copied"), sem("tables"), sem("onehot_made"), sem("counted"), sem("stepped"), sem("placed"),
        sem("before_made"), sem("after_made"), sem("column_set"), sem("scattered"), sem("places_free"))
    bins = sb("bins", [P, BINS], F32)
    oh = sb("oh", [EL, BINS], BF16)
    cnt = sb("cnt", [P, BINS], F32)
    base = sb("base", [P, BINS], F32)
    zer = sb("zer", [P, BINS], F32)
    prod = sb("prod", [EL, BINS], F32)
    upper, rest, onesb = (sb(x, [P, P], BF16) for x in ("upper", "rest", "onesb"))
    pf = sb("pf", [EL, 1], F32)
    pi, si, di = (sb(x, [EL, 1], I32) for x in ("pi", "si", "di"))
    ps = ctx.enter_context(nc.psum_tensor("sort_ps", [P, 3 * 512], F32))
    cuts = [(a, min(a + 512, BINS)) for a in range(0, BINS, 512)]
    block = ctx.enter_context(nc.Block())

    def flag(eng):
        return eng.value_load(flags[0:1, 0:1], min_val=0, max_val=1)

    @block.sync
    def _(sp):
        with sp.If(sp.value_load(flags[0:1, 1:2], min_val=0, max_val=1)):
            sp.dma_start(K.srt_src[0:1, 0:E], src.rearrange("(a n) -> a n", a=1)).then_inc(copied, 16)
            sp.dma_start(K.srt_dst[0:1, 0:E], dst.rearrange("(a n) -> a n", a=1)).then_inc(copied, 16)
            sp.wait_ge(copied, 32)

    @block.gpsimd
    def _(pool):
        with pool.If(flag(pool)):
            pool.iota(bins[:, :], [[1, BINS]], base=0, channel_multiplier=0,
                      allow_small_or_imprecise_dtypes=True).then_inc(tables, 1)
            for x in (upper, rest, onesb):
                pool.memset(x[:, :], 1.0).then_inc(tables, 1)
            pool.wait_ge(tables, 4)
            pool.affine_select(out=upper[:, :], in_=upper[:, :], compare_op=ALU.is_gt, fill=0.0, base=0,
                               pattern=[[1, P]], channel_multiplier=-1).then_inc(tables, 1)
            pool.affine_select(out=rest[:, :], in_=rest[:, :], compare_op=ALU.is_ge, fill=0.0, base=0,
                               pattern=[[-1, P]], channel_multiplier=1).then_inc(tables, 1)
            with pool.Fori(0, EC) as c:
                pool.tensor_copy(si[:, :], K.sall[:, bass.ds(c, 1)]).then_inc(column_set, 1)
                pool.tensor_copy(di[:, :], K.dall[:, bass.ds(c, 1)]).then_inc(column_set, 1)
                pool.wait_ge(placed, c + 1)
                pool.nop(nofuse=True)
                pool.wait_ge(column_set, 2 * c + 2)
                pool.nop(nofuse=True)
                for col, out in ((si, K.srt_src), (di, K.srt_dst)):
                    pool.indirect_dma_start(out.rearrange("a n -> (a n)").rearrange("(n b) -> n b", b=1),
                                            bass.IndirectOffsetOnAxis(ap=pi[:, :], axis=0), col[:, :], None)\
                        .then_inc(scattered, 16)
                pool.wait_ge(scattered, 32 * c + 32)
                pool.nop(nofuse=True)
                pool.sem_inc(places_free, 1)

    @block.tensor
    def _(pe):
        def add_up(weights, moving, start, stop):
            for a, b in cuts:
                last = pe.matmul(ps[:, a:b], weights, moving[:, a:b], start=start, stop=stop, skip_group_check=True)
            return last

        with pe.If(flag(pe)):
            pe.wait_ge(tables, 6)
            pe.wait_ge(stepped, 1)
            add_up(K.ident[:, :], zer, True, False)
            with pe.Fori(0, EC) as c:
                pe.wait_ge(onehot_made, c + 1)
                pe.nop(nofuse=True)
                add_up(onesb[0:EL, :], oh, False, False).then_inc(after_made, 1)
            add_up(K.ident[:, :], zer, False, True).then_inc(counted, 1)
            pe.wait_ge(counted, 2)
            add_up(K.ident[:, :], base, True, False)
            with pe.Fori(0, EC) as c:
                pe.wait_ge(onehot_made, c + EC + 1)
                pe.nop(nofuse=True)
                add_up(upper[0:EL, :], oh, False, False).then_inc(before_made, 1)
                pe.wait_ge(placed, c + 1)
                pe.nop(nofuse=True)
                add_up(rest[0:EL, :], oh, False, False).then_inc(after_made, 1)
            add_up(K.ident[:, :], zer, False, True).then_inc(counted, 1)

    @block.vector
    def _(dve):
        with dve.If(flag(dve)):
            step = Chain(dve, stepped)
            dve.sem_inc(places_free, 1)
            dve.sem_inc(after_made, 1)
            step(dve.memset(zer[:, :], 0.0))
            dve.wait_ge(tables, 6)

            def onehot(c, n):
                dve.wait_ge(after_made, n + 1)
                dve.nop(nofuse=True)
                dve.tensor_scalar(oh[:, :], bins[0:EL, :], K.dallf[:, bass.ds(c, 1)], None, ALU.is_equal)\
                   .then_inc(onehot_made, 1)

            with dve.Fori(0, EC) as c:
                onehot(c, c)
            dve.wait_ge(counted, 1)
            step(dve.tensor_copy(cnt[:, :], ps[:, 0:BINS]))
            step(dve.tensor_tensor_scan(base[:, :], cnt[:, :], zer[:, :], 0.0, ALU.add, ALU.add))
            dve.tensor_tensor(base[:, :], base[:, :], cnt[:, :], ALU.subtract).then_inc(counted, 1)
            dve.wait_ge(counted, 2)
            with dve.Fori(0, EC) as c:
                onehot(c, c + EC)
                dve.wait_ge(before_made, c + 1)
                dve.nop(nofuse=True)
                dve.tensor_tensor(prod[:, :], ps[0:EL, 0:BINS], oh[:, :], ALU.mult).then_inc(stepped, 1)
                dve.wait_ge(stepped, 2 * c + step.n + 1)
                dve.nop(nofuse=True)
                dve.tensor_reduce(pf[:, :], prod[:, :], AX.X, ALU.add).then_inc(stepped, 1)
                dve.wait_ge(places_free, c + 1)
                dve.nop(nofuse=True)
                dve.wait_ge(stepped, 2 * c + step.n + 2)
                dve.nop(nofuse=True)
                dve.tensor_copy(pi[:, :], pf[:, :]).then_inc(placed, 1)
            dve.wait_ge(counted, 3)


def edge_tables(nc, K):
    NB = NT
    with ExitStack() as ctx:
        def sem(n):
            return ctx.enter_context(stage_semaphore(nc, f"edges_{n}"))

        def sb(n, shape, dt):
            return ctx.enter_context(nc.sbuf_tensor(f"edges_{n}", shape, dt))
        stepped, counted = sem("stepped"), sem("counted")
        rows_in, units_made, rows_made, turned = sem("rows_in"), sem("units_made"), sem("rows_made"), sem("turned")
        junk = sb("junk", [EL, EC], F32)
        cnt = sb("cnt", [EL, NB + 1], F32)
        st = sb("st", [P, NB + 1], F32)
        sz = sb("sz", [P, NB], F32)
        szi = sb("szi", [P, NB], I32)
        zer = sb("zer", [P, NB], F32)
        ginc = sb("ginc", [P, NB], F32)
        cbase = sb("cbase", [P, NB + 1], F32)
        ig = sb("ig", [P, NG], F32)
        blk = sb("blk", [P, NG], F32)
        offf = sb("offf", [P, NG], F32)
        tmp = sb("tmp", [P, NG], F32)
        first = sb("first", [P, 1], F32)
        first_i = sb("first_i", [P, 1], I32)
        unit_i = sb("unit_i", [P, UNITS], I32)
        bit = sb("bit", [P, 1], F32)
        rows = sb("rows", [P, 2, UNITS * UNIT], I32)
        rows_f = sb("rows_f", [P, 2, UNITS * UNIT], F32)
        moved = sb("moved", [P, 2, UNITS * UNIT], F32)
        own = sb("own", [P, NTILE], F32)
        iota_made = sem("iota_made")
        ps = ctx.enter_context(nc.psum_tensor("edges_ps", [P, 512], F32))
        psT = ctx.enter_context(nc.psum_tensor("edges_psT", [P, 2, 2, P], F32))
        block = ctx.enter_context(nc.Block())

        @block.gpsimd
        def _(pool):
            pool.iota(ig[:, :], [[1, NG]], base=0, channel_multiplier=0,
                      allow_small_or_imprecise_dtypes=True).then_inc(iota_made, 1)
            for c in range(UNITS):
                pool.wait_ge(units_made, c + 1)
                for i, arr in enumerate((K.srt_src, K.srt_dst)):
                    pool.indirect_dma_start(rows[0:NG, i, c * UNIT:(c + 1) * UNIT], None,
                                            arr.rearrange("a (n u) -> (a n) u", u=UNIT),
                                            bass.IndirectOffsetOnAxis(ap=unit_i[0:NG, c:c + 1], axis=0))\
                        .then_inc(rows_in, 16)

        @block.vector
        def _(dve):
            step = Chain(dve, stepped)
            for b in range(NB + 1):
                step(dve.tensor_scalar(junk[:, :], K.dallf[:, :], float(P * b), 0.0, ALU.is_lt, ALU.add,
                                       accum_out=cnt[:, b:b + 1]))
            dve.engine_nop().then_inc(counted, 1)
            dve.wait_ge(counted, 2)
            step(dve.tensor_copy(st[:, :], ps[:, 0:NB + 1]))
            step(dve.tensor_tensor(sz[:, :], st[:, 1:NB + 1], st[:, 0:NB], ALU.subtract))
            step(dve.tensor_scalar(szi[:, :], sz[:, :], float(GE - 1), None, ALU.add))
            step(dve.tensor_scalar(szi[:, :], szi[:, :], GE.bit_length() - 1, None, ALU.arith_shift_right))
            step(dve.tensor_copy(sz[:, :], szi[:, :]))
            step(dve.memset(zer[:, :], 0.0))
            step(dve.tensor_tensor_scan(ginc[:, :], sz[:, :], zer[:, :], 0.0, ALU.add, ALU.add))
            step(dve.tensor_tensor(sz[:, :], ginc[:, :], sz[:, :], ALU.subtract))
            step(dve.memset(cbase[:, NB:NB + 1], float(E)))
            step(dve.scalar_tensor_tensor(out=cbase[:, 0:NB], in0=sz[:, :], scalar=-float(GE), in1=st[:, 0:NB],
                                          op0=ALU.mult, op1=ALU.add))
            dve.wait_ge(iota_made, 1)
            step(dve.memset(blk[:, :], 0.0))
            for b in range(NB):
                step(dve.scalar_tensor_tensor(out=blk[:, :], in0=ig[:, :], scalar=ginc[:, b:b + 1], in1=blk[:, :],
                                              op0=ALU.is_ge, op1=ALU.add))
            step(dve.tensor_scalar(offf[:, :], ig[:, :], float(GE), None, ALU.mult))
            for b in range(NB + 1):
                step(dve.tensor_scalar(tmp[:, :], blk[:, :], float(b), cbase[:, b:b + 1], ALU.is_equal, ALU.mult))
                step(dve.tensor_tensor(offf[:, :], offf[:, :], tmp[:, :], ALU.add))
            step(dve.tensor_scalar(offf[:, :], offf[:, :], float(E), 0.0, ALU.min, ALU.max))
            step(dve.tensor_scalar(blk[:, :], blk[:, :], float(NB - 1), None, ALU.min))
            step(dve.tensor_copy(K.off_i[:, :], offf[:, :]))
            step(dve.tensor_copy(K.blk_i[:, :], blk[:, :]))
            step(dve.tensor_scalar(K.blkiota[:, :], blk[:, :], float(P), K.iota_part[:, 0:1], ALU.mult, ALU.add))
            step(dve.tensor_tensor(offf[:, :], offf[:, :], K.ident[:, 0:NG], ALU.mult))
            step(dve.tensor_reduce(first[:, :], offf[:, :], AX.X, ALU.add))
            step(dve.tensor_copy(first_i[:, :], first[:, :]))
            step(dve.tensor_scalar(unit_i[:, 0:1], first_i[:, :], UNIT.bit_length() - 1, None, ALU.arith_shift_right))
            dve.engine_nop().then_inc(units_made, 1)
            for c in range(1, UNITS):
                dve.tensor_scalar(unit_i[:, c:c + 1], unit_i[:, 0:1], float(c), None, ALU.add).then_inc(units_made, 1)
            step(dve.tensor_scalar(first_i[:, :], first_i[:, :], UNIT - 1, None, ALU.bitwise_and))
            step(dve.tensor_copy(first[:, :], first_i[:, :]))
            step(dve.tensor_scalar(tmp[:, :], blk[:, :], float(P), None, ALU.mult))
            step(dve.memset(K.dcolf[:, NTILE:NTP], float(SENTINEL)))
            dve.wait_ge(rows_in, 32 * UNITS)
            step(dve.tensor_copy(rows_f[:NG, :, :], rows[:NG, :, :]))
            w, by = UNITS * UNIT, UNIT // 2
            while by:
                step(dve.tensor_scalar(bit[:, 0:1], first[:, :], float(by), None, ALU.is_ge))
                step(dve.scalar_tensor_tensor(out=first[:, :], in0=bit[:, 0:1], scalar=-float(by), in1=first[:, :],
                                              op0=ALU.mult, op1=ALU.add))
                step(dve.tensor_tensor(moved[:NG, :, 0:w - by], rows_f[:NG, :, by:w], rows_f[:NG, :, 0:w - by],
                                       ALU.subtract))
                step(dve.scalar_tensor_tensor(out=rows_f[:NG, :, 0:w - by], in0=moved[:NG, :, 0:w - by],
                                              scalar=bit[:NG, 0:1], in1=rows_f[:NG, :, 0:w - by],
                                              op0=ALU.mult, op1=ALU.add))
                w, by = w - by, by // 2
            dve.engine_nop().then_inc(rows_made, 1)
            dve.wait_ge(turned, 1)
            for i, col in enumerate((K.srccol, K.dcolf)):
                step(dve.tensor_copy(col[:, 0:NTILE].rearrange("p (g j) -> p j g", j=2), psT[:, i, :, 0:NG]))
            step(dve.tensor_tensor(K.drel[:, :].rearrange("p (g j) -> p g j", j=2),
                                   K.dcolf[:, 0:NTILE].rearrange("p (g j) -> p g j", j=2),
                                   tmp[:, :].rearrange("p (g j) -> p g j", j=1).broadcast_to([P, NG, 2]),
                                   ALU.subtract))
            for bound, op in ((0.0, ALU.is_ge), (float(P), ALU.is_lt)):
                step(dve.tensor_scalar(own[:, :], K.drel[:, :], bound, None, op))
                step(dve.tensor_scalar(K.dcolf[:, 0:NTILE], K.dcolf[:, 0:NTILE], -float(SENTINEL), None, ALU.add))
                step(dve.tensor_tensor(K.dcolf[:, 0:NTILE], K.dcolf[:, 0:NTILE], own[:, :], ALU.mult))
                step(dve.tensor_scalar(K.dcolf[:, 0:NTILE], K.dcolf[:, 0:NTILE], float(SENTINEL), None, ALU.add))

        @block.tensor
        def _(pe):
            pe.wait_ge(counted, 1)
            pe.matmul(ps[:, 0:NB + 1], K.ones[0:EL, :], cnt[:, :], start=True, stop=True).then_inc(counted, 1)
            pe.wait_ge(rows_made, 1)
            for i in range(2):
                for j in range(2):
                    last = pe.transpose(psT[:, i, j, 0:NG], rows_f[0:NG, i, j * P:(j + 1) * P], K.ident[0:NG, 0:NG])
            last.then_inc(turned, 1)


def segment_tables(nc, K):
    with ExitStack() as ctx:
        def sem(n):
            return ctx.enter_context(stage_semaphore(nc, f"seg_{n}"))

        def sb(n, shape, dt):
            return ctx.enter_context(nc.sbuf_tensor(f"seg_{n}", shape, dt))
        stepped, turned, ends_out, rows_in, links_out, links_in = (
            sem("stepped"), sem("turned"), sem("ends_out"), sem("rows_in"), sem("links_out"), sem("links_in"))
        drep = sb("drep", [P, NTP, H], F32)
        dT = sb("dT", [P, NC, P], F32)
        ends = sb("ends", [P, 2, NC], F32)
        rows = sb("rows", [H, 2, NC, TPC], F32)
        link = sb("link", [H, 2, NC * TPC], F32)
        whole = sb("whole", [H, NC * TPC], F32)
        linkT = sb("linkT", [P, 2, NC], F32)
        ps = [ctx.enter_context(nc.psum_tensor(f"seg_ps{i}", [P, 512], F32)) for i in range(3)]
        made = sem("made")
        block = ctx.enter_context(nc.Block())

        @block.tensor
        def _(pe):
            pe.wait_ge(made, 1)
            for c in range(NC):
                last = pe.transpose(ps[c // 4][:, (c % 4) * P:(c % 4 + 1) * P],
                                    drep[:, c * TPC:(c + 1) * TPC, :].rearrange("p t h -> p (t h)"), K.ident[:, :])
            last.then_inc(turned, 1)

        @block.sync
        def _(sp):
            sp.wait_ge(made, 2)
            sp.dma_start(K.bounce[0], ends[:, :, :].rearrange("p a c -> p (a c)")).then_inc(ends_out, 16)
            sp.wait_ge(ends_out, 16)
            for a in range(2):
                for c in range(NC):
                    sp.dma_start(rows[:, a, c, :], K.bounce[0].rearrange("(t h) n -> h t n", h=H)[:, :, a * NC + c],
                             allow_slow_non_contiguous=True).then_inc(rows_in, 16)
            sp.wait_ge(made, 3)
            sp.dma_start(K.bounce[1].rearrange("(h a) n -> h (a n)", h=H)[:, 0:2 * NTP],
                         link[:, :, :].rearrange("h a n -> h (a n)")).then_inc(links_out, 16)
            sp.wait_ge(links_out, 16)
            for h in range(H):
                for t in range(1):
                    pass
            lv = K.bounce[1].rearrange("(h a) n -> h (a n)", h=H)[:, 0:2 * NTP]\
                  .rearrange("h (a c t) -> t h a c", a=2, t=TPC)
            for t in range(TPC):
                sp.dma_start(linkT[t * H:(t + 1) * H, :, :], lv[t], allow_slow_non_contiguous=True)\
                  .then_inc(links_in, 16)

        @block.vector
        def _(dve):
            step = Chain(dve, stepped)
            dve.tensor_copy(drep[:, :, :], K.dcolf[:, :].rearrange("p (t h) -> p t h", h=1)
                            .broadcast_to([P, NTP, H])).then_inc(made, 1)
            dve.wait_ge(turned, 1)
            for i in range(3):
                last = dve.tensor_copy(dT[:, 4 * i:4 * i + 4, :].rearrange("p c l -> p (c l)"), ps[i][:, :])
            step(last)
            step(dve.tensor_copy(ends[:, 0, :], dT[:, :, 0]))
            dve.tensor_copy(ends[:, 1, :], dT[:, :, P - 1]).then_inc(made, 1)

            def penalty(out, mask):
                return dve.tensor_scalar(out, mask, 1.0, BIG, ALU.subtract, ALU.mult)

            same = K.pen_start
            step(dve.memset(K.pen_start[:, :, 0:1], -BIG))
            step(dve.memset(K.pen_end[:, :, P - 1:P], -BIG))
            step(dve.tensor_tensor(K.pen_start[:, :, 1:P], dT[:, :, 1:P], dT[:, :, 0:P - 1], ALU.is_equal))
            step(penalty(K.pen_start[:, :, 1:P], K.pen_start[:, :, 1:P]))
            step(dve.tensor_copy(K.pen_end[:, :, 0:P - 1], K.pen_start[:, :, 1:P]))
            dve.wait_ge(rows_in, 16 * 2 * NC)
            first = rows[:, 0, :, :].rearrange("h c t -> h (c t)")
            last_ = rows[:, 1, :, :].rearrange("h c t -> h (c t)")
            step(dve.memset(link[:, :, :], 0.0))
            step(dve.tensor_tensor(link[:, 0, 1:NTP], first[:, 1:NTP], last_[:, 0:NTP - 1], ALU.is_equal))
            step(dve.tensor_copy(link[:, 1, 0:NTP - 1], link[:, 0, 1:NTP]))
            step(dve.tensor_tensor(whole[:, :], first, last_, ALU.is_equal))
            for a in range(2):
                step(dve.tensor_tensor(K.pen_carry[:, a, :], whole[:, :], link[:, a, :], ALU.mult))
                step(penalty(K.pen_carry[:, a, :], K.pen_carry[:, a, :]))
            dve.engine_nop().then_inc(made, 1)
            dve.wait_ge(links_in, 16 * TPC)
            for a, pen in ((0, K.pen_first), (1, K.pen_last)):
                e = ends[:, a, :].rearrange("p (c l) -> p c l", l=1).broadcast_to([P, NC, P])
                lk = linkT[:, a, :].rearrange("p (c l) -> p c l", l=1).broadcast_to([P, NC, P])
                step(dve.tensor_tensor(pen[:, :, :], dT[:, :, :], e, ALU.is_equal))
                step(dve.tensor_tensor(pen[:, :, :], pen[:, :, :], lk, ALU.mult))
                step(penalty(pen[:, :, :], pen[:, :, :]))


def project(nc, K, l, A):
    with ExitStack() as ctx:
        def sem(n):
            return ctx.enter_context(stage_semaphore(nc, f"proj{l}_{n}"))

        def sb(n, shape, dt):
            return ctx.enter_context(nc.sbuf_tensor(f"proj{l}_{n}", shape, dt))
        weights_in, rows_in, turned, hT_made, proj_made, out_made, table_out, parts = (
            sem("weights_in"), sem("rows_in"), sem("turned"), sem("hT_made"), sem("proj_made"), sem("out_made"),
            sem("table_out"), sem("parts"))
        stepped = sem("stepped")
        Ws = sb("Ws", [P, KC, DM], F32)
        Wd = sb("Wd", [P, KC, DM], F32)
        brow = sb("brow", [P, 2, DM], F32)
        arow = sb("arow", [P, DM], F32)
        hT = sb("hT", [P, 2, KC, P], F32)
        row = sb("row", [P, 2, 2, HW], F32)
        prod = sb("prod", [P, DM], F32)
        rest = sb("rest", [P, ROW], F32)
        psT = ctx.enter_context(nc.psum_tensor(f"proj{l}_psT", [P, 2, 512], F32))
        psP = [ctx.enter_context(nc.psum_tensor(f"proj{l}_psP{i}", [P, 2, 512], F32)) for i in range(2)]
        block = ctx.enter_context(nc.Block())

        @block.sync
        def _(sp):
            sp.dma_start(Ws[:, :, :], A["L0_gnn_Wsrc"][l].rearrange("(k p) n -> p k n", p=P)).then_inc(weights_in, 16)
            sp.dma_start(Wd[:, :, :], A["L0_gnn_Wdst"][l].rearrange("(k p) n -> p k n", p=P)).then_inc(weights_in, 16)
            sp.dma_start(brow[:, 0, :], bcast(A["L0_gnn_bsrc"][l], P)).then_inc(rows_in, 16)
            sp.dma_start(brow[:, 1, :], bcast(A["L0_gnn_bdst"][l], P)).then_inc(rows_in, 16)
            sp.dma_start(arow[:, :], bcast(A["L0_gnn_attn"][l].rearrange("h d -> (h d)"), P)).then_inc(rows_in, 16)
            for t in range(NT):
                sp.wait_ge(out_made, 2 * t + 1)
                sp.dma_start(K.hs_tab[t * P:(t + 1) * P, :], row[:, 0, :, :].rearrange("p a n -> p (a n)"))\
                  .then_inc(table_out, 16)
            sp.wait_ge(table_out, 16 * NT)

        @block.tensor
        def _(pe):
            def turn(t):
                if t >= 1:
                    pe.wait_ge(hT_made, t)
                for k in range(KC):
                    last = pe.transpose(psT[:, k // 3, (k % 3) * P:(k % 3 + 1) * P],
                                        K.h[:, t, k * P:(k + 1) * P], K.ident[:, :])
                last.then_inc(turned, 1)
            turn(0)
            pe.wait_ge(weights_in, 32)
            for t in range(NT):
                pe.wait_ge(hT_made, t + 1)
                for s, W in ((0, Ws), (1, Wd)):
                    if t >= 1:
                        pe.wait_ge(out_made, 2 * (t - 1) + s + 1)
                    for n in range(2):
                        for k in range(KC):
                            last = pe.matmul(psP[s][:, n, 0:HALF], hT[:, t % 2, k, :],
                                             W[:, k, n * HALF:(n + 1) * HALF], start=(k == 0), stop=(k == KC - 1))
                    last.then_inc(proj_made, 1)
                    if s == 0 and t + 1 < NT:
                        turn(t + 1)

        @block.scalar
        def _(act):
            for t in range(NT):
                act.wait_ge(turned, t + 1)
                if t >= 2:
                    act.wait_ge(proj_made, 2 * (t - 1))
                for c in range(2):
                    last = act.activation(hT[:, t % 2, 3 * c:3 * c + 3, :].rearrange("p k n -> p (k n)"),
                                          psT[:, c, 0:3 * P], ACT.Copy)
                last.then_inc(hT_made, 1)

        @block.vector
        def _(dve):
            step = Chain(dve, stepped)
            dve.wait_ge(rows_in, 48)
            for t in range(NT):
                for s in range(2):
                    dve.wait_ge(proj_made, 2 * t + s + 1)
                    if s == 0 and t >= 1:
                        dve.wait_ge(table_out, 16 * t)
                    step(dve.tensor_tensor(row[:, s, :, 0:HALF], psP[s][:, :, 0:HALF],
                                           brow[:, s, :].rearrange("p (a n) -> p a n", a=2), ALU.add))
                    step(dve.tensor_tensor(prod[:, :].rearrange("p (a n) -> p a n", a=2), row[:, s, :, 0:HALF],
                                           arow[:, :].rearrange("p (a n) -> p a n", a=2), ALU.mult))
                    step(dve.tensor_reduce(rest[:, 0:H], prod[:, :].rearrange("p (h d) -> p h d", h=H), AX.X, ALU.add))
                    if s == 0:
                        dve.tensor_scalar(row[:, s, :, HALF:HW], rest[:, 0:H].rearrange("p (a h) -> p a h", a=2),
                                          (1 + SLOPE) / 2, None, ALU.mult).then_inc(out_made, 1)
                        continue
                    step(dve.tensor_scalar(row[:, s, :, HALF:HW], rest[:, 0:H].rearrange("p (a h) -> p a h", a=2),
                                           (1 + SLOPE) / 2, None, ALU.mult))
                    full = row[:, 1, :, :].rearrange("p a n -> p (a n)")
                    step(dve.tensor_copy(K.hdp[:, t, 0, :], full))
                    step(dve.tensor_tensor(rest[:, :], full, K.hdp[:, t, 0, :], ALU.subtract))
                    step(dve.tensor_copy(K.hdp[:, t, 1, :], rest[:, :]))
                    step(dve.tensor_tensor(rest[:, :], rest[:, :], K.hdp[:, t, 1, :], ALU.subtract))
                    dve.tensor_copy(K.hdp[:, t, 2, :], rest[:, :]).then_inc(out_made, 1)


def ring_loop(eng, R, first, step):
    turns = (NG - first) // R
    with eng.Fori(0, turns) as i:
        for u in range(R):
            step(R * i + first + u, (first + u) % R, i + (first + u) // R)
    for n in range(first + R * turns, NG):
        step(n, n % R, n // R)


class Gatherer:

    def __init__(self, pool, K, R, ix, hse, gathered, index_set, slot_free):
        self.R = R
        self.pool, self.K, self.ix, self.hse = pool, K, ix, hse
        self.gathered, self.index_set, self.slot_free = gathered, index_set, slot_free

    def index(self, n, k):
        for j in range(2):
            self.pool.tensor_copy(self.ix[k][j][:, :], self.K.srccol[:, bass.ds(2 * n + j, 1)])\
                .then_inc(self.index_set, 1)

    def gather(self, n, k):
        self.pool.wait_ge(self.index_set, 2 * n + 2)
        self.pool.nop(nofuse=True)
        for j in range(2):
            self.pool.indirect_dma_start(self.hse[:, k, j, :], None, self.K.hs_tab,
                                         bass.IndirectOffsetOnAxis(ap=self.ix[k][j][:, :], axis=0))\
                .then_inc(self.gathered[k][j], 16)

    def step(self, n, k):
        self.gather(n, k)
        self.slot_free(n + 1)
        self.index(n + 1, (k + 1) % self.R)


def edge_logits(nc, K, l, A):
    R = RING_LOGITS
    CREDIT = R
    with ExitStack() as ctx:
        def sem(n):
            return ctx.enter_context(stage_semaphore(nc, f"lg{l}_{n}"))

        def sb(n, shape, dt):
            return ctx.enter_context(nc.sbuf_tensor(f"lg{l}_{n}", shape, dt))
        row_in = [sem(f"row_in{k}") for k in range(R)]
        gathered = [[sem(f"gathered{k}{j}") for j in range(2)] for k in range(R)]
        t_made = [sem(f"t_made{j}") for j in range(2)]
        attn_in, attn_made, index_set, onehot_made, summed, abs_made, abs2_made, weighed, reduced, summed_up, logit_made = (
            sem("attn_in"), sem("attn_made"), sem("index_set"), sem("onehot_made"), sem("summed"), sem("abs_made"),
            sem("abs2_made"), sem("weighed"), sem("reduced"), sem("summed_up"), sem("logit_made"))
        dstrow = sb("dstrow", [P, R, GE], I32)
        ix = [[sb(f"ix{k}{j}", [P, 1], I32) for j in range(2)] for k in range(R)]
        hse = sb("hse", [P, R, 2, ROW], F32)
        tt = sb("tt", [P, R, 2, 2, HW], F32)
        part = sb("part", [P, R, 2 * H], F32)
        arow = sb("arow", [P, 2, HALF], F32)
        ohT = sb("ohT", [P, 3, GE], BF16)
        ps = [[ctx.enter_context(nc.psum_tensor(f"lg{l}_ps{k}{j}", [P, 2, 512], F32)) for j in range(2)]
              for k in range(2)]
        block = ctx.enter_context(nc.Block())

        @block.sync
        def _(sp):
            sp.dma_start(arow[:, :, :].rearrange("p a n -> p (a n)"),
                         bcast(A["L0_gnn_attn"][l].rearrange("h d -> (h d)"), P)).then_inc(attn_in, 16)

            def step(n, k, it):
                off = sp.value_load(K.off_i[0:1, bass.ds(n, 1)], min_val=0, max_val=E)
                sp.wait_ge(onehot_made, n - R + 1 + CREDIT)
                sp.nop(nofuse=True)
                sp.dma_start(dstrow[:, k, :], K.srt_dst[0:1, bass.ds(off, GE)].broadcast_to([P, GE]))\
                  .then_inc(row_in[k], 16)
            ring_loop(sp, R, 0, step)

        @block.gpsimd
        def _(pool):
            def slot_free(n):
                pool.wait_ge(summed, n - R + 1 + CREDIT)
                pool.nop(nofuse=True)
                pool.wait_ge(t_made[1], n - R + 1 + CREDIT)
                pool.nop(nofuse=True)

            g = Gatherer(pool, K, R, ix, hse, gathered, index_set, slot_free)

            def logit(n, k):
                for s in (reduced, summed_up):
                    pool.wait_ge(s, n + 1 + CREDIT)
                    pool.nop(nofuse=True)
                pool.tensor_tensor(K.lg[:, bass.ds(n, 1), :].rearrange("p g (a h) -> p (g a) h", a=4),
                                   part[:, k, :].rearrange("p (a h) -> p a h", a=4),
                                   tt[:, k, :, :, HALF:HW].rearrange("p j a n -> p (j a) n"), ALU.add)\
                    .then_inc(logit_made, 1)

            def step(n, k, it):
                g.step(n - 1, (k - 1) % R)
                logit(n - LAG, (k - LAG) % R)
            g.slot_free(0)
            g.index(0, 0)
            for n in range(LAG - 1):
                g.step(n, n)
            ring_loop(pool, R, LAG, step)
            g.gather(NG - 1, (NG - 1) % R)
            for n in range(NG - LAG, NG):
                logit(n, n % R)

        @block.tensor
        def _(pe):
            def step(n, k, it):
                q = k % 2
                b = pe.value_load(K.blk_i[0:1, bass.ds(n, 1)], min_val=0, max_val=NT - 1)
                pe.wait_ge(onehot_made, n + 1 + CREDIT)
                pe.nop(nofuse=True)
                for j in range(2):
                    if j == 0:
                        pe.wait_ge(summed, n - 1 + CREDIT)
                        pe.nop(nofuse=True)
                    else:
                        pe.wait_ge(abs2_made, n - 1 + CREDIT)
                        pe.nop(nofuse=True)
                        pe.wait_ge(gathered[k][1], 16 * it + 16)
                        pe.nop(nofuse=True)
                    for a in range(2):
                        for part_ in range(3):
                            last = pe.matmul(ps[q][j][:, a, 0:HW], ohT[:, k % 3, j * P:(j + 1) * P],
                                             K.hdp[:, bass.ds(b, 1), part_, a * HW:(a + 1) * HW],
                                             start=(part_ == 0), stop=(part_ == 2 and j == 0))
                        if j == 1:
                            last = pe.matmul(ps[q][j][:, a, 0:HW], K.ident[:, :], hse[:, k, j, a * HW:(a + 1) * HW],
                                             start=False, stop=True)
                    last.then_inc(t_made[j], 1)
            ring_loop(pe, R, 0, step)

        @block.scalar
        def _(act):
            def step(n, k, it):
                act.wait_ge(summed, n + 1 + CREDIT)
                act.nop(nofuse=True)
                act.activation(tt[:, k, 0, :, 0:HALF], tt[:, k, 0, :, 0:HALF], ACT.Abs).then_inc(abs_made, 1)
                act.wait_ge(t_made[1], n + 1 + CREDIT)
                act.nop(nofuse=True)
                act.wait_ge(logit_made, n - R + 1 + CREDIT)
                act.nop(nofuse=True)
                act.activation(tt[:, k, 1, :, HALF:HW], ps[k % 2][1][:, :, HALF:HW], ACT.Copy)
                act.activation(tt[:, k, 1, :, 0:HALF], ps[k % 2][1][:, :, 0:HALF], ACT.Abs).then_inc(abs2_made, 1)

            def sum_up(n, k):
                act.wait_ge(weighed, n + 1 + CREDIT)
                act.nop(nofuse=True)
                for h in range(HH):
                    half = tt[:, k, 1, 0, h * HD:(h + 1) * HD]
                    last = act.activation(half, half, ACT.Copy, accum_out=part[:, k, H + h:H + h + 1])
                last.then_inc(summed_up, 1)

            def both(n, k, it):
                step(n, k, it)
                sum_up(n - 1, (k - 1) % R)
            step(0, 0, 0)
            ring_loop(act, R, 1, both)
            sum_up(NG - 1, (NG - 1) % R)

        @block.vector
        def _(dve):
            for s in (onehot_made, summed, t_made[0], t_made[1], abs2_made, weighed, reduced, summed_up, logit_made):
                dve.sem_inc(s, CREDIT)
            dve.wait_ge(attn_in, 16)
            dve.tensor_scalar(arow[:, :, :], arow[:, :, :], (1 - SLOPE) / 2, None, ALU.mult).then_inc(attn_made, 1)
            dve.wait_ge(attn_made, 1)

            def onehot(n, k, it):
                dve.wait_ge(row_in[k], 16 * it + 16)
                dve.nop(nofuse=True)
                dve.wait_ge(t_made[1], n - 2 + CREDIT)
                dve.nop(nofuse=True)
                dve.tensor_scalar(ohT[:, k % 3, :], dstrow[:, k, :], K.blkiota[:, bass.ds(n, 1)], None, ALU.is_equal)\
                   .then_inc(onehot_made, 1)

            def add(n, k, it):
                dve.wait_ge(gathered[k][0], 16 * it + 16)
                dve.nop(nofuse=True)
                dve.wait_ge(t_made[0], n + 1 + CREDIT)
                dve.nop(nofuse=True)
                dve.wait_ge(logit_made, n - R + 1 + CREDIT)
                dve.nop(nofuse=True)
                dve.tensor_tensor(tt[:, k, 0, :, :], ps[k % 2][0][:, :, 0:HW],
                                  hse[:, k, 0, :].rearrange("p (a n) -> p a n", a=2), ALU.add).then_inc(summed, 1)

            def weigh(n, k):
                dve.wait_ge(abs_made, n + 1)
                dve.nop(nofuse=True)
                dve.wait_ge(abs2_made, n + 1 + CREDIT)
                dve.nop(nofuse=True)
                t4 = tt[:, k, :, :, :].rearrange("p j a n -> p (j a) n")
                dve.tensor_tensor(t4[:, 2, 0:HALF], t4[:, 2, 0:HALF], arow[:, 0, :], ALU.mult).then_inc(weighed, 1)
                for x in (*range(H), *range(H + HH, 2 * H)):
                    cols = slice(x % HH * HD, (x % HH + 1) * HD)
                    last = dve.tensor_tensor_reduce(out=t4[:, x // HH, cols], in0=t4[:, x // HH, cols],
                                                    in1=arow[:, x // HH % 2, cols], scale=1.0, scalar=0.0,
                                                    op0=ALU.mult, op1=ALU.add, accum_out=part[:, k, x:x + 1])
                last.then_inc(reduced, 1)

            def step(n, k, it):
                onehot(n, k, it)
                add(n - 1, (k - 1) % R, it - (1 if k == 0 else 0))
                weigh(n - 2, (k - 2) % R)
            onehot(0, 0, 0)
            onehot(1, 1, 0)
            add(0, 0, 0)
            ring_loop(dve, R, 2, step)
            add(NG - 1, (NG - 1) % R, (NG - 1) // R)
            weigh(NG - 2, (NG - 2) % R)
            weigh(NG - 1, (NG - 1) % R)


def segment_softmax(nc, K, l):
    with ExitStack() as ctx:
        def sem(n):
            return ctx.enter_context(stage_semaphore(nc, f"sm{l}_{n}"))

        def sb(n, shape, dt):
            return ctx.enter_context(nc.sbuf_tensor(f"sm{l}_{n}", shape, dt))
        stepped, pads_set, turned, made, ends_out, rows_in, carry_out, carry_in, back = (
            sem("stepped"), sem("pads_set"), sem("turned"), sem("made"), sem("ends_out"), sem("rows_in"),
            sem("carry_out"), sem("carry_in"), sem("back"))
        lgT = sb("lgT", [P, NC, P], F32)
        fw = sb("fw", [P, NC, P], F32)
        bw = sb("bw", [P, NC, P], F32)
        ends = sb("ends", [P, 2, NC], F32)
        rows = sb("rows", [H, 2, NC * TPC], F32)
        run = sb("run", [H, 2, NC * TPC], F32)
        carry = sb("carry", [H, 2, NC * TPC], F32)
        carryT = sb("carryT", [P, 2, NC], F32)
        ps = [ctx.enter_context(nc.psum_tensor(f"sm{l}_ps{i}", [P, 512], F32)) for i in range(3)]
        block = ctx.enter_context(nc.Block())
        lg3 = K.lg[:, :, :].rearrange("p g x -> p (g x)")

        @block.tensor
        def _(pe):
            pe.wait_ge(pads_set, 1)
            for c in range(NC):
                last = pe.transpose(ps[c // 4][:, (c % 4) * P:(c % 4 + 1) * P], lg3[:, c * P:(c + 1) * P],
                                    K.ident[:, :])
            last.then_inc(turned, 1)
            pe.wait_ge(made, 3)
            for c in range(NC):
                last = pe.transpose(ps[c // 4][:, (c % 4) * P:(c % 4 + 1) * P], lgT[:, c, :], K.ident[:, :])
            last.then_inc(turned, 1)

        @block.sync
        def _(sp):
            sp.wait_ge(made, 1)
            sp.dma_start(K.bounce[2], ends[:, :, :].rearrange("p a c -> p (a c)")).then_inc(ends_out, 16)
            sp.wait_ge(ends_out, 16)
            for a in range(2):
                for c in range(NC):
                    sp.dma_start(rows[:, a, c * TPC:(c + 1) * TPC],
                                 K.bounce[2].rearrange("(t h) n -> h t n", h=H)[:, :, a * NC + c],
                             allow_slow_non_contiguous=True).then_inc(rows_in, 16)
            sp.wait_ge(made, 2)
            sp.dma_start(K.bounce[3].rearrange("(h a) n -> h (a n)", h=H)[:, 0:2 * NTP],
                         carry[:, :, :].rearrange("h a n -> h (a n)")).then_inc(carry_out, 16)
            sp.wait_ge(carry_out, 16)
            cv = K.bounce[3].rearrange("(h a) n -> h (a n)", h=H)[:, 0:2 * NTP]\
                  .rearrange("h (a c t) -> t h a c", a=2, t=TPC)
            for t in range(TPC):
                sp.dma_start(carryT[t * H:(t + 1) * H, :, :], cv[t], allow_slow_non_contiguous=True)\
                  .then_inc(carry_in, 16)

        @block.vector
        def _(dve):
            step = Chain(dve, stepped)
            dve.memset(lg3[:, NTILE * H:NTP * H], 0.0).then_inc(pads_set, 1)
            dve.wait_ge(turned, 1)
            for i in range(3):
                last = dve.tensor_copy(lgT[:, 4 * i:4 * i + 4, :].rearrange("p c l -> p (c l)"), ps[i][:, :])
            step(last)

            def flat(x):
                return x[:, :, :].rearrange("p c l -> p (c l)")
            step(dve.tensor_tensor_scan(flat(fw), flat(K.pen_start), flat(lgT), -BIG, ALU.add, ALU.max))
            step(dve.tensor_tensor_scan(flat(bw)[:, ::-1], flat(K.pen_end)[:, ::-1], flat(lgT)[:, ::-1], -BIG,
                                        ALU.add, ALU.max))
            step(dve.tensor_copy(ends[:, 0, :], fw[:, :, P - 1]))
            dve.tensor_copy(ends[:, 1, :], bw[:, :, 0]).then_inc(made, 1)
            step(dve.tensor_tensor(flat(fw), flat(fw), flat(bw), ALU.max))
            dve.wait_ge(rows_in, 16 * 2 * NC)
            step(dve.memset(carry[:, :, :], -BIG))
            step(dve.tensor_tensor_scan(run[:, 0, :], K.pen_carry[:, 0, :], rows[:, 0, :], -BIG, ALU.add, ALU.max))
            step(dve.tensor_tensor_scan(run[:, 1, ::-1], K.pen_carry[:, 1, ::-1], rows[:, 1, ::-1], -BIG,
                                        ALU.add, ALU.max))
            step(dve.tensor_copy(carry[:, 0, 1:NTP], run[:, 0, 0:NTP - 1]))
            dve.tensor_copy(carry[:, 1, 0:NTP - 1], run[:, 1, 1:NTP]).then_inc(made, 1)
            dve.wait_ge(carry_in, 16 * TPC)
            for a, pen in ((0, K.pen_first), (1, K.pen_last)):
                cb = carryT[:, a, :].rearrange("p (c l) -> p c l", l=1).broadcast_to([P, NC, P])
                step(dve.tensor_tensor(bw[:, :, :], pen[:, :, :], cb, ALU.add))
                step(dve.tensor_tensor(fw[:, :, :], fw[:, :, :], bw[:, :, :], ALU.max))
            dve.tensor_tensor(bw[:, :, :], lgT[:, :, :], fw[:, :, :], ALU.subtract).then_inc(back, 1)
            dve.wait_ge(turned, 2)
            for i in range(3):
                last = dve.tensor_copy(lg3[:, i * 512:(i + 1) * 512], ps[i][:, :])
            step(last)

        @block.scalar
        def _(act):
            act.wait_ge(back, 1)
            act.activation(lgT[:, :, :].rearrange("p c l -> p (c l)"), bw[:, :, :].rearrange("p c l -> p (c l)"),
                           ACT.Exp).then_inc(made, 1)


def aggregate(nc, K, l):
    R = RING_SUMS
    CREDIT = R
    with ExitStack() as ctx:
        def sem(n):
            return ctx.enter_context(stage_semaphore(nc, f"ag{l}_{n}"))

        def sb(n, shape, dt):
            return ctx.enter_context(nc.sbuf_tensor(f"ag{l}_{n}", shape, dt))
        gathered = [[sem(f"gathered{k}{j}") for j in range(2)] for k in range(R)]
        message_made = [sem(f"message_made{j}") for j in range(2)]
        index_set, summed, added, zeroed = sem("index_set"), sem("summed"), sem("added"), sem("zeroed")
        ix = [[sb(f"ix{k}{j}", [P, 1], I32) for j in range(2)] for k in range(R)]
        hse = sb("hse", [P, R, 2, ROW], F32)
        msg = sb("msg", [P, R, 2, ROW], F32)
        oh = sb("oh", [P, R, 2, P], F32)
        ps = [ctx.enter_context(nc.psum_tensor(f"ag{l}_ps{k}", [P, 2, 512], F32)) for k in range(R)]
        block = ctx.enter_context(nc.Block())

        @block.gpsimd
        def _(pool):
            def slot_free(n):
                for j in range(2):
                    pool.wait_ge(message_made[j], n - R + 1 + CREDIT)
                    pool.nop(nofuse=True)
            g = Gatherer(pool, K, R, ix, hse, gathered, index_set, slot_free)
            slot_free(0)
            g.index(0, 0)
            ring_loop(pool, R, 1, lambda n, k, it: g.step(n - 1, (k - 1) % R))
            g.gather(NG - 1, (NG - 1) % R)

        @block.tensor
        def _(pe):
            def step(n, k, it):
                pe.wait_ge(message_made[0], n + 1 + CREDIT)
                pe.nop(nofuse=True)
                pe.wait_ge(message_made[1], n + 1 + CREDIT)
                pe.nop(nofuse=True)
                pe.wait_ge(added, n - R + 1 + CREDIT)
                pe.nop(nofuse=True)
                for a in range(2):
                    for j in range(2):
                        last = pe.matmul(ps[k][:, a, 0:HW], oh[:, k, j, :], msg[:, k, j, a * HW:(a + 1) * HW],
                                         start=(j == 0), stop=(j == 1))
                last.then_inc(summed, 1)
            ring_loop(pe, R, 0, step)

        @block.scalar
        def _(act):
            def step(n, k, it):
                act.wait_ge(gathered[k][1], 16 * it + 16)
                act.nop(nofuse=True)
                act.wait_ge(summed, n - R + 1 + CREDIT)
                act.nop(nofuse=True)
                for h in range(H):
                    at = h // HH * HW + h % HH * HD
                    last = act.activation(msg[:, k, 1, at:at + HD], hse[:, k, 1, at:at + HD], ACT.Copy,
                                          scale=K.lg[:, bass.ds(n, 1), H + h:H + h + 1].rearrange("p g x -> p (g x)"))
                last.then_inc(message_made[1], 1)
            ring_loop(act, R, 0, step)

        @block.vector
        def _(dve):
            for s in (message_made[0], message_made[1], added, summed):
                dve.sem_inc(s, CREDIT)
            dve.memset(K.acc[:, :, :], 0.0).then_inc(zeroed, 1)
            dve.wait_ge(zeroed, 1)

            def message(n, k, it):
                dve.wait_ge(summed, n - R + 1 + CREDIT)
                dve.nop(nofuse=True)
                for j in range(2):
                    dve.tensor_scalar(oh[:, k, j, :], K.iota_free[:, :], K.drel[:, bass.ds(2 * n + j, 1)], None,
                                      ALU.is_equal)
                m4 = msg[:, k, :, :].rearrange("p j (a n) -> p (j a) n", a=2)
                dve.tensor_copy(m4[:, :, HALF:HW], K.lg[:, bass.ds(n, 1), :].rearrange("p g (a h) -> p (g a) h", a=4))
                dve.wait_ge(gathered[k][0], 16 * it + 16)
                dve.nop(nofuse=True)
                h4 = hse[:, k, 0, :].rearrange("p (a n) -> p a n", a=2)
                for a in range(2):
                    exh = K.lg[:, bass.ds(n, 1), a * HH:(a + 1) * HH]\
                        .rearrange("p g (h d) -> p (g h) d", d=1).broadcast_to([P, HH, HD])
                    last = dve.tensor_tensor(m4[:, a, 0:HALF].rearrange("p (h d) -> p h d", d=HD),
                                             h4[:, a, 0:HALF].rearrange("p (h d) -> p h d", d=HD), exh, ALU.mult)
                last.then_inc(message_made[0], 1)

            def add(n, k):
                b = dve.value_load(K.blk_i[0:1, bass.ds(n, 1)], min_val=0, max_val=NT - 1)
                dve.wait_ge(added, n + CREDIT)
                dve.nop(nofuse=True)
                dve.wait_ge(summed, n + 1 + CREDIT)
                dve.nop(nofuse=True)
                a = K.acc[:, bass.ds(b, 1), :].rearrange("p b (a n) -> p (b a) n", a=2)
                dve.tensor_tensor(a, a, ps[k][:, :, 0:HW], ALU.add).then_inc(added, 1)

            def step(n, k, it):
                message(n, k, it)
                add(n - 2, (k - 2) % R)
            message(0, 0, 0)
            message(1, 1, 0)
            ring_loop(dve, R, 2, step)
            add(NG - 2, (NG - 2) % R)
            add(NG - 1, (NG - 1) % R)


def node_update(nc, K, l, A):
    with ExitStack() as ctx:
        def sem(n):
            return ctx.enter_context(stage_semaphore(nc, f"up{l}_{n}"))

        def sb(n, shape, dt):
            return ctx.enter_context(nc.sbuf_tensor(f"up{l}_{n}", shape, dt))
        stepped, low_made, exp_made, rows_in = sem("stepped"), sem("low_made"), sem("exp_made"), sem("rows_in")
        rs = sb("rs", [P, NT, H], F32)
        o = sb("o", [P, 2, DM], F32)
        m = sb("m", [P, 2, DM], F32)
        block = ctx.enter_context(nc.Block())

        @block.sync
        def _(sp):
            sp.dma_start(K.lnw[:, :], bcast(A["L0_gnn_ln_w"][l], P)).then_inc(rows_in, 16)
            sp.dma_start(K.lnb[:, :], bcast(A["L0_gnn_ln_b"][l], P)).then_inc(rows_in, 16)
            if l == L - 1:
                sp.dma_start(K.onw[:, :], bcast(A["L0_gnn_on_w"], P)).then_inc(rows_in, 16)
                sp.dma_start(K.onb[:, :], bcast(A["L0_gnn_on_b"], P)).then_inc(rows_in, 16)
            sp.wait_ge(rows_in, 64 if l == L - 1 else 32)

        @block.vector
        def _(dve):
            step = Chain(dve, stepped)
            acc4 = K.acc[:, :, :].rearrange("p t (a n) -> p t a n", a=2)
            for a in range(2):
                step(dve.tensor_scalar(rs[:, :, a * HH:(a + 1) * HH], acc4[:, :, a, HALF:HW], 1e-30, None, ALU.max))
            step(dve.reciprocal(rs[:, :, :], rs[:, :, :]))

            def first(t):
                for a in range(2):
                    r = rs[:, t, a * HH:(a + 1) * HH].rearrange("p (h d) -> p h d", d=1).broadcast_to([P, HH, HD])
                    last = dve.tensor_tensor(o[:, t % 2, a * HALF:(a + 1) * HALF].rearrange("p (h d) -> p h d", d=HD),
                                             acc4[:, t, a, 0:HALF].rearrange("p (h d) -> p h d", d=HD), r, ALU.mult)
                step(last)
                dve.tensor_scalar(m[:, t % 2, :], o[:, t % 2, :], 0.0, None, ALU.min).then_inc(low_made, 1)

            def second(t):
                dve.wait_ge(exp_made, t + 1)
                step(dve.scalar_tensor_tensor(out=o[:, t % 2, :], in0=o[:, t % 2, :], scalar=0.0, in1=m[:, t % 2, :],
                                              op0=ALU.max, op1=ALU.add))
                step(dve.scalar_tensor_tensor(out=K.h[:, t, :], in0=o[:, t % 2, :], scalar=-1.0, in1=K.h[:, t, :],
                                              op0=ALU.add, op1=ALU.add))
            first(0)
            for t in range(NT):
                if t + 1 < NT:
                    first(t + 1)
                second(t)

        @block.scalar
        def _(act):
            for t in range(NT):
                act.wait_ge(low_made, t + 1)
                act.activation(m[:, t % 2, :], m[:, t % 2, :], ACT.Exp).then_inc(exp_made, 1)


class Keep:
    pass


def gnn(nc, K, A):
    with ExitStack() as ctx:
        def sb(n, shape, dt):
            return ctx.enter_context(nc.sbuf_tensor(n, shape, dt))
        K.hdp = sb("hd_parts", [P, NT, 3, ROW], BF16)
        K.lg = sb("logits", [P, NTP // 2, 2 * H], F32)
        K.srccol = sb("src_columns", [P, NTILE], I32)
        K.dcolf = sb("dst_columns", [P, NTP], F32)
        K.drel = sb("dst_in_block", [P, NTILE], F32)
        K.off_i = sb("group_offset", [P, NG], I32)
        K.blk_i = sb("group_block", [P, NG], I32)
        K.blkiota = sb("block_members", [P, NG], F32)
        K.pen_start = sb("pen_start", [P, NC, P], F32)
        K.pen_end = sb("pen_end", [P, NC, P], F32)
        K.pen_first = sb("pen_first", [P, NC, P], F32)
        K.pen_last = sb("pen_last", [P, NC, P], F32)
        K.pen_carry = sb("pen_carry", [H, 2, NTP], F32)
        with ExitStack() as c2:
            K.dall = c2.enter_context(nc.sbuf_tensor("dst_all", [EL, EC], I32))
            K.sall = c2.enter_context(nc.sbuf_tensor("src_all", [EL, EC], I32))
            K.dallf = c2.enter_context(nc.sbuf_tensor("dst_all_f", [EL, EC], F32))
            order_edges(nc, K, A["src"], A["dst"])
            edge_tables(nc, K)
        segment_tables(nc, K)
        for l in range(L):
            if l > 0:
                recycle(nc)
            project(nc, K, l, A)
            edge_logits(nc, K, l, A)
            segment_softmax(nc, K, l)
            with ExitStack() as c2:
                K.acc = c2.enter_context(nc.sbuf_tensor(f"acc{l}", [P, NT, ROW], F32))
                aggregate(nc, K, l)
                node_update(nc, K, l, A)
            if l < L - 1:
                norm_block(nc, K, f"ln{l}", K.h, K.h, K.lnw, K.lnb)


NE = 16
NGRP = 8
PER = NE // NGRP
TOPG = 4
TOPE = 4
SCALE = 2.5
HID = 512
KH = HID // P
TM = (N * TOPE + NE * (P - 1)) // P
TM -= 0 if TM % 2 == 0 else -1
BW = 2 * HID + DM
LOADS = 4 * 16
SLOTS = 3
SURE = (N * TOPE + P - 1) // P // 2


def bias_parts(nc, K, A):
    with ExitStack() as ctx:
        def sem(n):
            return ctx.enter_context(stage_semaphore(nc, f"bias_{n}"))

        def sb(n, shape, dt):
            return ctx.enter_context(nc.sbuf_tensor(f"bias_{n}", shape, dt))
        rows_in, stepped, parts_made, parts_out = sem("rows_in"), sem("stepped"), sem("parts_made"), sem("parts_out")
        full = sb("full", [NE + 1, BW], F32)
        parts = sb("parts", [NE + 1, 3, BW], BF16)
        block = ctx.enter_context(nc.Block())

        @block.sync
        def _(sp):
            for name, at, w in (("bu", 0, HID), ("bg", HID, HID), ("bd", 2 * HID, DM)):
                sp.dma_start(full[0:NE, at:at + w], A["L0_ffn_" + name]).then_inc(rows_in, 16)
                sp.dma_start(full[NE:NE + 1, at:at + w], A["L0_ffn_s" + name].rearrange("(a n) -> a n", a=1))\
                  .then_inc(rows_in, 16)
            sp.wait_ge(parts_made, 1)
            sp.dma_start(K.bias_tab, parts[:, :, :]).then_inc(parts_out, 16)
            sp.wait_ge(parts_out, 16)

        @block.vector
        def _(dve):
            step = Chain(dve, stepped)
            dve.wait_ge(rows_in, 96)
            step(dve.tensor_copy(parts[:, 0, :], full[:, :]))
            step(dve.tensor_tensor(full[:, :], full[:, :], parts[:, 0, :], ALU.subtract))
            step(dve.tensor_copy(parts[:, 1, :], full[:, :]))
            step(dve.tensor_tensor(full[:, :], full[:, :], parts[:, 1, :], ALU.subtract))
            dve.tensor_copy(parts[:, 2, :], full[:, :]).then_inc(parts_made, 1)


def route(nc, K, A):
    with ExitStack() as ctx:
        def sem(n):
            return ctx.enter_context(stage_semaphore(nc, f"route_{n}"))

        def sb(n, shape, dt):
            return ctx.enter_context(nc.sbuf_tensor(f"route_{n}", shape, dt))
        weights_in, rows_out, turned, xT_made, logits_made, exp_ready, exp_made = (
            sem("weights_in"), sem("rows_out"), sem("turned"), sem("xT_made"), sem("logits_made"), sem("exp_ready"),
            sem("exp_made"))
        stepped, iotas, chosen, counted, zeroed = sem("stepped"), sem("iotas"), sem("chosen"), sem("counted"), sem("zeroed")
        gw = sb("gw", [P, KC, NE], F32)
        rows = sb("rows", [P, 2, NE], F32)
        xT = sb("xT", [P, 2, KC, P], F32)
        lo = sb("lo", [P, NT, NE], F32)
        sc = sb("sc", [P, NT, NE], F32)
        s = sb("s", [P, NT, NE], F32)
        mx = sb("mx", [P, NT], F32)
        g = sb("g", [P, NT, NGRP], F32)
        cmp_ = sb("cmp", [P, NT, NE, NE], F32)
        eq = sb("eq", [P, NT, NE, NE], F32)
        rank = sb("rank", [P, NT, NE], F32)
        tri = sb("tri", [P, NE, NE], F32)
        tri8 = sb("tri8", [P, NGRP, NGRP], F32)
        upper = sb("upper", [P, P], F32)
        tok = sb("tok", [P, NT], F32)
        valid = sb("valid", [P, NT], F32)
        sel = sb("sel", [P, NT, NE], F32)
        c1 = sb("c1", [P, NT, NE], F32)
        c2 = sb("c2", [P, NT, NE], F32)
        pos = sb("pos", [P, NT, NE], F32)
        tot = sb("tot", [P, NT, NE], F32)
        run = sb("run", [P, NE], F32)
        nt = sb("nt", [P, NE], F32)
        nti = sb("nti", [P, NE], I32)
        zer = sb("zer", [P, NE], F32)
        cum = sb("cum", [P, NE], F32)
        base = sb("base", [P, NE], F32)
        it = sb("it", [P, TM], F32)
        te = sb("te", [P, TM], F32)
        pk = sb("pk", [P, TOPE, NT], F32)
        lane = sb("lane", [P, TOPE, NT], I32)
        none = sb("none", [P, TM], I32)
        zrow = sb("zrow", [P, 1, DM], F32)
        new, zt, runs, before, before2, used = (
            sb(x, [P, TM], F32) for x in ("new", "zt", "runs", "before", "before2", "used"))
        lastp = sb("lastp", [P, 1], F32)
        lastp_i = sb("lastp_i", [P, 1], I32)
        psT = ctx.enter_context(nc.psum_tensor("route_psT", [P, 2, 512], F32))
        psL = ctx.enter_context(nc.psum_tensor("route_psL", [P, NT * NE], F32))
        psC = [ctx.enter_context(nc.psum_tensor(f"route_psC{i}", [P, NT * NE], F32)) for i in range(2)]
        block = ctx.enter_context(nc.Block())

        @block.sync
        def _(sp):
            sp.dma_start(gw[:, :, :], A["L0_ffn_gate_w"].rearrange("(k p) n -> p k n", p=P)).then_inc(weights_in, 16)
            sp.dma_start(rows[:, 0, :], bcast(A["L0_ffn_gate_b"], P)).then_inc(weights_in, 16)
            sp.dma_start(rows[:, 1, :], bcast(A["L0_ffn_bias"], P)).then_inc(weights_in, 16)
            sp.dma_start(K.xn_tab.rearrange("(t p) d -> p t d", p=P), K.xn[:, :, :]).then_inc(rows_out, 16)
            sp.wait_ge(zeroed, 2)
            sp.dma_start(K.pair_tab.rearrange("(p k) a -> p (k a)", p=P), none[:, :]).then_inc(rows_out, 16)
            sp.dma_start(K.pair_y[2 * SURE * P:, :].rearrange("(t p) d -> p t d", p=P),
                         zrow[:, :, :].broadcast_to([P, TM - 2 * SURE, DM])).then_inc(rows_out, 16)
            sp.wait_ge(rows_out, 48)

        @block.gpsimd
        def _(pool):
            pool.memset(none[:, :], 0).then_inc(zeroed, 1)
            pool.memset(zrow[:, :, :], 0.0).then_inc(zeroed, 1)
            pool.memset(upper[:, :], 1.0).then_inc(iotas, 1)
            pool.memset(tri[:, :, :], 1.0).then_inc(iotas, 1)
            pool.memset(tri8[:, :, :], 1.0).then_inc(iotas, 1)
            pool.wait_ge(iotas, 3)
            pool.affine_select(out=upper[:, :], in_=upper[:, :], compare_op=ALU.is_gt, fill=0.0, base=0,
                               pattern=[[1, P]], channel_multiplier=-1).then_inc(iotas, 1)
            pool.affine_select(out=tri[:, :, :], in_=tri[:, :, :], compare_op=ALU.is_gt, fill=0.0, base=0,
                               pattern=[[1, NE], [-1, NE]], channel_multiplier=0).then_inc(iotas, 1)
            pool.affine_select(out=tri8[:, :, :], in_=tri8[:, :, :], compare_op=ALU.is_gt, fill=0.0, base=0,
                               pattern=[[1, NGRP], [-1, NGRP]], channel_multiplier=0).then_inc(iotas, 1)
            pool.iota(tok[:, :], [[P, NT]], base=0, channel_multiplier=1,
                      allow_small_or_imprecise_dtypes=True).then_inc(iotas, 1)
            pool.iota(it[:, :], [[1, TM]], base=0, channel_multiplier=0,
                      allow_small_or_imprecise_dtypes=True).then_inc(iotas, 1)

        @block.tensor
        def _(pe):
            pe.wait_ge(weights_in, 48)
            for t in range(NT):
                if t >= 1:
                    pe.wait_ge(xT_made, t)
                for k in range(KC):
                    last = pe.transpose(psT[:, k // 3, (k % 3) * P:(k % 3 + 1) * P], K.xn[:, t, k * P:(k + 1) * P],
                                        K.ident[:, :])
                last.then_inc(turned, 1)
                pe.wait_ge(xT_made, t + 1)
                for k in range(KC):
                    last = pe.matmul(psL[:, t * NE:(t + 1) * NE], xT[:, t % 2, k, :], gw[:, k, :], start=(k == 0),
                                     stop=(k == KC - 1))
                last.then_inc(logits_made, 1)
            pe.wait_ge(chosen, 1)
            selv = sel[:, :, :].rearrange("p t e -> p (t e)")
            pe.matmul(psC[0][:, :], upper[:, :], selv, start=True, stop=True)
            pe.matmul(psC[1][:, :], K.ones[:, :], selv, start=True, stop=True).then_inc(counted, 1)

        @block.scalar
        def _(act):
            for t in range(NT):
                act.wait_ge(turned, t + 1)
                if t >= 2:
                    act.wait_ge(logits_made, t - 1)
                for c in range(2):
                    last = act.activation(xT[:, t % 2, 3 * c:3 * c + 3, :].rearrange("p k n -> p (k n)"),
                                          psT[:, c, 0:3 * P], ACT.Copy)
                last.then_inc(xT_made, 1)
            act.wait_ge(exp_ready, 1)
            act.activation(sc[:, :, :], lo[:, :, :], ACT.Exp).then_inc(exp_made, 1)

        @block.vector
        def _(dve):
            step = Chain(dve, stepped)

            def over(x, n):
                return x.rearrange("p (t e) -> p t e", e=1).broadcast_to([P, NT, n])

            dve.wait_ge(logits_made, NT)
            gb = rows[:, 0:1, :].broadcast_to([P, NT, NE])
            step(dve.tensor_tensor(lo[:, :, :], psL[:, :].rearrange("p (t e) -> p t e", e=NE), gb, ALU.add))
            step(dve.tensor_reduce(mx[:, :], lo[:, :, :], AX.X, ALU.max))
            dve.tensor_tensor(lo[:, :, :], lo[:, :, :], over(mx[:, :], NE), ALU.subtract).then_inc(exp_ready, 1)
            dve.wait_ge(exp_made, 1)
            step(dve.tensor_reduce(mx[:, :], sc[:, :, :], AX.X, ALU.add))
            step(dve.reciprocal(mx[:, :], mx[:, :]))
            step(dve.tensor_tensor(sc[:, :, :], sc[:, :, :], over(mx[:, :], NE), ALU.mult))
            step(dve.tensor_tensor(s[:, :, :], sc[:, :, :], rows[:, 1:2, :].broadcast_to([P, NT, NE]), ALU.add))
            s4 = s[:, :, :].rearrange("p t (g a) -> p t g a", a=PER)
            step(dve.tensor_tensor(g[:, :, :], s4[:, :, :, 0], s4[:, :, :, 1], ALU.add))
            dve.wait_ge(iotas, 8)

            def top(x, n, k, low, out):
                for t in range(NT):
                    xj = x[:, t:t + 1, :].broadcast_to([P, n, n])
                    xi = x[:, t, :].rearrange("p (i j) -> p i j", j=1).broadcast_to([P, n, n])
                    dve.tensor_tensor(cmp_[:, t, 0:n, 0:n], xj, xi, ALU.is_gt)
                    last = dve.tensor_tensor(eq[:, t, 0:n, 0:n], xj, xi, ALU.is_equal)
                step(last)
                for t in range(NT):
                    last = dve.tensor_tensor(eq[:, t, 0:n, 0:n], eq[:, t, 0:n, 0:n], low[:, :, :], ALU.mult)
                step(last)
                for t in range(NT):
                    last = dve.tensor_tensor(cmp_[:, t, 0:n, 0:n], cmp_[:, t, 0:n, 0:n], eq[:, t, 0:n, 0:n], ALU.add)
                step(last)
                for t in range(NT):
                    last = dve.tensor_reduce(rank[:, t, 0:n], cmp_[:, t, 0:n, 0:n], AX.X, ALU.add)
                step(last)
                step(dve.tensor_scalar(out, rank[:, :, 0:n], float(k), None, ALU.is_lt))

            top(g, NGRP, TOPG, tri8, c1[:, :, 0:NGRP])
            for a in range(PER):
                step(dve.tensor_scalar(c2[:, :, 0:NGRP], c1[:, :, 0:NGRP], 1.0, BIG, ALU.subtract, ALU.mult))
                step(dve.tensor_tensor(s4[:, :, :, a], s4[:, :, :, a], c1[:, :, 0:NGRP], ALU.mult))
                step(dve.tensor_tensor(s4[:, :, :, a], s4[:, :, :, a], c2[:, :, 0:NGRP], ALU.add))
            top(s, NE, TOPE, tri, sel[:, :, :])
            step(dve.tensor_scalar(valid[:, :], tok[:, :], float(N), None, ALU.is_lt))
            dve.tensor_tensor(sel[:, :, :], sel[:, :, :], over(valid[:, :], NE), ALU.mult).then_inc(chosen, 1)
            dve.wait_ge(chosen, 1)
            src_, n = sel, 1
            for dst_ in (c1, c2, c1, c2):
                dve.tensor_copy(dst_[:, :, 0:n], src_[:, :, 0:n])
                step(dve.tensor_tensor(dst_[:, :, n:NE], src_[:, :, n:NE], src_[:, :, 0:NE - n], ALU.add))
                src_, n = dst_, 2 * n
            dve.wait_ge(counted, 1)
            step(dve.tensor_copy(pos[:, :, :], psC[0][:, :].rearrange("p (t e) -> p t e", e=NE)))
            step(dve.tensor_copy(tot[:, :, :], psC[1][:, :].rearrange("p (t e) -> p t e", e=NE)))
            step(dve.memset(run[:, :], 0.0))
            for t in range(NT):
                step(dve.tensor_tensor(pos[:, t, :], pos[:, t, :], run[:, :], ALU.add))
                step(dve.tensor_tensor(run[:, :], run[:, :], tot[:, t, :], ALU.add))
            step(dve.tensor_scalar(nti[:, :], run[:, :], float(P - 1), None, ALU.add))
            step(dve.tensor_scalar(nti[:, :], nti[:, :], P.bit_length() - 1, None, ALU.arith_shift_right))
            step(dve.tensor_copy(nt[:, :], nti[:, :]))
            step(dve.memset(zer[:, :], 0.0))
            step(dve.tensor_tensor_scan(cum[:, :], nt[:, :], zer[:, :], 0.0, ALU.add, ALU.add))
            step(dve.tensor_tensor(base[:, :], cum[:, :], nt[:, :], ALU.subtract))
            step(dve.tensor_scalar(base[:, :], base[:, :], float(P), None, ALU.mult))
            step(dve.tensor_tensor(pos[:, :, :], pos[:, :, :],
                                   base[:, :].rearrange("p (a e) -> p a e", a=1).broadcast_to([P, NT, NE]), ALU.add))
            step(dve.memset(te[:, :], 0.0))
            for e in range(NE):
                step(dve.scalar_tensor_tensor(out=te[:, :], in0=it[:, :], scalar=cum[:, e:e + 1], in1=te[:, :],
                                              op0=ALU.is_ge, op1=ALU.add))
            step(dve.tensor_scalar(te[:, :], te[:, :], float(NE - 1), None, ALU.min))
            step(dve.tensor_copy(K.tile_expert[:, :], te[:, :]))
            step(dve.memset(new[:, 0:1], 1.0))
            step(dve.tensor_tensor(new[:, 1:TM], te[:, 1:TM], te[:, 0:TM - 1], ALU.not_equal))
            step(dve.memset(zt[:, :], 0.0))
            step(dve.tensor_tensor_scan(runs[:, :], new[:, :], zt[:, :], 0.0, ALU.add, ALU.add))
            step(dve.tensor_tensor(te[:, :], new[:, :], it[:, :], ALU.mult))
            step(dve.tensor_tensor_scan(te[:, :], zt[:, :], te[:, :], 0.0, ALU.add, ALU.max))
            step(dve.memset(before[:, :], 0.0))
            step(dve.tensor_copy(before[:, 1:TM], te[:, 0:TM - 1]))
            step(dve.tensor_tensor(before2[:, :], new[:, :], before[:, :], ALU.mult))
            step(dve.tensor_tensor_scan(before2[:, :], zt[:, :], before2[:, :], 0.0, ALU.add, ALU.max))
            step(dve.memset(before[:, :], 0.0))
            step(dve.tensor_copy(before[:, 1:TM], before2[:, 0:TM - 1]))
            step(dve.tensor_scalar(lastp[:, :], cum[:, NE - 1:NE], 1.0, None, ALU.add))
            step(dve.tensor_copy(lastp_i[:, :], lastp[:, :]))
            step(dve.tensor_scalar(lastp_i[:, :], lastp_i[:, :], 1, None, ALU.arith_shift_right))
            step(dve.tensor_copy(lastp[:, :], lastp_i[:, :]))
            step(dve.tensor_scalar(lastp[:, :], lastp[:, :], 2.0, None, ALU.mult))
            step(dve.tensor_scalar(used[:, :], it[:, :], lastp[:, :], None, ALU.is_lt))
            step(dve.tensor_copy(K.tile_used[:, :], used[:, :]))
            step(dve.tensor_scalar(lastp[:, :], lastp[:, :], 0.5, -1.0, ALU.mult, ALU.add))
            step(dve.tensor_copy(K.last_pair[:, :], lastp[:, :]))
            step(dve.tensor_tensor(new[:, :], new[:, :], used[:, :], ALU.mult))
            step(dve.tensor_copy(K.run_new[:, :], new[:, :]))
            step(dve.tensor_scalar(te[:, :], runs[:, :], float(LOADS), None, ALU.mult))
            step(dve.tensor_copy(K.run_loads[:, :], te[:, :]))
            step(dve.memset(te[:, :], 0.0))
            for r in range(SLOTS, NE + 1, SLOTS):
                step(dve.scalar_tensor_tensor(out=te[:, :], in0=runs[:, :], scalar=float(r), in1=te[:, :],
                                              op0=ALU.is_ge, op1=ALU.add))
            step(dve.scalar_tensor_tensor(out=te[:, :], in0=te[:, :], scalar=-float(SLOTS), in1=runs[:, :],
                                          op0=ALU.mult, op1=ALU.add))
            step(dve.tensor_copy(K.run_slot[:, :], te[:, :]))
            step(dve.tensor_copy(K.run_before[:, :], before[:, :]))
            for q in range(TOPE):
                step(dve.tensor_scalar(c1[:, :, :], c2[:, :, :], float(q + 1), None, ALU.is_equal))
                step(dve.tensor_tensor(c1[:, :, :], c1[:, :, :], sel[:, :, :], ALU.mult))
                step(dve.tensor_tensor(s[:, :, :], c1[:, :, :], pos[:, :, :], ALU.mult))
                step(dve.tensor_reduce(pk[:, q, :], s[:, :, :], AX.X, ALU.add))
                step(dve.tensor_tensor(s[:, :, :], c1[:, :, :], sc[:, :, :], ALU.mult))
                step(dve.tensor_reduce(K.pair_w[:, q, :], s[:, :, :], AX.X, ALU.add))
            step(dve.tensor_scalar(K.pair_w[:, :, :], K.pair_w[:, :, :], SCALE, None, ALU.mult))
            step(dve.tensor_copy(K.pair_row[:, :, :], pk[:, :, :]))
            step(dve.tensor_scalar(lane[:, :, :], K.pair_row[:, :, :], P - 1, None, ALU.bitwise_and))
            step(dve.tensor_scalar(K.pair_at[:, :, :], K.pair_row[:, :, :], P.bit_length() - 1, None,
                                   ALU.arith_shift_right))
            step(dve.scalar_tensor_tensor(out=K.pair_at[:, :, :], in0=lane[:, :, :], scalar=float(TM),
                                          in1=K.pair_at[:, :, :], op0=ALU.mult, op1=ALU.add))
            step(dve.tensor_copy(K.token_id[:, :], tok[:, :]))


def load_expert(sp, K, A, n):
    e = sp.value_load(K.tile_expert[0:1, bass.ds(n, 1)], min_val=0, max_val=NE - 1)
    slot = sp.value_load(K.run_slot[0:1, bass.ds(n, 1)], min_val=0, max_val=SLOTS - 1)
    loads = sp.value_load(K.run_loads[0:1, bass.ds(n, 1)], min_val=LOADS, max_val=LOADS * TM)
    sp.wait_ge(K.weights_in, loads)
    sp.nop(nofuse=True)
    for w, dram in ((K.Wu, "Wu"), (K.Wg, "Wg"), (K.Wd, "Wd")):
        sp.dma_start(w[:, bass.ds(slot, 1), :, :].rearrange("p s k n -> p (s k) n"),
                     A["L0_ffn_" + dram][bass.ds(e, 1)].rearrange("e (k p) n -> p (e k) n", p=P))\
          .then_inc(K.weights_in, 16)
    sp.dma_start(K.br[:, bass.ds(slot, 1), :].rearrange("c s n -> c (s n)"),
                 K.bias_tab[bass.ds(e, 1)].rearrange("e c n -> c (e n)")).then_inc(K.weights_in, 16)


def expert_tiles(nc, K, A, name, count, routed):
    C = 2
    with ExitStack() as ctx:
        def sem(n):
            return ctx.enter_context(stage_semaphore(nc, f"{name}_{n}"))

        def sb(n, shape, dt):
            return ctx.enter_context(nc.sbuf_tensor(f"{name}_{n}", shape, dt))
        Wu, Wg, Wd, br = K.Wu, K.Wg, K.Wd, K.br
        weights_in = K.weights_in if routed else sem("weights_in")
        x_in = [sem(f"x_in{k}") for k in range(2)]
        y_out = [sem(f"y_out{k}") for k in range(2)]
        x_turned, xT_made, up_made, silu_made, act_made, act_turned, actT_made, y_made, y_taken = (
            sem("x_turned"), sem("xT_made"), sem("up_made"), sem("silu_made"), sem("act_made"), sem("act_turned"),
            sem("actT_made"), sem("y_made"), sem("y_taken"))
        scattered, pairs_in, index_set = sem("scattered"), sem("pairs_in"), sem("index_set")
        xe = sb("xe", [P, 2, DM], F32)
        ix = [sb(f"ix{k}", [P, 1], I32) for k in range(2)]
        xT = sb("xT", [P, 2, KC, P], F32)
        su = sb("su", [P, 2, HID], F32)
        aa = sb("aa", [P, 2, HID], F32)
        aT = sb("aT", [P, 2, KH, P], F32)
        y = sb("y", [P, 2, DM], F32)
        psG = [ctx.enter_context(nc.psum_tensor(f"{name}_psG{k}", [P, 512], F32)) for k in range(2)]
        psU = [ctx.enter_context(nc.psum_tensor(f"{name}_psU{k}", [P, 512], F32)) for k in range(2)]
        psX = ctx.enter_context(nc.psum_tensor(f"{name}_psX", [P, 2, 512], F32))
        psY = ctx.enter_context(nc.psum_tensor(f"{name}_psY", [P, 2, 512], F32))
        block = ctx.enter_context(nc.Block())
        half = count // 2
        yrows = K.pair_y if routed else K.shared_y

        @block.sync
        def _(sp):
            def load_x(i):
                for k in range(2):
                    n = 2 * i + k
                    sp.wait_ge(x_turned, n - 1 + C)
                    sp.nop(nofuse=True)
                    sp.dma_start(xe[:, k, :], K.xn_tab[bass.ds(n * P, P), :]).then_inc(x_in[k], 16)

            def load_next_run(n):
                new = sp.value_load(K.run_new[0:1, bass.ds(n, 1)], min_val=0, max_val=1)
                with sp.If(new):
                    before = sp.value_load(K.run_before[0:1, bass.ds(n, 1)], min_val=0, max_val=TM)
                    sp.wait_ge(y_made, before + C)
                    sp.nop(nofuse=True)
                    load_expert(sp, K, A, n)

            if routed:
                with sp.Fori(1, TM) as n:
                    load_next_run(n)
                return
            load_x(0)
            for w, dram in ((Wu, "sWu"), (Wg, "sWg"), (Wd, "sWd")):
                sp.dma_start(w[:, 0, :, :], A["L0_ffn_" + dram].rearrange("(k p) n -> p k n", p=P))\
                  .then_inc(weights_in, 16)
            sp.dma_start(br[:, 0, :], K.bias_tab[NE]).then_inc(weights_in, 16)
            load_expert(sp, K, A, 0)
            with sp.Fori(1, half) as i:
                load_x(i)

        @block.gpsimd
        def _(pool):
            if not routed:
                for t in range(NT):
                    m = P if t < NT - 1 else NLAST
                    for q in range(TOPE):
                        pool.indirect_dma_start(K.pair_tab, bass.IndirectOffsetOnAxis(ap=K.pair_at[0:m, q, t:t + 1], axis=0),
                                                K.token_id[0:m, t:t + 1], None).then_inc(scattered, 16)
                pool.wait_ge(scattered, 16 * NT * TOPE)
                pool.dma_start(K.pairs[:, :], K.pair_tab.rearrange("(p k) a -> p (k a)", p=P)).then_inc(pairs_in, 16)
                pool.wait_ge(pairs_in, 16)
                return
            def gather_pair(i):
                for k in range(2):
                    n = 2 * i + k
                    pool.wait_ge(x_turned, n - 1 + C)
                    pool.nop(nofuse=True)
                    pool.tensor_copy(ix[k][:, :], K.pairs[:, bass.ds(n, 1)]).then_inc(index_set, 1)
                    pool.wait_ge(index_set, n + 1)
                    pool.nop(nofuse=True)
                    pool.indirect_dma_start(xe[:, k, :], None, K.xn_tab,
                                            bass.IndirectOffsetOnAxis(ap=ix[k][:, :], axis=0)).then_inc(x_in[k], 16)

            with pool.Fori(0, SURE) as i:
                gather_pair(i)
            with pool.Fori(SURE, half) as i:
                with pool.If(pool.value_load(K.tile_used[0:1, bass.ds(2 * i, 1)], min_val=0, max_val=1)):
                    gather_pair(i)

        def in_pairs(eng, first, step, last):
            def pair(i):
                step(2 * i + 1, 1, i)
                step(2 * i + 2, 0, i + 1)
            first()
            if not routed:
                with eng.Fori(0, half - 1) as i:
                    pair(i)
                last(half - 1)
                return
            with eng.Fori(0, SURE - 1) as i:
                pair(i)
            with eng.Fori(SURE - 1, half - 1) as i:
                with eng.If(eng.value_load(K.tile_used[0:1, bass.ds(2 * i + 2, 1)], min_val=0, max_val=1)):
                    pair(i)
            last(eng.value_load(K.last_pair[0:1, 0:1], min_val=SURE - 1, max_val=half - 1))

        @block.tensor
        def _(pe):
            def turn_x(n, k, it):
                pe.wait_ge(x_in[k], 16 * it + 16)
                pe.nop(nofuse=True)
                for c in range(KC):
                    last = pe.transpose(psX[:, c // 4, (c % 4) * P:(c % 4 + 1) * P], xe[:, k, c * P:(c + 1) * P],
                                        K.ident[:, :])
                last.then_inc(x_turned, 1)

            def slot_of(n):
                if not routed:
                    return 0
                return pe.value_load(K.run_slot[0:1, bass.ds(n, 1)], min_val=0, max_val=SLOTS - 1)

            def product(ps, W, at, k, s):
                pe.matmul(ps[:, :], K.ones3[:, :], br[:, bass.ds(s, 1), at:at + HID], start=True, stop=False)
                for c in range(KC):
                    last = pe.matmul(ps[:, :], xT[:, k, c, :], W[:, bass.ds(s, 1), c, :], start=False,
                                     stop=(c == KC - 1))
                return last

            def gate(n, k, it):
                pe.wait_ge(xT_made, n + 1)
                pe.wait_ge(act_made, n - 1 + C)
                if routed:
                    loads = pe.value_load(K.run_loads[0:1, bass.ds(n, 1)], min_val=LOADS, max_val=LOADS * TM)
                    pe.wait_ge(weights_in, loads + LOADS)
                    pe.nop(nofuse=True)
                s = slot_of(n)
                product(psG[k], Wg, HID, k, s)
                return s

            def up(n, k, s):
                product(psU[k], Wu, 0, k, s).then_inc(up_made, 1)

            def turn_act(n, k):
                pe.wait_ge(act_made, n + 1 + C)
                pe.nop(nofuse=True)
                for c in range(KH):
                    last = pe.transpose(psX[:, 0, c * P:(c + 1) * P], aa[:, k, c * P:(c + 1) * P], K.ident[:, :])
                last.then_inc(act_turned, 1)

            def down(n, k):
                s = slot_of(n)
                pe.wait_ge(actT_made, n + 1)
                pe.wait_ge(y_taken, n + 1)
                pe.nop(nofuse=True)
                for a in range(2):
                    cols = slice(a * HALF, (a + 1) * HALF)
                    pe.matmul(psY[:, a, 0:HALF], K.ones3[:, :], br[:, bass.ds(s, 1), 2 * HID + a * HALF:2 * HID + (a + 1) * HALF],
                              start=True, stop=False)
                    for c in range(KH):
                        last = pe.matmul(psY[:, a, 0:HALF], aT[:, k, c, :], Wd[:, bass.ds(s, 1), c, cols], start=False,
                                         stop=(c == KH - 1))
                last.then_inc(y_made, 1)

            def first():
                turn_x(0, 0, 0)
                if not routed:
                    pe.wait_ge(weights_in, LOADS)
                up(0, 0, gate(0, 0, 0))
                turn_x(1, 1, 0)

            def step(n, k, it):
                s = gate(n, k, it)
                turn_act(n - 1, 1 - k)
                up(n, k, s)
                pe.wait_ge(actT_made, n)
                pe.nop(nofuse=True)
                turn_x(n + 1, 1 - k, it + (1 if k else 0))
                down(n - 1, 1 - k)

            def last(turn):
                n = 2 * turn + 1
                s = gate(n, 1, turn)
                turn_act(n - 1, 0)
                up(n, 1, s)
                down(n - 1, 0)
                turn_act(n, 1)
                down(n, 1)
            in_pairs(pe, first, step, last)

        @block.scalar
        def _(act):
            for k in range(2):
                act.sem_inc(y_out[k], 16)
            act.sem_inc(y_taken, 1)

            def take_x(n, k):
                act.wait_ge(x_turned, n + 1 + C)
                act.nop(nofuse=True)
                act.activation(xT[:, k, 0:4, :].rearrange("p c n -> p (c n)"), psX[:, 0, :], ACT.Copy)
                act.activation(xT[:, k, 4:KC, :].rearrange("p c n -> p (c n)"), psX[:, 1, 0:2 * P], ACT.Copy)\
                   .then_inc(xT_made, 1)

            def silu(n, k):
                act.wait_ge(up_made, n + 1)
                act.nop(nofuse=True)
                act.activation(su[:, k, :], psU[k][:, :], ACT.Silu).then_inc(silu_made, 1)

            def take_y(n, k, it):
                act.wait_ge(y_made, n + 1 + C)
                act.wait_ge(y_out[k], 16 * it + 16)
                act.nop(nofuse=True)
                act.activation(y[:, k, :].rearrange("p (a n) -> p a n", a=2), psY[:, :, 0:HALF], ACT.Copy)\
                   .then_inc(y_taken, 1)
                act.wait_ge(y_taken, n + 2)
                act.nop(nofuse=True)
                act.dma_start(yrows[bass.ds(n * P, P), :], y[:, k, :]).then_inc(y_out[k], 16)

            def first():
                take_x(0, 0)
                silu(0, 0)
                take_x(1, 1)

            def step(n, k, it):
                silu(n, k)
                take_x(n + 1, 1 - k)
                take_y(n - 1, 1 - k, it if k else it - 1)

            def last(turn):
                silu(2 * turn + 1, 1)
                take_y(2 * turn, 0, turn)
                take_y(2 * turn + 1, 1, turn)
                for k in range(2):
                    act.wait_ge(y_out[k], 16 * turn + 32)
                    act.nop(nofuse=True)
            in_pairs(act, first, step, last)

        @block.vector
        def _(dve):
            dve.sem_inc(x_turned, C)
            dve.sem_inc(act_made, C)
            dve.sem_inc(y_made, C)
            if not routed:
                dve.sem_inc(K.weights_in, LOADS)

            def multiply(n, k):
                dve.wait_ge(silu_made, n + 1)
                dve.nop(nofuse=True)
                dve.tensor_tensor(aa[:, k, :], psG[k][:, :], su[:, k, :], ALU.mult).then_inc(act_made, 1)

            def take_act(n, k):
                dve.wait_ge(act_turned, n + 1)
                dve.nop(nofuse=True)
                dve.tensor_copy(aT[:, k, :, :].rearrange("p c n -> p (c n)"), psX[:, 0, :]).then_inc(actT_made, 1)

            def first():
                multiply(0, 0)

            def step(n, k, it):
                take_act(n - 1, 1 - k)
                multiply(n, k)

            def last(turn):
                take_act(2 * turn, 0)
                multiply(2 * turn + 1, 1)
                take_act(2 * turn + 1, 1)
            in_pairs(dve, first, step, last)


def combine(nc, K, A, out):
    with ExitStack() as ctx:
        def sem(n):
            return ctx.enter_context(stage_semaphore(nc, f"comb_{n}"))

        def sb(n, shape, dt):
            return ctx.enter_context(nc.sbuf_tensor(f"comb_{n}", shape, dt))
        gathered = [sem(f"gathered{k}") for k in range(2)]
        shared_in = [sem(f"shared_in{k}") for k in range(2)]
        stepped, tile_made, out_written = sem("stepped"), sem("tile_made"), sem("out_written")
        yq = sb("yq", [P, 2, TOPE, DM], F32)
        ys = sb("ys", [P, 2, DM], F32)
        block = ctx.enter_context(nc.Block())

        @block.gpsimd
        def _(pool):
            for t in range(NT):
                m = P if t < NT - 1 else NLAST
                if t >= 2:
                    pool.wait_ge(tile_made, t - 1)
                for q in range(TOPE):
                    pool.indirect_dma_start(yq[0:m, t % 2, q, :], None, K.pair_y,
                                            bass.IndirectOffsetOnAxis(ap=K.pair_row[0:m, q, t:t + 1], axis=0))\
                        .then_inc(gathered[t % 2], 16)

        @block.sync
        def _(sp):
            for t in range(NT):
                if t >= 2:
                    sp.wait_ge(tile_made, t - 1)
                sp.dma_start(ys[:, t % 2, :], K.shared_y[t * P:(t + 1) * P, :]).then_inc(shared_in[t % 2], 16)

        @block.scalar
        def _(act):
            for t in range(NT):
                m = P if t < NT - 1 else NLAST
                act.wait_ge(tile_made, t + 1)
                act.dma_start(out[t * P:t * P + m, :], K.h[0:m, t, :]).then_inc(out_written, 16)
            act.wait_ge(out_written, 16 * NT)

        @block.vector
        def _(dve):
            step = Chain(dve, stepped)
            for t in range(NT):
                m = P if t < NT - 1 else NLAST
                dve.wait_ge(shared_in[t % 2], 16 * (t // 2 + 1))
                dve.wait_ge(gathered[t % 2], 16 * TOPE * (t // 2 + 1))
                acc = ys[0:m, t % 2, :]
                for q in range(TOPE):
                    step(dve.scalar_tensor_tensor(out=acc, in0=yq[0:m, t % 2, q, :], scalar=K.pair_w[0:m, q, t:t + 1],
                                                  in1=acc, op0=ALU.mult, op1=ALU.add))
                dve.tensor_tensor(K.h[0:m, t, :], K.h[0:m, t, :], acc, ALU.add).then_inc(tile_made, 1)


def ffn(nc, K, A, out):
    K.xn_tab = nc.dram_tensor("xn_table", (NP, DM), F32).ap()
    K.pair_tab = nc.dram_tensor("pair_table", (P * TM, 1), I32).ap()
    K.bias_tab = nc.dram_tensor("bias_table", (NE + 1, 3, BW), BF16).ap()
    K.pair_y = nc.dram_tensor("pair_rows", (TM * P, DM), F32).ap()
    K.shared_y = nc.dram_tensor("shared_rows", (NP, DM), F32).ap()
    with ExitStack() as ctx:
        def sb(n, shape, dt):
            return ctx.enter_context(nc.sbuf_tensor(n, shape, dt))
        K.ones3 = sb("ones3", [3, P], BF16)
        K.tile_expert, K.run_new, K.run_loads, K.run_slot, K.run_before = (
            sb(x, [P, TM], I32) for x in ("tile_expert", "run_new", "run_loads", "run_slot", "run_before"))
        K.tile_used = sb("tile_used", [P, TM], I32)
        K.last_pair = sb("last_pair", [P, 1], I32)
        K.pair_w = sb("pair_w", [P, TOPE, NT], F32)
        K.pair_row = sb("pair_row", [P, TOPE, NT], I32)
        K.pair_at = sb("pair_at", [P, TOPE, NT], I32)
        K.token_id = sb("token_id", [P, NT], I32)
        K.pairs = sb("pairs", [P, TM], I32)
        with ExitStack() as c2:
            made = c2.enter_context(stage_semaphore(nc, "ones3_made"))
            block = c2.enter_context(nc.Block())

            @block.vector
            def _(dve):
                dve.memset(K.ones3[:, :], 1.0).then_inc(made, 1)
                dve.wait_ge(made, 1)
        bias_parts(nc, K, A)
        with ExitStack() as c2:
            K.xn = c2.enter_context(nc.sbuf_tensor("xn", [P, NT, DM], F32))
            norm_block(nc, K, "ln_ffn", K.h, K.xn)
            route(nc, K, A)
        with ExitStack() as c2:
            K.Wu, K.Wg = (c2.enter_context(nc.sbuf_tensor(x, [P, SLOTS, KC, HID], F32)) for x in ("Wu", "Wg"))
            K.Wd = c2.enter_context(nc.sbuf_tensor("Wd", [P, SLOTS, KH, DM], F32))
            K.br = c2.enter_context(nc.sbuf_tensor("bias_rows", [3, SLOTS, BW], BF16))
            K.weights_in = c2.enter_context(stage_semaphore(nc, "routed_weights_in"))
            expert_tiles(nc, K, A, "shared", NT, False)
            expert_tiles(nc, K, A, "routed", TM, True)
        combine(nc, K, A, out)


def build(nc, A, out):
    RETIRED.clear()
    K = Keep()
    K.srt_src = nc.dram_tensor("sorted_src", (1, ES), I32).ap()
    K.srt_dst = nc.dram_tensor("sorted_dst", (1, ES), I32).ap()
    K.hs_tab = nc.dram_tensor("hs_table", (NP, ROW), F32).ap()
    K.bounce = [nc.dram_tensor(f"bounce{i}", (P, 2 * NC), F32).ap() for i in range(4)]
    with ExitStack() as ctx:
        def sb(n, shape, dt):
            return ctx.enter_context(nc.sbuf_tensor(n, shape, dt))
        K.ident = sb("ident", [P, P], F32)
        K.ones = sb("ones", [P, P], F32)
        K.iota_free = sb("iota_free", [P, P], F32)
        K.iota_part = sb("iota_part", [P, 1], F32)
        K.h = sb("h", [P, NT, DM], F32)
        constants(nc, K)
        with ExitStack() as c2:
            x_in = c2.enter_context(nc.sbuf_tensor("x_in", [P, NT, DM], F32))
            norm_block(nc, K, "ln_in", x_in, K.h, load=A["x"])
        with ExitStack() as c2:
            K.lnw, K.lnb, K.onw, K.onb = (c2.enter_context(nc.sbuf_tensor(n, [P, DM], F32))
                                          for n in ("ln_w", "ln_b", "on_w", "on_b"))
            gnn(nc, K, A)
            x_again = c2.enter_context(nc.sbuf_tensor("x_again", [P, NT, DM], F32))
            norm_block(nc, K, f"ln{L - 1}", K.h, K.h, K.lnw, K.lnb, also=(K.onw, K.onb, x_again), load=A["x"],
                       load_to=x_again)
        recycle(nc)
        ffn(nc, K, A, out)


_INS = ['x', 'src', 'dst', 'L0_gnn_Wsrc', 'L0_gnn_bsrc', 'L0_gnn_Wdst', 'L0_gnn_bdst', 'L0_gnn_attn', 'L0_gnn_ln_w',
        'L0_gnn_ln_b', 'L0_gnn_on_w', 'L0_gnn_on_b', 'L0_ffn_gate_w', 'L0_ffn_gate_b', 'L0_ffn_bias', 'L0_ffn_Wu',
        'L0_ffn_bu', 'L0_ffn_Wg', 'L0_ffn_bg', 'L0_ffn_Wd', 'L0_ffn_bd', 'L0_ffn_sWu', 'L0_ffn_sbu', 'L0_ffn_sWg',
        'L0_ffn_sbg', 'L0_ffn_sWd', 'L0_ffn_sbd']
_OUTS = [((N, DM), 'float32')]


def kernel(**inputs):
    import numpy as _np
    import concourse.bacc as _bacc
    from concourse import mybir as _mybir
    from concourse.bass_utils import run_bass_kernel_spmd as _run

    nc = _bacc.Bacc("TRN2", target_bir_lowering=False, num_devices=1)
    arrays, args = {}, {}
    for name in _INS:
        a = _np.ascontiguousarray(inputs[name])
        arrays[f"in_{name}_dram"] = a
        args[name] = nc.dram_tensor(f"in_{name}_dram", a.shape, _mybir.dt.from_np(a.dtype), kind="ExternalInput").ap()
    out = nc.dram_tensor("out_0_dram", _OUTS[0][0], _mybir.dt.from_np(_np.dtype(_OUTS[0][1])),
                         kind="ExternalOutput").ap()
    build(nc, args, out)
    r = _run(nc, [arrays], core_ids=[0])
    return r.results[0]["out_0_dram"]
```

```python
from contextlib import ExitStack, contextmanager

import concourse.bass as bass
from concourse import mybir

P = 128
N = 1250
E = 21250
DM = 768
H = 8
HD = DM // H
L = 2
NT = (N + P - 1) // P
NLAST = N - (NT - 1) * P
NP = NT * P
KC = DM // P
HALF = DM // 2
HH = H // 2
HW = HALF + HH
ROW = 2 * HW
GE = 2 * P
NG = (E + NT * (GE - 1)) // GE
NG += NG % 2
NTILE = 2 * NG
RING_LOGITS = 6
LAG = 5
RING_SUMS = 4
TPC = P // H
NC = (NTILE + TPC - 1) // TPC
NTP = NC * TPC
SENTINEL = 4095
UNIT = 64
UNITS = GE // UNIT + 1
ES = (E + GE + UNIT) // UNIT * UNIT
BIG = 1.0e30
EL = 125
EC = E // EL
SLOPE = 0.2
LN_EPS = 1e-5

F32 = mybir.dt.float32
I32 = mybir.dt.int32
BF16 = mybir.dt.bfloat16
ALU = mybir.AluOpType
ACT = mybir.ActivationFunctionType
AX = mybir.AxisListType


@contextmanager
def stage_semaphore(nc, name):
    handle = nc.alloc_semaphore(name)
    yield handle
    RETIRED.append(handle)


RETIRED = []


def recycle(nc):
    nc.clear_and_free_semaphores(list(RETIRED))
    RETIRED.clear()
    nc.all_engine_barrier()


class Chain:

    def __init__(self, eng, sem):
        self.eng, self.sem, self.n = eng, sem, 0

    def __call__(self, instruction):
        self.n += 1
        instruction.then_inc(self.sem, 1)
        self.eng.wait_ge(self.sem, self.n)


def bcast(row, parts):
    return row.rearrange("(a n) -> a n", a=1).broadcast_to([parts, row.shape[0]])


def constants(nc, K):
    with ExitStack() as ctx:
        s_zero = ctx.enter_context(stage_semaphore(nc, "identity_zeroed"))
        s_all = ctx.enter_context(stage_semaphore(nc, "constants_made"))
        s_sel = ctx.enter_context(stage_semaphore(nc, "selectors_made"))
        block = ctx.enter_context(nc.Block())

        @block.gpsimd
        def _(pool):
            pool.memset(K.ident[:, :], 0.0).then_inc(s_zero, 1)
            pool.memset(K.ones[:, :], 1.0).then_inc(s_all, 1)
            pool.wait_ge(s_zero, 1)
            pool.affine_select(out=K.ident[:, :], in_=K.ident[:, :], compare_op=ALU.not_equal, fill=1.0,
                               base=0, pattern=[[-1, P]], channel_multiplier=1).then_inc(s_all, 1)
            pool.iota(K.iota_free[:, :], [[1, P]], base=0, channel_multiplier=0,
                      allow_small_or_imprecise_dtypes=True).then_inc(s_all, 1)
            pool.iota(K.iota_part[:, :], [[0, 1]], base=0, channel_multiplier=1,
                      allow_small_or_imprecise_dtypes=True).then_inc(s_all, 1)
            pool.wait_ge(s_all, 4)

        @block.vector
        def _(dve):
            dve.wait_ge(s_all, 4)
            dve.tensor_reduce(K.sel_head[:, :], K.ident[:, :].rearrange("p (t h) -> p h t", h=H), AX.X, ALU.add)\
               .then_inc(s_sel, 1)
            dve.tensor_reduce(K.sel_tile[:, :], K.ident[:, :].rearrange("p (t h) -> p t h", h=H), AX.X, ALU.add)\
               .then_inc(s_sel, 1)
            dve.tensor_copy(K.sel_headT[:, :].rearrange("p (t h) -> p t h", h=H),
                            K.ident[0:H, 0:H].rearrange("p (t h) -> p t h", t=1).broadcast_to([H, TPC, H]))\
               .then_inc(s_sel, 1)
            dve.wait_ge(s_sel, 3)


def norm_block(nc, K, name, src, dst, weight=None, bias=None, also=None, load=None, load_to=None, ahead=None):
    load_to = src if load_to is None else load_to
    rounds = [(src, weight, bias)] + ([(dst, also[0], also[1])] if also is not None else [])
    groups = [range(0, NT // 2), range(NT // 2, NT)]
    by_pool = NT // 2 + 1
    with ExitStack() as ctx:
        def sem(n):
            return ctx.enter_context(stage_semaphore(nc, f"{name}_{n}"))
        loaded = [sem(f"loaded{i}") for i in range(2)]
        stepped, dev_made, root_made = sem("stepped"), sem("deviation_made"), sem("root_made")
        scales_made, centred, normalised, weighed, added, summed = (
            sem("scales_made"), sem("centred"), sem("normalised"), sem("weighed"), sem("added"), sem("summed"))
        stats = ctx.enter_context(nc.sbuf_tensor(f"{name}_stats", [P, NT, 2, 6], F32))
        mv = ctx.enter_context(nc.sbuf_tensor(f"{name}_mv", [P, NT, 2], F32))
        var = ctx.enter_context(nc.sbuf_tensor(f"{name}_var", [P, NT], F32))
        std = ctx.enter_context(nc.sbuf_tensor(f"{name}_std", [P, NT], F32))
        rstd = ctx.enter_context(nc.sbuf_tensor(f"{name}_rstd", [P, NT], F32))
        less = ctx.enter_context(nc.sbuf_tensor(f"{name}_less", [P, NT], F32))
        block = ctx.enter_context(nc.Block())

        if ahead is not None:
            @block.sync
            def _(sp):
                ahead(sp)

        if load is not None:
            @block.sync
            def _(sp):
                half = NT // 2
                sp.dma_start(load_to[:, 0:half, :], load[0:half * P, :].rearrange("(t p) d -> p t d", p=P))\
                  .then_inc(loaded[0], 16)
                sp.wait_ge(stepped, 1)
                sp.dma_start(load_to[:, half:NT - 1, :],
                             load[half * P:(NT - 1) * P, :].rearrange("(t p) d -> p t d", p=P)).then_inc(loaded[1], 16)
                sp.dma_start(load_to[0:NLAST, NT - 1, :], load[(NT - 1) * P:N, :]).then_inc(loaded[1], 16)
                for i in range(2):
                    sp.wait_ge(loaded[i], 16 * (i + 1))

        @block.vector
        def _(dve):
            step = Chain(dve, stepped)
            if load is not None:
                step(dve.memset(load_to[:, NT - 1, :], 0.0))
            for r, (x, w, b) in enumerate(rounds):
                for i, tiles in enumerate(groups):
                    a, z = tiles[0], tiles[-1] + 1
                    if r == 0 and load is not None and load_to is src:
                        dve.wait_ge(loaded[i], 16 * (i + 1))
                    if r > 0:
                        dve.wait_ge(added, (r - 1) * by_pool + min(z, by_pool))
                    for t in tiles:
                        for h in range(2):
                            last = dve.bn_stats(stats[:, t, h, :], x[:, t, h * HALF:(h + 1) * HALF])
                    step(last)
                    for t in tiles:
                        last = dve.bn_aggr(mv[:, t, :], stats[:, t, :, :].rearrange("p a b -> p (a b)"))
                    step(last)
                    step(dve.tensor_scalar(less[:, a:z], mv[:, a:z, 0], -1.0, None, ALU.mult))
                    dve.tensor_scalar(var[:, a:z], mv[:, a:z, 1], LN_EPS, None, ALU.add).then_inc(dev_made, 1)
                for i, tiles in enumerate(groups):
                    a, z = tiles[0], tiles[-1] + 1
                    dve.wait_ge(root_made, 2 * r + i + 1)
                    dve.reciprocal(rstd[:, a:z], std[:, a:z]).then_inc(scales_made, 1)
                if w is None:
                    continue
                for t in range(NT):
                    dve.wait_ge(normalised, r * NT + t + 1)
                    weigh = dve.tensor_tensor(dst[:, t, :], dst[:, t, :], w[:, :], ALU.mult)
                    if t < by_pool:
                        weigh.then_inc(weighed, 1)
                        continue
                    step(weigh)
                    step(dve.tensor_tensor(dst[:, t, :], dst[:, t, :], b[:, :], ALU.add))
                    if r == 1:
                        if t == by_pool:
                            for i in range(2):
                                dve.wait_ge(loaded[i], 16 * (i + 1))
                        step(dve.tensor_tensor(dst[:, t, :], dst[:, t, :], also[2][:, t, :], ALU.add))

        @block.scalar
        def _(act):
            for r, (x, w, b) in enumerate(rounds):
                for i, tiles in enumerate(groups):
                    a, z = tiles[0], tiles[-1] + 1
                    if i == 0:
                        act.wait_ge(dev_made, 2 * r + 1)
                        act.activation(std[:, a:z], var[:, a:z], ACT.Sqrt).then_inc(root_made, 1)
                    for t in tiles:
                        act.activation(dst[:, t, :], x[:, t, :], ACT.Identity, bias=less[:, t:t + 1])\
                           .then_inc(centred, 1)
                    if i == 0:
                        act.wait_ge(dev_made, 2 * r + 2)
                        a2, z2 = groups[1][0], groups[1][-1] + 1
                        act.activation(std[:, a2:z2], var[:, a2:z2], ACT.Sqrt).then_inc(root_made, 1)
                    act.wait_ge(scales_made, 2 * r + i + 1)
                    for t in tiles:
                        act.wait_ge(centred, r * NT + t + 1)
                        act.activation(dst[:, t, :], dst[:, t, :], ACT.Copy, scale=rstd[:, t:t + 1])\
                           .then_inc(normalised, 1)

        @block.gpsimd
        def _(pool):
            for r, (x, w, b) in enumerate(rounds):
                if b is None:
                    continue
                if r == 1:
                    for i in range(2):
                        pool.wait_ge(loaded[i], 16 * (i + 1))
                    for t in range(by_pool):
                        pool.tensor_tensor(also[2][:, t, :], also[2][:, t, :], b[:, :], ALU.add).then_inc(summed, 1)
                    pool.wait_ge(summed, by_pool)
                for t in range(by_pool):
                    pool.wait_ge(weighed, r * by_pool + t + 1)
                    more = b[:, :] if r == 0 else also[2][:, t, :]
                    pool.tensor_tensor(dst[:, t, :], dst[:, t, :], more, ALU.add).then_inc(added, 1)


def load_x(sp, A, x_in, last_zeroed, nodes_in):
    x = A["x"]
    sp.dma_start(x_in[:, 0:NT - 1, :], x[0:(NT - 1) * P, :].rearrange("(t p) d -> p t d", p=P)).then_inc(nodes_in, 16)
    sp.wait_ge(last_zeroed, 1)
    sp.dma_start(x_in[0:NLAST, NT - 1, :], x[(NT - 1) * P:N, :]).then_inc(nodes_in, 16)


def order_edges(nc, K, src, dst):
    with ExitStack() as ctx:
        def sem(n):
            return ctx.enter_context(stage_semaphore(nc, f"order_{n}"))

        def sb(n, shape, dt):
            return ctx.enter_context(nc.sbuf_tensor(f"order_{n}", shape, dt))
        tails_set, tails_out, last_set, edges_in, compared, counted, stepped = (
            sem("tails_set"), sem("tails_out"), sem("last_set"), sem("edges_in"), sem("compared"), sem("counted"),
            sem("stepped"))
        tails = sb("tails", [1, 2, ES - E], I32)
        nxt = sb("nxt", [EL, EC], I32)
        junk = sb("junk", [EL, EC], F32)
        falls = sb("falls", [EL, 1], F32)
        some = sb("some", [P, 1], F32)
        flags = sb("flags", [P, 2], I32)
        ps = ctx.enter_context(nc.psum_tensor("order_ps", [P, 1], F32))
        with nc.Block() as block:
            @block.sync
            def _(sp):
                sp.dma_start(K.dall[:, :], dst.rearrange("(p c) -> p c", p=EL)).then_inc(edges_in, 16)
                sp.dma_start(K.sall[:, :], src.rearrange("(p c) -> p c", p=EL)).then_inc(edges_in, 16)
                sp.wait_ge(last_set, 1)
                sp.dma_start(nxt[0:EL - 1, :], dst[1:1 + (EL - 1) * EC].rearrange("(p c) -> p c", p=EL - 1))\
                  .then_inc(edges_in, 16)
                sp.dma_start(nxt[EL - 1:EL, 0:EC - 1], dst[1 + (EL - 1) * EC:E].rearrange("(a n) -> a n", a=1))\
                  .then_inc(edges_in, 16)
                sp.wait_ge(tails_set, 2)
                sp.dma_start(K.srt_src[0:1, E:ES], tails[:, 0, :]).then_inc(tails_out, 16)
                sp.dma_start(K.srt_dst[0:1, E:ES], tails[:, 1, :]).then_inc(tails_out, 16)
                sp.wait_ge(tails_out, 32)

            @block.gpsimd
            def _(pool):
                pool.memset(nxt[:, EC - 1:EC], SENTINEL).then_inc(last_set, 1)
                pool.memset(tails[:, 0, :], 0).then_inc(tails_set, 1)
                pool.memset(tails[:, 1, :], SENTINEL).then_inc(tails_set, 1)

            @block.vector
            def _(dve):
                step = Chain(dve, stepped)
                dve.wait_ge(edges_in, 64)
                step(dve.tensor_copy(K.dallf[:, :], K.dall[:, :]))
                step(dve.tensor_tensor(junk[:, :], K.dallf[:, :], nxt[:, :], ALU.is_gt))
                dve.tensor_reduce(falls[:, :], junk[:, :], AX.X, ALU.add).then_inc(compared, 1)
                dve.wait_ge(counted, 1)
                step(dve.tensor_scalar(some[:, :], ps[:, :], 1.0, None, ALU.min))
                step(dve.tensor_copy(flags[:, 0:1], some[:, :]))
                step(dve.tensor_scalar(flags[:, 1:2], some[:, :], -1.0, 1.0, ALU.mult, ALU.add))

            @block.tensor
            def _(pe):
                pe.wait_ge(compared, 1)
                pe.matmul(ps[:, :], K.ones[0:EL, :], falls[:, :], start=True, stop=True).then_inc(counted, 1)

        counting_sort(nc, ctx, K, src, dst, flags)


def counting_sort(nc, ctx, K, src, dst, flags):
    BINS = NP

    def sem(n):
        return ctx.enter_context(stage_semaphore(nc, f"sort_{n}"))

    def sb(n, shape, dt):
        return ctx.enter_context(nc.sbuf_tensor(f"sort_{n}", shape, dt))
    copied, tables, onehot_made, counted, stepped, placed, before_made, after_made, column_set, scattered, places_free = (
        sem("copied"), sem("tables"), sem("onehot_made"), sem("counted"), sem("stepped"), sem("placed"),
        sem("before_made"), sem("after_made"), sem("column_set"), sem("scattered"), sem("places_free"))
    bins = sb("bins", [P, BINS], F32)
    oh = sb("oh", [EL, BINS], BF16)
    cnt = sb("cnt", [P, BINS], F32)
    base = sb("base", [P, BINS], F32)
    zer = sb("zer", [P, BINS], F32)
    prod = sb("prod", [EL, BINS], F32)
    upper, rest, onesb = (sb(x, [P, P], BF16) for x in ("upper", "rest", "onesb"))
    pf = sb("pf", [EL, 1], F32)
    pi, si, di = (sb(x, [EL, 1], I32) for x in ("pi", "si", "di"))
    ps = ctx.enter_context(nc.psum_tensor("sort_ps", [P, 3 * 512], F32))
    cuts = [(a, min(a + 512, BINS)) for a in range(0, BINS, 512)]
    block = ctx.enter_context(nc.Block())

    def flag(eng):
        return eng.value_load(flags[0:1, 0:1], min_val=0, max_val=1)

    @block.sync
    def _(sp):
        with sp.If(sp.value_load(flags[0:1, 1:2], min_val=0, max_val=1)):
            sp.dma_start(K.srt_src[0:1, 0:E], src.rearrange("(a n) -> a n", a=1)).then_inc(copied, 16)
            sp.dma_start(K.srt_dst[0:1, 0:E], dst.rearrange("(a n) -> a n", a=1)).then_inc(copied, 16)
            sp.wait_ge(copied, 32)

    @block.gpsimd
    def _(pool):
        with pool.If(flag(pool)):
            pool.iota(bins[:, :], [[1, BINS]], base=0, channel_multiplier=0,
                      allow_small_or_imprecise_dtypes=True).then_inc(tables, 1)
            for x in (upper, rest, onesb):
                pool.memset(x[:, :], 1.0).then_inc(tables, 1)
            pool.wait_ge(tables, 4)
            pool.affine_select(out=upper[:, :], in_=upper[:, :], compare_op=ALU.is_gt, fill=0.0, base=0,
                               pattern=[[1, P]], channel_multiplier=-1).then_inc(tables, 1)
            pool.affine_select(out=rest[:, :], in_=rest[:, :], compare_op=ALU.is_ge, fill=0.0, base=0,
                               pattern=[[-1, P]], channel_multiplier=1).then_inc(tables, 1)
            with pool.Fori(0, EC) as c:
                pool.tensor_copy(si[:, :], K.sall[:, bass.ds(c, 1)]).then_inc(column_set, 1)
                pool.tensor_copy(di[:, :], K.dall[:, bass.ds(c, 1)]).then_inc(column_set, 1)
                pool.wait_ge(placed, c + 1)
                pool.nop(nofuse=True)
                pool.wait_ge(column_set, 2 * c + 2)
                pool.nop(nofuse=True)
                for col, out in ((si, K.srt_src), (di, K.srt_dst)):
                    pool.indirect_dma_start(out.rearrange("a n -> (a n)").rearrange("(n b) -> n b", b=1),
                                            bass.IndirectOffsetOnAxis(ap=pi[:, :], axis=0), col[:, :], None)\
                        .then_inc(scattered, 16)
                pool.wait_ge(scattered, 32 * c + 32)
                pool.nop(nofuse=True)
                pool.sem_inc(places_free, 1)

    @block.tensor
    def _(pe):
        def add_up(weights, moving, start, stop):
            for a, b in cuts:
                last = pe.matmul(ps[:, a:b], weights, moving[:, a:b], start=start, stop=stop, skip_group_check=True)
            return last

        with pe.If(flag(pe)):
            pe.wait_ge(tables, 6)
            pe.wait_ge(stepped, 1)
            add_up(K.ident[:, :], zer, True, False)
            with pe.Fori(0, EC) as c:
                pe.wait_ge(onehot_made, c + 1)
                pe.nop(nofuse=True)
                add_up(onesb[0:EL, :], oh, False, False).then_inc(after_made, 1)
            add_up(K.ident[:, :], zer, False, True).then_inc(counted, 1)
            pe.wait_ge(counted, 2)
            add_up(K.ident[:, :], base, True, False)
            with pe.Fori(0, EC) as c:
                pe.wait_ge(onehot_made, c + EC + 1)
                pe.nop(nofuse=True)
                add_up(upper[0:EL, :], oh, False, False).then_inc(before_made, 1)
                pe.wait_ge(placed, c + 1)
                pe.nop(nofuse=True)
                add_up(rest[0:EL, :], oh, False, False).then_inc(after_made, 1)
            add_up(K.ident[:, :], zer, False, True).then_inc(counted, 1)

    @block.vector
    def _(dve):
        with dve.If(flag(dve)):
            step = Chain(dve, stepped)
            dve.sem_inc(places_free, 1)
            dve.sem_inc(after_made, 1)
            step(dve.memset(zer[:, :], 0.0))
            dve.wait_ge(tables, 6)

            def onehot(c, n):
                dve.wait_ge(after_made, n + 1)
                dve.nop(nofuse=True)
                dve.tensor_scalar(oh[:, :], bins[0:EL, :], K.dallf[:, bass.ds(c, 1)], None, ALU.is_equal)\
                   .then_inc(onehot_made, 1)

            with dve.Fori(0, EC) as c:
                onehot(c, c)
            dve.wait_ge(counted, 1)
            step(dve.tensor_copy(cnt[:, :], ps[:, 0:BINS]))
            step(dve.tensor_tensor_scan(base[:, :], cnt[:, :], zer[:, :], 0.0, ALU.add, ALU.add))
            dve.tensor_tensor(base[:, :], base[:, :], cnt[:, :], ALU.subtract).then_inc(counted, 1)
            dve.wait_ge(counted, 2)
            with dve.Fori(0, EC) as c:
                onehot(c, c + EC)
                dve.wait_ge(before_made, c + 1)
                dve.nop(nofuse=True)
                dve.tensor_tensor(prod[:, :], ps[0:EL, 0:BINS], oh[:, :], ALU.mult).then_inc(stepped, 1)
                dve.wait_ge(stepped, 2 * c + step.n + 1)
                dve.nop(nofuse=True)
                dve.tensor_reduce(pf[:, :], prod[:, :], AX.X, ALU.add).then_inc(stepped, 1)
                dve.wait_ge(places_free, c + 1)
                dve.nop(nofuse=True)
                dve.wait_ge(stepped, 2 * c + step.n + 2)
                dve.nop(nofuse=True)
                dve.tensor_copy(pi[:, :], pf[:, :]).then_inc(placed, 1)
            dve.wait_ge(counted, 3)


def edge_tables(nc, K, ahead):
    NB = NT
    with ExitStack() as ctx:
        def sem(n):
            return ctx.enter_context(stage_semaphore(nc, f"edges_{n}"))

        def sb(n, shape, dt):
            return ctx.enter_context(nc.sbuf_tensor(f"edges_{n}", shape, dt))
        stepped, counted = sem("stepped"), sem("counted")
        rows_in, units_made, rows_made, turned = sem("rows_in"), sem("units_made"), sem("rows_made"), sem("turned")
        junk = sb("junk", [EL, EC], F32)
        cnt = sb("cnt", [EL, NB + 1], F32)
        st = sb("st", [P, NB + 1], F32)
        sz = sb("sz", [P, NB], F32)
        szi = sb("szi", [P, NB], I32)
        zer = sb("zer", [P, NB], F32)
        ginc = sb("ginc", [P, NB], F32)
        cbase = sb("cbase", [P, NB + 1], F32)
        ig = sb("ig", [P, NG], F32)
        blk = sb("blk", [P, NG], F32)
        offf = sb("offf", [P, NG], F32)
        tmp = sb("tmp", [P, NG], F32)
        grid = sb("grid", [P, NG, NB + 1], F32)
        first = sb("first", [P, 1], F32)
        first_i = sb("first_i", [P, 1], I32)
        unit_i = sb("unit_i", [P, UNITS], I32)
        bit = sb("bit", [P, 1], F32)
        rows = sb("rows", [P, 2, UNITS * UNIT], I32)
        rows_f = sb("rows_f", [P, 2, UNITS * UNIT], F32)
        moved = sb("moved", [P, 2, UNITS * UNIT], F32)
        own = sb("own", [P, NTILE], F32)
        iota_made = sem("iota_made")
        ps = ctx.enter_context(nc.psum_tensor("edges_ps", [P, 512], F32))
        psT = ctx.enter_context(nc.psum_tensor("edges_psT", [P, 2, 2, P], F32))
        block = ctx.enter_context(nc.Block())

        @block.sync
        def _(sp):
            ahead(sp)

        @block.gpsimd
        def _(pool):
            pool.iota(ig[:, :], [[1, NG]], base=0, channel_multiplier=0,
                      allow_small_or_imprecise_dtypes=True).then_inc(iota_made, 1)
            for c in range(UNITS):
                pool.wait_ge(units_made, c + 1)
                for i, arr in enumerate((K.srt_src, K.srt_dst)):
                    pool.indirect_dma_start(rows[0:NG, i, c * UNIT:(c + 1) * UNIT], None,
                                            arr.rearrange("a (n u) -> (a n) u", u=UNIT),
                                            bass.IndirectOffsetOnAxis(ap=unit_i[0:NG, c:c + 1], axis=0))\
                        .then_inc(rows_in, 16)

        @block.vector
        def _(dve):
            step = Chain(dve, stepped)
            for b in range(NB + 1):
                step(dve.tensor_scalar(junk[:, :], K.dallf[:, :], float(P * b), 0.0, ALU.is_lt, ALU.add,
                                       accum_out=cnt[:, b:b + 1]))
            dve.engine_nop().then_inc(counted, 1)
            dve.wait_ge(counted, 2)
            step(dve.tensor_copy(st[:, :], ps[:, 0:NB + 1]))
            step(dve.tensor_tensor(sz[:, :], st[:, 1:NB + 1], st[:, 0:NB], ALU.subtract))
            step(dve.tensor_scalar(szi[:, :], sz[:, :], float(GE - 1), None, ALU.add))
            step(dve.tensor_scalar(szi[:, :], szi[:, :], GE.bit_length() - 1, None, ALU.arith_shift_right))
            step(dve.tensor_copy(sz[:, :], szi[:, :]))
            step(dve.memset(zer[:, :], 0.0))
            step(dve.tensor_tensor_scan(ginc[:, :], sz[:, :], zer[:, :], 0.0, ALU.add, ALU.add))
            step(dve.tensor_tensor(sz[:, :], ginc[:, :], sz[:, :], ALU.subtract))
            step(dve.memset(cbase[:, NB:NB + 1], float(E)))
            step(dve.scalar_tensor_tensor(out=cbase[:, 0:NB], in0=sz[:, :], scalar=-float(GE), in1=st[:, 0:NB],
                                          op0=ALU.mult, op1=ALU.add))
            dve.wait_ge(iota_made, 1)
            step(dve.tensor_tensor(grid[:, :, 0:NB],
                                   ig[:, :].rearrange("p (g b) -> p g b", b=1).broadcast_to([P, NG, NB]),
                                   ginc[:, :].rearrange("p (g b) -> p g b", g=1).broadcast_to([P, NG, NB]), ALU.is_ge))
            step(dve.tensor_reduce(blk[:, :], grid[:, :, 0:NB], AX.X, ALU.add))
            step(dve.tensor_tensor(grid[:, :, :],
                                   blk[:, :].rearrange("p (g b) -> p g b", b=1).broadcast_to([P, NG, NB + 1]),
                                   K.iota_free[:, 0:NB + 1].rearrange("p (g b) -> p g b", g=1)
                                   .broadcast_to([P, NG, NB + 1]), ALU.is_equal))
            step(dve.tensor_tensor(grid[:, :, :], grid[:, :, :],
                                   cbase[:, :].rearrange("p (g b) -> p g b", g=1).broadcast_to([P, NG, NB + 1]),
                                   ALU.mult))
            step(dve.tensor_reduce(tmp[:, :], grid[:, :, :], AX.X, ALU.add))
            step(dve.scalar_tensor_tensor(out=offf[:, :], in0=ig[:, :], scalar=float(GE), in1=tmp[:, :],
                                          op0=ALU.mult, op1=ALU.add))
            step(dve.tensor_scalar(offf[:, :], offf[:, :], float(E), 0.0, ALU.min, ALU.max))
            step(dve.tensor_scalar(blk[:, :], blk[:, :], float(NB - 1), None, ALU.min))
            step(dve.tensor_copy(K.off_i[:, :], offf[:, :]))
            step(dve.tensor_copy(K.blk_i[:, :], blk[:, :]))
            step(dve.tensor_scalar(K.blkiota[:, :], blk[:, :], float(P), K.iota_part[:, 0:1], ALU.mult, ALU.add))
            step(dve.tensor_tensor(offf[:, :], offf[:, :], K.ident[:, 0:NG], ALU.mult))
            step(dve.tensor_reduce(first[:, :], offf[:, :], AX.X, ALU.add))
            step(dve.tensor_copy(first_i[:, :], first[:, :]))
            step(dve.tensor_scalar(unit_i[:, 0:1], first_i[:, :], UNIT.bit_length() - 1, None, ALU.arith_shift_right))
            dve.engine_nop().then_inc(units_made, 1)
            for c in range(1, UNITS):
                dve.tensor_scalar(unit_i[:, c:c + 1], unit_i[:, 0:1], float(c), None, ALU.add).then_inc(units_made, 1)
            step(dve.tensor_scalar(first_i[:, :], first_i[:, :], UNIT - 1, None, ALU.bitwise_and))
            step(dve.tensor_copy(first[:, :], first_i[:, :]))
            step(dve.tensor_scalar(tmp[:, :], blk[:, :], float(P), None, ALU.mult))
            step(dve.memset(K.dcolf[:, NTILE:NTP], float(SENTINEL)))
            dve.wait_ge(rows_in, 32 * UNITS)
            step(dve.tensor_copy(rows_f[:NG, :, :], rows[:NG, :, :]))
            w, by = UNITS * UNIT, UNIT // 2
            while by:
                step(dve.tensor_scalar(bit[:, 0:1], first[:, :], float(by), None, ALU.is_ge))
                step(dve.scalar_tensor_tensor(out=first[:, :], in0=bit[:, 0:1], scalar=-float(by), in1=first[:, :],
                                              op0=ALU.mult, op1=ALU.add))
                step(dve.tensor_tensor(moved[:NG, :, 0:w - by], rows_f[:NG, :, by:w], rows_f[:NG, :, 0:w - by],
                                       ALU.subtract))
                step(dve.scalar_tensor_tensor(out=rows_f[:NG, :, 0:w - by], in0=moved[:NG, :, 0:w - by],
                                              scalar=bit[:NG, 0:1], in1=rows_f[:NG, :, 0:w - by],
                                              op0=ALU.mult, op1=ALU.add))
                w, by = w - by, by // 2
            dve.engine_nop().then_inc(rows_made, 1)
            dve.wait_ge(turned, 1)
            for i, col in enumerate((K.srccol, K.dcolf)):
                step(dve.tensor_copy(col[:, 0:NTILE].rearrange("p (g j) -> p j g", j=2), psT[:, i, :, 0:NG]))
            step(dve.tensor_tensor(K.drel[:, :].rearrange("p (g j) -> p g j", j=2),
                                   K.dcolf[:, 0:NTILE].rearrange("p (g j) -> p g j", j=2),
                                   tmp[:, :].rearrange("p (g j) -> p g j", j=1).broadcast_to([P, NG, 2]),
                                   ALU.subtract))
            for bound, op in ((0.0, ALU.is_ge), (float(P), ALU.is_lt)):
                step(dve.tensor_scalar(own[:, :], K.drel[:, :], bound, None, op))
                step(dve.tensor_scalar(K.dcolf[:, 0:NTILE], K.dcolf[:, 0:NTILE], -float(SENTINEL), None, ALU.add))
                step(dve.tensor_tensor(K.dcolf[:, 0:NTILE], K.dcolf[:, 0:NTILE], own[:, :], ALU.mult))
                step(dve.tensor_scalar(K.dcolf[:, 0:NTILE], K.dcolf[:, 0:NTILE], float(SENTINEL), None, ALU.add))

        @block.tensor
        def _(pe):
            pe.wait_ge(counted, 1)
            pe.matmul(ps[:, 0:NB + 1], K.ones[0:EL, :], cnt[:, :], start=True, stop=True).then_inc(counted, 1)
            pe.wait_ge(rows_made, 1)
            for i in range(2):
                for j in range(2):
                    last = pe.transpose(psT[:, i, j, 0:NG], rows_f[0:NG, i, j * P:(j + 1) * P], K.ident[0:NG, 0:NG])
            last.then_inc(turned, 1)


def spread_ends(dve, K, spread, ends):
    return dve.tensor_tensor(spread[:, :, :], ends[:, :, :].rearrange("p a (c t) -> p (a c) t", t=1)
                             .broadcast_to([P, 2 * NC, TPC]),
                             K.sel_tile[:, :].rearrange("p (a t) -> p a t", a=1).broadcast_to([P, 2 * NC, TPC]),
                             ALU.mult)


def own_tile(dve, K, step, out, ps, spread):
    step(dve.tensor_tensor(spread[:, :, :], ps[:, :].rearrange("p (a t) -> p a t", t=TPC),
                           K.sel_tile[:, :].rearrange("p (a t) -> p a t", a=1).broadcast_to([P, 2 * NC, TPC]),
                           ALU.mult))
    step(dve.tensor_reduce(out[:, :, :].rearrange("p a c -> p (a c)"), spread[:, :, :], AX.X, ALU.add))


def segment_tables(nc, K):
    with ExitStack() as ctx:
        def sem(n):
            return ctx.enter_context(stage_semaphore(nc, f"seg_{n}"))

        def sb(n, shape, dt):
            return ctx.enter_context(nc.sbuf_tensor(f"seg_{n}", shape, dt))
        stepped, turned, rows_made, links_made = sem("stepped"), sem("turned"), sem("rows_made"), sem("links_made")
        drep = sb("drep", [P, NTP, H], F32)
        dT = sb("dT", [P, NC, P], F32)
        ends = sb("ends", [P, 2, NC], F32)
        rows = sb("rows", [H, 2, NC, TPC], F32)
        link = sb("link", [H, 2, NC * TPC], F32)
        whole = sb("whole", [H, NC * TPC], F32)
        linkT = sb("linkT", [P, 2, NC], F32)
        ps = [ctx.enter_context(nc.psum_tensor(f"seg_ps{i}", [P, 512], F32)) for i in range(3)]
        spread = sb("spread", [P, 2 * NC, TPC], F32)
        ps_rows = ctx.enter_context(nc.psum_tensor("seg_ps_rows", [H, 2 * NTP], F32))
        ps_links = ctx.enter_context(nc.psum_tensor("seg_ps_links", [P, 2 * NTP], F32))
        made = sem("made")
        block = ctx.enter_context(nc.Block())

        @block.tensor
        def _(pe):
            pe.wait_ge(made, 1)
            for c in range(NC):
                last = pe.transpose(ps[c // 4][:, (c % 4) * P:(c % 4 + 1) * P],
                                    drep[:, c * TPC:(c + 1) * TPC, :].rearrange("p t h -> p (t h)"), K.ident[:, :])
            last.then_inc(turned, 1)
            pe.wait_ge(made, 2)
            pe.matmul(ps_rows[:, :], K.sel_head[:, :], spread[:, :, :].rearrange("p a t -> p (a t)"), start=True,
                      stop=True).then_inc(rows_made, 1)
            pe.wait_ge(made, 3)
            pe.matmul(ps_links[:, :], K.sel_headT[:, :], link[:, :, :].rearrange("h a n -> h (a n)"), start=True,
                      stop=True).then_inc(links_made, 1)

        @block.vector
        def _(dve):
            step = Chain(dve, stepped)
            dve.tensor_copy(drep[:, :, :], K.dcolf[:, :].rearrange("p (t h) -> p t h", h=1)
                            .broadcast_to([P, NTP, H])).then_inc(made, 1)
            dve.wait_ge(turned, 1)
            for i in range(3):
                last = dve.tensor_copy(dT[:, 4 * i:4 * i + 4, :].rearrange("p c l -> p (c l)"), ps[i][:, :])
            step(last)
            step(dve.tensor_copy(ends[:, 0, :], dT[:, :, 0]))
            step(dve.tensor_copy(ends[:, 1, :], dT[:, :, P - 1]))
            spread_ends(dve, K, spread, ends).then_inc(made, 1)

            def penalty(out, mask):
                return dve.tensor_scalar(out, mask, 1.0, BIG, ALU.subtract, ALU.mult)

            step(dve.memset(K.pen_start[:, :, 0:1], -BIG))
            step(dve.memset(K.pen_end[:, :, P - 1:P], -BIG))
            step(dve.tensor_tensor(K.pen_start[:, :, 1:P], dT[:, :, 1:P], dT[:, :, 0:P - 1], ALU.is_equal))
            step(penalty(K.pen_start[:, :, 1:P], K.pen_start[:, :, 1:P]))
            step(dve.tensor_copy(K.pen_end[:, :, 0:P - 1], K.pen_start[:, :, 1:P]))
            dve.wait_ge(rows_made, 1)
            step(dve.tensor_copy(rows[:, :, :, :].rearrange("h a c t -> h (a c t)"), ps_rows[:, :]))
            first = rows[:, 0, :, :].rearrange("h c t -> h (c t)")
            last_ = rows[:, 1, :, :].rearrange("h c t -> h (c t)")
            step(dve.memset(link[:, :, :], 0.0))
            step(dve.tensor_tensor(link[:, 0, 1:NTP], first[:, 1:NTP], last_[:, 0:NTP - 1], ALU.is_equal))
            step(dve.tensor_copy(link[:, 1, 0:NTP - 1], link[:, 0, 1:NTP]))
            step(dve.tensor_tensor(whole[:, :], first, last_, ALU.is_equal))
            for a in range(2):
                step(dve.tensor_tensor(K.pen_carry[:, a, :], whole[:, :], link[:, a, :], ALU.mult))
                step(penalty(K.pen_carry[:, a, :], K.pen_carry[:, a, :]))
            dve.engine_nop().then_inc(made, 1)
            dve.wait_ge(links_made, 1)
            own_tile(dve, K, step, linkT, ps_links, spread)
            for a, pen in ((0, K.pen_first), (1, K.pen_last)):
                e = ends[:, a, :].rearrange("p (c l) -> p c l", l=1).broadcast_to([P, NC, P])
                lk = linkT[:, a, :].rearrange("p (c l) -> p c l", l=1).broadcast_to([P, NC, P])
                step(dve.tensor_tensor(pen[:, :, :], dT[:, :, :], e, ALU.is_equal))
                step(dve.tensor_tensor(pen[:, :, :], pen[:, :, :], lk, ALU.mult))
                step(penalty(pen[:, :, :], pen[:, :, :]))


def node_weights(nc, K, l, A, ctx):
    K.Ws = ctx.enter_context(nc.sbuf_tensor(f"Ws{l}", [P, KC, DM], F32))
    K.Wd = ctx.enter_context(nc.sbuf_tensor(f"Wd{l}", [P, KC, DM], F32))
    K.node_weights_in = ctx.enter_context(stage_semaphore(nc, f"node_weights_in{l}"))

    def start(sp):
        for w, dram in ((K.Ws, "L0_gnn_Wsrc"), (K.Wd, "L0_gnn_Wdst")):
            sp.dma_start(w[:, :, :], A[dram][l].rearrange("(k p) n -> p k n", p=P)).then_inc(K.node_weights_in, 16)
    return start


def project(nc, K, l, A):
    with ExitStack() as ctx:
        def sem(n):
            return ctx.enter_context(stage_semaphore(nc, f"proj{l}_{n}"))

        def sb(n, shape, dt):
            return ctx.enter_context(nc.sbuf_tensor(f"proj{l}_{n}", shape, dt))
        rows_in, turned, hT_made, proj_made, out_made, table_out = (
            sem("rows_in"), sem("turned"), sem("hT_made"), sem("proj_made"), sem("out_made"), sem("table_out"))
        stepped = sem("stepped")
        Ws, Wd = K.Ws, K.Wd
        brow = sb("brow", [P, 2, DM], F32)
        arow = sb("arow", [P, DM], F32)
        hT = sb("hT", [P, 2, KC, P], F32)
        row = sb("row", [P, 2, 2, HW], F32)
        prod = sb("prod", [P, DM], F32)
        rest = sb("rest", [P, ROW], F32)
        psT = ctx.enter_context(nc.psum_tensor(f"proj{l}_psT", [P, 2, 512], F32))
        psP = [ctx.enter_context(nc.psum_tensor(f"proj{l}_psP{i}", [P, 2, 512], F32)) for i in range(2)]
        block = ctx.enter_context(nc.Block())

        @block.sync
        def _(sp):
            sp.dma_start(brow[:, 0, :], bcast(A["L0_gnn_bsrc"][l], P)).then_inc(rows_in, 16)
            sp.dma_start(brow[:, 1, :], bcast(A["L0_gnn_bdst"][l], P)).then_inc(rows_in, 16)
            sp.dma_start(arow[:, :], bcast(A["L0_gnn_attn"][l].rearrange("h d -> (h d)"), P)).then_inc(rows_in, 16)
            for t in range(NT):
                sp.wait_ge(out_made, 2 * t + 1)
                sp.dma_start(K.hs_tab[t * P:(t + 1) * P, :], row[:, 0, :, :].rearrange("p a n -> p (a n)"))\
                  .then_inc(table_out, 16)
            sp.wait_ge(table_out, 16 * NT)

        @block.tensor
        def _(pe):
            def turn(t):
                if t >= 1:
                    pe.wait_ge(hT_made, t)
                for k in range(KC):
                    last = pe.transpose(psT[:, k // 3, (k % 3) * P:(k % 3 + 1) * P],
                                        K.h[:, t, k * P:(k + 1) * P], K.ident[:, :])
                last.then_inc(turned, 1)
            turn(0)
            pe.wait_ge(K.node_weights_in, 32)
            for t in range(NT):
                pe.wait_ge(hT_made, t + 1)
                for s, W in ((0, Ws), (1, Wd)):
                    if t >= 1:
                        pe.wait_ge(out_made, 2 * (t - 1) + s + 1)
                    for n in range(2):
                        for k in range(KC):
                            last = pe.matmul(psP[s][:, n, 0:HALF], hT[:, t % 2, k, :],
                                             W[:, k, n * HALF:(n + 1) * HALF], start=(k == 0), stop=(k == KC - 1))
                    last.then_inc(proj_made, 1)
                    if s == 0 and t + 1 < NT:
                        turn(t + 1)

        @block.scalar
        def _(act):
            for t in range(NT):
                act.wait_ge(turned, t + 1)
                if t >= 2:
                    act.wait_ge(proj_made, 2 * (t - 1))
                for c in range(2):
                    last = act.activation(hT[:, t % 2, 3 * c:3 * c + 3, :].rearrange("p k n -> p (k n)"),
                                          psT[:, c, 0:3 * P], ACT.Copy)
                last.then_inc(hT_made, 1)

        @block.vector
        def _(dve):
            step = Chain(dve, stepped)
            dve.wait_ge(rows_in, 48)
            for t in range(NT):
                for s in range(2):
                    dve.wait_ge(proj_made, 2 * t + s + 1)
                    if s == 0 and t >= 1:
                        dve.wait_ge(table_out, 16 * t)
                    step(dve.tensor_tensor(row[:, s, :, 0:HALF], psP[s][:, :, 0:HALF],
                                           brow[:, s, :].rearrange("p (a n) -> p a n", a=2), ALU.add))
                    step(dve.tensor_tensor(prod[:, :].rearrange("p (a n) -> p a n", a=2), row[:, s, :, 0:HALF],
                                           arow[:, :].rearrange("p (a n) -> p a n", a=2), ALU.mult))
                    step(dve.tensor_reduce(rest[:, 0:H], prod[:, :].rearrange("p (h d) -> p h d", h=H), AX.X, ALU.add))
                    if s == 0:
                        dve.tensor_scalar(row[:, s, :, HALF:HW], rest[:, 0:H].rearrange("p (a h) -> p a h", a=2),
                                          (1 + SLOPE) / 2, None, ALU.mult).then_inc(out_made, 1)
                        continue
                    step(dve.tensor_scalar(row[:, s, :, HALF:HW], rest[:, 0:H].rearrange("p (a h) -> p a h", a=2),
                                           (1 + SLOPE) / 2, None, ALU.mult))
                    full = row[:, 1, :, :].rearrange("p a n -> p (a n)")
                    step(dve.tensor_copy(K.hdp[:, t, 0, :], full))
                    step(dve.tensor_tensor(rest[:, :], full, K.hdp[:, t, 0, :], ALU.subtract))
                    step(dve.tensor_copy(K.hdp[:, t, 1, :], rest[:, :]))
                    step(dve.tensor_tensor(rest[:, :], rest[:, :], K.hdp[:, t, 1, :], ALU.subtract))
                    dve.tensor_copy(K.hdp[:, t, 2, :], rest[:, :]).then_inc(out_made, 1)


def ring_loop(eng, R, first, step):
    turns = (NG - first) // R
    with eng.Fori(0, turns) as i:
        for u in range(R):
            step(R * i + first + u, (first + u) % R, i + (first + u) // R)
    for n in range(first + R * turns, NG):
        step(n, n % R, n // R)


class Gatherer:

    def __init__(self, pool, K, R, ix, hse, gathered, index_set, slot_free):
        self.R = R
        self.pool, self.K, self.ix, self.hse = pool, K, ix, hse
        self.gathered, self.index_set, self.slot_free = gathered, index_set, slot_free

    def index(self, n, k):
        for j in range(2):
            self.pool.tensor_copy(self.ix[k][j][:, :], self.K.srccol[:, bass.ds(2 * n + j, 1)])\
                .then_inc(self.index_set, 1)

    def gather(self, n, k):
        self.pool.wait_ge(self.index_set, 2 * n + 2)
        self.pool.nop(nofuse=True)
        for j in range(2):
            self.pool.indirect_dma_start(self.hse[:, k, j, :], None, self.K.hs_tab,
                                         bass.IndirectOffsetOnAxis(ap=self.ix[k][j][:, :], axis=0))\
                .then_inc(self.gathered[k][j], 16)

    def step(self, n, k):
        self.gather(n, k)
        self.slot_free(n + 1)
        self.index(n + 1, (k + 1) % self.R)


def edge_logits(nc, K, l, A):
    R = RING_LOGITS
    AHEAD = 2
    SLOTS_1H = 3
    CREDIT = R
    with ExitStack() as ctx:
        def sem(n):
            return ctx.enter_context(stage_semaphore(nc, f"lg{l}_{n}"))

        def sb(n, shape, dt):
            return ctx.enter_context(nc.sbuf_tensor(f"lg{l}_{n}", shape, dt))
        row_in = [sem(f"row_in{k}") for k in range(R)]
        gathered = [[sem(f"gathered{k}{j}") for j in range(2)] for k in range(R)]
        t_made = [sem(f"t_made{j}") for j in range(2)]
        attn_in, attn_made, index_set, onehot_made, summed, abs_made, abs2_made, weighed, reduced, summed_up, logit_made = (
            sem("attn_in"), sem("attn_made"), sem("index_set"), sem("onehot_made"), sem("summed"), sem("abs_made"),
            sem("abs2_made"), sem("weighed"), sem("reduced"), sem("summed_up"), sem("logit_made"))
        dstrow = sb("dstrow", [P, 3, GE], I32)
        ix = [[sb(f"ix{k}{j}", [P, 1], I32) for j in range(2)] for k in range(R)]
        hse = sb("hse", [P, R, 2, ROW], F32)
        tt = sb("tt", [P, R, 2, 2, HW], F32)
        part = sb("part", [P, R, 2 * H], F32)
        arow = sb("arow", [P, 2, HALF], F32)
        ohT = sb("ohT", [P, SLOTS_1H, GE], BF16)
        far = sb("far", [P, GE], F32)
        distance_made = sem("distance_made")
        ps = [[ctx.enter_context(nc.psum_tensor(f"lg{l}_ps{k}{j}", [P, 2, 512], F32)) for j in range(2)]
              for k in range(2)]
        block = ctx.enter_context(nc.Block())

        @block.sync
        def _(sp):
            sp.dma_start(arow[:, :, :].rearrange("p a n -> p (a n)"),
                         bcast(A["L0_gnn_attn"][l].rearrange("h d -> (h d)"), P)).then_inc(attn_in, 16)

            def step(n, k, it):
                off = sp.value_load(K.off_i[0:1, bass.ds(n, 1)], min_val=0, max_val=E)
                sp.wait_ge(onehot_made, n - 2 + CREDIT)
                sp.nop(nofuse=True)
                sp.dma_start(dstrow[:, k % 3, :], K.srt_dst[0:1, bass.ds(off, GE)].broadcast_to([P, GE]))\
                  .then_inc(row_in[k], 16)
            ring_loop(sp, R, 0, step)

        @block.gpsimd
        def _(pool):
            def slot_free(n):
                pool.wait_ge(summed, n - R + 1 + CREDIT)
                pool.nop(nofuse=True)
                pool.wait_ge(t_made[1], n - R + 1 + CREDIT)
                pool.nop(nofuse=True)

            g = Gatherer(pool, K, R, ix, hse, gathered, index_set, slot_free)

            def logit(n, k):
                for s in (reduced, summed_up):
                    pool.wait_ge(s, n + 1 + CREDIT)
                    pool.nop(nofuse=True)
                pool.tensor_tensor(K.lg[:, bass.ds(n, 1), :].rearrange("p g (a h) -> p (g a) h", a=4),
                                   part[:, k, :].rearrange("p (a h) -> p a h", a=4),
                                   tt[:, k, :, :, HALF:HW].rearrange("p j a n -> p (j a) n"), ALU.add)\
                    .then_inc(logit_made, 1)

            def step(n, k, it):
                g.step(n - 1, (k - 1) % R)
                logit(n - LAG, (k - LAG) % R)
            g.slot_free(0)
            g.index(0, 0)
            for n in range(LAG - 1):
                g.step(n, n)
            ring_loop(pool, R, LAG, step)
            g.gather(NG - 1, (NG - 1) % R)
            for n in range(NG - LAG, NG):
                logit(n, n % R)

        @block.tensor
        def _(pe):
            def step(n, k, it):
                q = k % 2
                b = pe.value_load(K.blk_i[0:1, bass.ds(n, 1)], min_val=0, max_val=NT - 1)
                pe.wait_ge(onehot_made, n + 1 + CREDIT)
                pe.nop(nofuse=True)
                for j in range(2):
                    if j == 0:
                        pe.wait_ge(summed, n - 1 + CREDIT)
                        pe.nop(nofuse=True)
                    else:
                        pe.wait_ge(abs2_made, n - 1 + CREDIT)
                        pe.nop(nofuse=True)
                        pe.wait_ge(gathered[k][1], 16 * it + 16)
                        pe.nop(nofuse=True)
                    for a in range(2):
                        for part_ in range(3):
                            last = pe.matmul(ps[q][j][:, a, 0:HW], ohT[:, k % SLOTS_1H, j * P:(j + 1) * P],
                                             K.hdp[:, bass.ds(b, 1), part_, a * HW:(a + 1) * HW],
                                             start=(part_ == 0), stop=(part_ == 2 and j == 0))
                        if j == 1:
                            last = pe.matmul(ps[q][j][:, a, 0:HW], K.ident[:, :], hse[:, k, j, a * HW:(a + 1) * HW],
                                             start=False, stop=True)
                    last.then_inc(t_made[j], 1)
            ring_loop(pe, R, 0, step)

        @block.scalar
        def _(act):
            def step(n, k, it):
                act.wait_ge(summed, n + 1 + CREDIT)
                act.nop(nofuse=True)
                act.activation(tt[:, k, 0, :, 0:HALF], tt[:, k, 0, :, 0:HALF], ACT.Abs).then_inc(abs_made, 1)
                act.wait_ge(t_made[1], n + 1 + CREDIT)
                act.nop(nofuse=True)
                act.wait_ge(logit_made, n - R + 1 + CREDIT)
                act.nop(nofuse=True)
                act.activation(tt[:, k, 1, :, HALF:HW], ps[k % 2][1][:, :, HALF:HW], ACT.Copy)
                act.activation(tt[:, k, 1, :, 0:HALF], ps[k % 2][1][:, :, 0:HALF], ACT.Abs).then_inc(abs2_made, 1)

            def sum_up(n, k):
                act.wait_ge(weighed, n + 1 + CREDIT)
                act.nop(nofuse=True)
                for h in range(HH):
                    half = tt[:, k, 1, 0, h * HD:(h + 1) * HD]
                    last = act.activation(half, half, ACT.Copy, accum_out=part[:, k, H + h:H + h + 1])
                last.then_inc(summed_up, 1)

            def distance(n, k, it):
                act.wait_ge(row_in[k], 16 * it + 16)
                act.nop(nofuse=True)
                act.wait_ge(onehot_made, n + CREDIT)
                act.nop(nofuse=True)
                act.activation(far[:, :], dstrow[:, k % 3, :], ACT.Abs, scale=-1.0,
                               bias=K.blkiota[:, bass.ds(n, 1)]).then_inc(distance_made, 1)

            def onehot(n, k):
                act.wait_ge(distance_made, n + 1)
                act.nop(nofuse=True)
                act.wait_ge(t_made[1], n - SLOTS_1H + 1 + CREDIT)
                act.nop(nofuse=True)
                act.activation(ohT[:, k % SLOTS_1H, :], far[:, :], ACT.Relu, scale=-1.0, bias=K.ones[:, 0:1])\
                   .then_inc(onehot_made, 1)

            def all_(n, k, it):
                distance(n, k, it)
                step(n - AHEAD, (k - AHEAD) % R, it - (1 if k < AHEAD else 0))
                onehot(n, k)
                sum_up(n - AHEAD - 1, (k - AHEAD - 1) % R)
            for n in range(AHEAD + 1):
                distance(n, n, 0)
                if n == AHEAD:
                    step(0, 0, 0)
                onehot(n, n)
            ring_loop(act, R, AHEAD + 1, all_)
            for n in range(NG - AHEAD, NG):
                step(n, n % R, n // R)
                sum_up(n - 1, (n - 1) % R)
            sum_up(NG - 1, (NG - 1) % R)

        @block.vector
        def _(dve):
            for s in (onehot_made, summed, t_made[0], t_made[1], abs2_made, weighed, reduced, summed_up, logit_made):
                dve.sem_inc(s, CREDIT)
            dve.wait_ge(attn_in, 16)
            dve.tensor_scalar(arow[:, :, :], arow[:, :, :], (1 - SLOPE) / 2, None, ALU.mult).then_inc(attn_made, 1)
            dve.wait_ge(attn_made, 1)

            def add(n, k, it):
                dve.wait_ge(gathered[k][0], 16 * it + 16)
                dve.nop(nofuse=True)
                dve.wait_ge(t_made[0], n + 1 + CREDIT)
                dve.nop(nofuse=True)
                dve.wait_ge(logit_made, n - R + 1 + CREDIT)
                dve.nop(nofuse=True)
                dve.tensor_tensor(tt[:, k, 0, :, :], ps[k % 2][0][:, :, 0:HW],
                                  hse[:, k, 0, :].rearrange("p (a n) -> p a n", a=2), ALU.add).then_inc(summed, 1)

            def weigh(n, k):
                dve.wait_ge(abs_made, n + 1)
                dve.nop(nofuse=True)
                dve.wait_ge(abs2_made, n + 1 + CREDIT)
                dve.nop(nofuse=True)
                t4 = tt[:, k, :, :, :].rearrange("p j a n -> p (j a) n")
                dve.tensor_tensor(t4[:, 2, 0:HALF], t4[:, 2, 0:HALF], arow[:, 0, :], ALU.mult).then_inc(weighed, 1)
                for x in (*range(H), *range(H + HH, 2 * H)):
                    cols = slice(x % HH * HD, (x % HH + 1) * HD)
                    last = dve.tensor_tensor_reduce(out=t4[:, x // HH, cols], in0=t4[:, x // HH, cols],
                                                    in1=arow[:, x // HH % 2, cols], scale=1.0, scalar=0.0,
                                                    op0=ALU.mult, op1=ALU.add, accum_out=part[:, k, x:x + 1])
                last.then_inc(reduced, 1)

            def step(n, k, it):
                add(n, k, it)
                weigh(n - 1, (k - 1) % R)
            add(0, 0, 0)
            ring_loop(dve, R, 1, step)
            weigh(NG - 1, (NG - 1) % R)


def segment_softmax(nc, K, l):
    with ExitStack() as ctx:
        def sem(n):
            return ctx.enter_context(stage_semaphore(nc, f"sm{l}_{n}"))

        def sb(n, shape, dt):
            return ctx.enter_context(nc.sbuf_tensor(f"sm{l}_{n}", shape, dt))
        stepped, pads_set, turned, made, rows_made, carries_made, back = (
            sem("stepped"), sem("pads_set"), sem("turned"), sem("made"), sem("rows_made"), sem("carries_made"),
            sem("back"))
        zeroed = sem("zeroed")
        spread = sb("spread", [P, 2 * NC, TPC], F32)
        ps_rows = ctx.enter_context(nc.psum_tensor(f"sm{l}_ps_rows", [H, 2 * NTP], F32))
        ps_carry = ctx.enter_context(nc.psum_tensor(f"sm{l}_ps_carry", [P, 2 * NTP], F32))
        lgT = sb("lgT", [P, NC, P], F32)
        fw = sb("fw", [P, NC, P], F32)
        bw = sb("bw", [P, NC, P], F32)
        ends = sb("ends", [P, 2, NC], F32)
        rows = sb("rows", [H, 2, NC * TPC], F32)
        run = sb("run", [H, 2, NC * TPC], F32)
        carry = sb("carry", [H, 2, NC * TPC], F32)
        carryT = sb("carryT", [P, 2, NC], F32)
        ps = [ctx.enter_context(nc.psum_tensor(f"sm{l}_ps{i}", [P, 512], F32)) for i in range(3)]
        block = ctx.enter_context(nc.Block())
        lg3 = K.lg[:, :, :].rearrange("p g x -> p (g x)")

        @block.gpsimd
        def _(pool):
            pool.memset(K.acc[:, :, :], 0.0).then_inc(zeroed, 1)
            pool.wait_ge(zeroed, 1)

        @block.tensor
        def _(pe):
            pe.wait_ge(pads_set, 1)
            for c in range(NC):
                last = pe.transpose(ps[c // 4][:, (c % 4) * P:(c % 4 + 1) * P], lg3[:, c * P:(c + 1) * P],
                                    K.ident[:, :])
            last.then_inc(turned, 1)
            pe.wait_ge(made, 1)
            pe.matmul(ps_rows[:, :], K.sel_head[:, :], spread[:, :, :].rearrange("p a t -> p (a t)"), start=True,
                      stop=True).then_inc(rows_made, 1)
            pe.wait_ge(made, 2)
            pe.matmul(ps_carry[:, :], K.sel_headT[:, :], carry[:, :, :].rearrange("h a n -> h (a n)"), start=True,
                      stop=True).then_inc(carries_made, 1)
            pe.wait_ge(made, 3)
            for c in range(NC):
                last = pe.transpose(ps[c // 4][:, (c % 4) * P:(c % 4 + 1) * P], lgT[:, c, :], K.ident[:, :])
            last.then_inc(turned, 1)

        @block.vector
        def _(dve):
            step = Chain(dve, stepped)
            dve.memset(lg3[:, NTILE * H:NTP * H], 0.0).then_inc(pads_set, 1)
            dve.wait_ge(turned, 1)
            for i in range(3):
                last = dve.tensor_copy(lgT[:, 4 * i:4 * i + 4, :].rearrange("p c l -> p (c l)"), ps[i][:, :])
            step(last)

            def flat(x):
                return x[:, :, :].rearrange("p c l -> p (c l)")
            step(dve.tensor_tensor_scan(flat(fw), flat(K.pen_start), flat(lgT), -BIG, ALU.add, ALU.max))
            step(dve.tensor_tensor_scan(flat(bw)[:, ::-1], flat(K.pen_end)[:, ::-1], flat(lgT)[:, ::-1], -BIG,
                                        ALU.add, ALU.max))
            step(dve.tensor_copy(ends[:, 0, :], fw[:, :, P - 1]))
            step(dve.tensor_copy(ends[:, 1, :], bw[:, :, 0]))
            spread_ends(dve, K, spread, ends).then_inc(made, 1)
            step(dve.tensor_tensor(flat(fw), flat(fw), flat(bw), ALU.max))
            dve.wait_ge(rows_made, 1)
            step(dve.tensor_copy(rows[:, :, :].rearrange("h a n -> h (a n)"), ps_rows[:, :]))
            step(dve.memset(carry[:, :, :], -BIG))
            step(dve.tensor_tensor_scan(run[:, 0, :], K.pen_carry[:, 0, :], rows[:, 0, :], -BIG, ALU.add, ALU.max))
            step(dve.tensor_tensor_scan(run[:, 1, ::-1], K.pen_carry[:, 1, ::-1], rows[:, 1, ::-1], -BIG,
                                        ALU.add, ALU.max))
            step(dve.tensor_copy(carry[:, 0, 1:NTP], run[:, 0, 0:NTP - 1]))
            dve.tensor_copy(carry[:, 1, 0:NTP - 1], run[:, 1, 1:NTP]).then_inc(made, 1)
            dve.wait_ge(carries_made, 1)
            own_tile(dve, K, step, carryT, ps_carry, spread)
            for a, pen in ((0, K.pen_first), (1, K.pen_last)):
                cb = carryT[:, a, :].rearrange("p (c l) -> p c l", l=1).broadcast_to([P, NC, P])
                step(dve.tensor_tensor(bw[:, :, :], pen[:, :, :], cb, ALU.add))
                step(dve.tensor_tensor(fw[:, :, :], fw[:, :, :], bw[:, :, :], ALU.max))
            dve.tensor_tensor(bw[:, :, :], lgT[:, :, :], fw[:, :, :], ALU.subtract).then_inc(back, 1)
            dve.wait_ge(turned, 2)
            for i in range(3):
                last = dve.tensor_copy(lg3[:, i * 512:(i + 1) * 512], ps[i][:, :])
            step(last)

        @block.scalar
        def _(act):
            act.wait_ge(back, 1)
            act.activation(lgT[:, :, :].rearrange("p c l -> p (c l)"), bw[:, :, :].rearrange("p c l -> p (c l)"),
                           ACT.Exp).then_inc(made, 1)


def aggregate(nc, K, l):
    R = RING_SUMS
    CREDIT = R
    with ExitStack() as ctx:
        def sem(n):
            return ctx.enter_context(stage_semaphore(nc, f"ag{l}_{n}"))

        def sb(n, shape, dt):
            return ctx.enter_context(nc.sbuf_tensor(f"ag{l}_{n}", shape, dt))
        gathered = [[sem(f"gathered{k}{j}") for j in range(2)] for k in range(R)]
        message_made = [sem(f"message_made{j}") for j in range(2)]
        index_set, summed, added = sem("index_set"), sem("summed"), sem("added")
        ix = [[sb(f"ix{k}{j}", [P, 1], I32) for j in range(2)] for k in range(R)]
        hse = sb("hse", [P, R, 2, ROW], F32)
        msg = sb("msg", [P, R, 2, ROW], F32)
        oh = sb("oh", [P, R, 2, P], F32)
        ps = [ctx.enter_context(nc.psum_tensor(f"ag{l}_ps{k}", [P, 2, 512], F32)) for k in range(R)]
        block = ctx.enter_context(nc.Block())

        @block.gpsimd
        def _(pool):
            def slot_free(n):
                for j in range(2):
                    pool.wait_ge(message_made[j], n - R + 1 + CREDIT)
                    pool.nop(nofuse=True)
            g = Gatherer(pool, K, R, ix, hse, gathered, index_set, slot_free)
            slot_free(0)
            g.index(0, 0)
            ring_loop(pool, R, 1, lambda n, k, it: g.step(n - 1, (k - 1) % R))
            g.gather(NG - 1, (NG - 1) % R)

        @block.tensor
        def _(pe):
            def step(n, k, it):
                pe.wait_ge(message_made[0], n + 1 + CREDIT)
                pe.nop(nofuse=True)
                pe.wait_ge(message_made[1], n + 1 + CREDIT)
                pe.nop(nofuse=True)
                pe.wait_ge(added, n - R + 1 + CREDIT)
                pe.nop(nofuse=True)
                for a in range(2):
                    for j in range(2):
                        last = pe.matmul(ps[k][:, a, 0:HW], oh[:, k, j, :], msg[:, k, j, a * HW:(a + 1) * HW],
                                         start=(j == 0), stop=(j == 1))
                last.then_inc(summed, 1)
            ring_loop(pe, R, 0, step)

        @block.scalar
        def _(act):
            def step(n, k, it):
                act.wait_ge(gathered[k][1], 16 * it + 16)
                act.nop(nofuse=True)
                act.wait_ge(summed, n - R + 1 + CREDIT)
                act.nop(nofuse=True)
                for h in range(H):
                    at = h // HH * HW + h % HH * HD
                    last = act.activation(msg[:, k, 1, at:at + HD], hse[:, k, 1, at:at + HD], ACT.Copy,
                                          scale=K.lg[:, bass.ds(n, 1), H + h:H + h + 1].rearrange("p g x -> p (g x)"))
                last.then_inc(message_made[1], 1)
            ring_loop(act, R, 0, step)

        @block.vector
        def _(dve):
            for s in (message_made[0], message_made[1], added, summed):
                dve.sem_inc(s, CREDIT)

            def message(n, k, it):
                dve.wait_ge(summed, n - R + 1 + CREDIT)
                dve.nop(nofuse=True)
                for j in range(2):
                    dve.tensor_scalar(oh[:, k, j, :], K.iota_free[:, :], K.drel[:, bass.ds(2 * n + j, 1)], None,
                                      ALU.is_equal)
                m4 = msg[:, k, :, :].rearrange("p j (a n) -> p (j a) n", a=2)
                dve.tensor_copy(m4[:, :, HALF:HW], K.lg[:, bass.ds(n, 1), :].rearrange("p g (a h) -> p (g a) h", a=4))
                dve.wait_ge(gathered[k][0], 16 * it + 16)
                dve.nop(nofuse=True)
                h4 = hse[:, k, 0, :].rearrange("p (a n) -> p a n", a=2)
                for a in range(2):
                    exh = K.lg[:, bass.ds(n, 1), a * HH:(a + 1) * HH]\
                        .rearrange("p g (h d) -> p (g h) d", d=1).broadcast_to([P, HH, HD])
                    last = dve.tensor_tensor(m4[:, a, 0:HALF].rearrange("p (h d) -> p h d", d=HD),
                                             h4[:, a, 0:HALF].rearrange("p (h d) -> p h d", d=HD), exh, ALU.mult)
                last.then_inc(message_made[0], 1)

            def add(n, k):
                b = dve.value_load(K.blk_i[0:1, bass.ds(n, 1)], min_val=0, max_val=NT - 1)
                dve.wait_ge(added, n + CREDIT)
                dve.nop(nofuse=True)
                dve.wait_ge(summed, n + 1 + CREDIT)
                dve.nop(nofuse=True)
                a = K.acc[:, bass.ds(b, 1), :].rearrange("p b (a n) -> p (b a) n", a=2)
                dve.tensor_tensor(a, a, ps[k][:, :, 0:HW], ALU.add).then_inc(added, 1)

            def step(n, k, it):
                message(n, k, it)
                add(n - 2, (k - 2) % R)
            message(0, 0, 0)
            message(1, 1, 0)
            ring_loop(dve, R, 2, step)
            add(NG - 2, (NG - 2) % R)
            add(NG - 1, (NG - 1) % R)


def node_update(nc, K, l, A):
    with ExitStack() as ctx:
        def sem(n):
            return ctx.enter_context(stage_semaphore(nc, f"up{l}_{n}"))

        def sb(n, shape, dt):
            return ctx.enter_context(nc.sbuf_tensor(f"up{l}_{n}", shape, dt))
        stepped, low_made, exp_made, rows_in = sem("stepped"), sem("low_made"), sem("exp_made"), sem("rows_in")
        out_made, tile_done = sem("out_made"), sem("tile_done")
        rs = sb("rs", [P, NT, H], F32)
        o = sb("o", [P, 2, DM], F32)
        m = sb("m", [P, 2, DM], F32)
        block = ctx.enter_context(nc.Block())

        @block.sync
        def _(sp):
            sp.dma_start(K.lnw[:, :], bcast(A["L0_gnn_ln_w"][l], P)).then_inc(rows_in, 16)
            sp.dma_start(K.lnb[:, :], bcast(A["L0_gnn_ln_b"][l], P)).then_inc(rows_in, 16)
            if l == L - 1:
                sp.dma_start(K.onw[:, :], bcast(A["L0_gnn_on_w"], P)).then_inc(rows_in, 16)
                sp.dma_start(K.onb[:, :], bcast(A["L0_gnn_on_b"], P)).then_inc(rows_in, 16)
            sp.wait_ge(rows_in, 64 if l == L - 1 else 32)

        @block.vector
        def _(dve):
            step = Chain(dve, stepped)
            acc4 = K.acc[:, :, :].rearrange("p t (a n) -> p t a n", a=2)
            for a in range(2):
                step(dve.tensor_scalar(rs[:, :, a * HH:(a + 1) * HH], acc4[:, :, a, HALF:HW], 1e-30, None, ALU.max))
            step(dve.reciprocal(rs[:, :, :], rs[:, :, :]))

            def first(t):
                for a in range(2):
                    r = rs[:, t, a * HH:(a + 1) * HH].rearrange("p (h d) -> p h d", d=1).broadcast_to([P, HH, HD])
                    last = dve.tensor_tensor(o[:, t % 2, a * HALF:(a + 1) * HALF].rearrange("p (h d) -> p h d", d=HD),
                                             acc4[:, t, a, 0:HALF].rearrange("p (h d) -> p h d", d=HD), r, ALU.mult)
                last.then_inc(out_made, 1)

            def second(t):
                dve.wait_ge(exp_made, t + 1)
                dve.scalar_tensor_tensor(out=o[:, t % 2, :], in0=o[:, t % 2, :], scalar=0.0, in1=m[:, t % 2, :],
                                         op0=ALU.max, op1=ALU.add).then_inc(tile_done, 1)
                dve.wait_ge(tile_done, t + 1)
                step(dve.scalar_tensor_tensor(out=K.h[:, t, :], in0=o[:, t % 2, :], scalar=-1.0, in1=K.h[:, t, :],
                                              op0=ALU.add, op1=ALU.add))
            first(0)
            for t in range(NT):
                if t + 1 < NT:
                    first(t + 1)
                second(t)

        @block.scalar
        def _(act):
            for t in range(NT):
                act.wait_ge(out_made, t + 1)
                if t >= 2:
                    act.wait_ge(tile_done, t - 1)
                act.activation(m[:, t % 2, :], o[:, t % 2, :], ACT.Relu, scale=-1.0).then_inc(low_made, 1)
                act.wait_ge(low_made, t + 1)
                act.activation(m[:, t % 2, :], m[:, t % 2, :], ACT.Exp, scale=-1.0).then_inc(exp_made, 1)


class Keep:
    pass


def gnn(nc, K, A):
    with ExitStack() as ctx:
        def sb(n, shape, dt):
            return ctx.enter_context(nc.sbuf_tensor(n, shape, dt))
        K.hdp = sb("hd_parts", [P, NT, 3, ROW], BF16)
        K.lg = sb("logits", [P, NTP // 2, 2 * H], F32)
        K.srccol = sb("src_columns", [P, NTILE], I32)
        K.drel = sb("dst_in_block", [P, NTILE], F32)
        K.off_i = sb("group_offset", [P, NG], I32)
        K.blk_i = sb("group_block", [P, NG], I32)
        K.blkiota = sb("block_members", [P, NG], F32)
        K.pen_start = sb("pen_start", [P, NC, P], F32)
        K.pen_end = sb("pen_end", [P, NC, P], F32)
        K.pen_first = sb("pen_first", [P, NC, P], F32)
        K.pen_last = sb("pen_last", [P, NC, P], F32)
        K.pen_carry = sb("pen_carry", [H, 2, NTP], F32)
        with ExitStack() as cw:
            start = node_weights(nc, K, 0, A, cw)
            with ExitStack() as c2:
                K.dcolf = c2.enter_context(nc.sbuf_tensor("dst_columns", [P, NTP], F32))
                K.dall = c2.enter_context(nc.sbuf_tensor("dst_all", [EL, EC], I32))
                K.sall = c2.enter_context(nc.sbuf_tensor("src_all", [EL, EC], I32))
                K.dallf = c2.enter_context(nc.sbuf_tensor("dst_all_f", [EL, EC], F32))
                order_edges(nc, K, A["src"], A["dst"])
                edge_tables(nc, K, start)
                segment_tables(nc, K)
            project(nc, K, 0, A)
        for l in range(L):
            edge_logits(nc, K, l, A)
            with ExitStack() as c2:
                K.acc = c2.enter_context(nc.sbuf_tensor(f"acc{l}", [P, NT, ROW], F32))
                segment_softmax(nc, K, l)
                aggregate(nc, K, l)
                node_update(nc, K, l, A)
            if l < L - 1:
                recycle(nc)
                with ExitStack() as cw:
                    start = node_weights(nc, K, l + 1, A, cw)
                    norm_block(nc, K, f"ln{l}", K.h, K.h, K.lnw, K.lnb, ahead=start)
                    project(nc, K, l + 1, A)


NE = 16
NGRP = 8
PER = NE // NGRP
TOPG = 4
TOPE = 4
SCALE = 2.5
HID = 512
KH = HID // P
TM = (N * TOPE + NE * (P - 1)) // P
TM -= 0 if TM % 2 == 0 else -1
BW = 2 * HID + DM
LOADS = 4 * 16
SLOTS = 3
SURE = (N * TOPE + P - 1) // P // 2


def first_loads(nc, K, A, x_in):
    with ExitStack() as ctx:
        def sem(n):
            return ctx.enter_context(stage_semaphore(nc, f"bias_{n}"))

        def sb(n, shape, dt):
            return ctx.enter_context(nc.sbuf_tensor(f"bias_{n}", shape, dt))
        rows_in, stepped, parts_made, parts_out = sem("rows_in"), sem("stepped"), sem("parts_made"), sem("parts_out")
        nodes_in, last_zeroed = sem("nodes_in"), sem("last_zeroed")
        full = sb("full", [NE + 1, BW], F32)
        parts = sb("parts", [NE + 1, 3, BW], BF16)
        block = ctx.enter_context(nc.Block())

        @block.sync
        def _(sp):
            for name, at, w in (("bu", 0, HID), ("bg", HID, HID), ("bd", 2 * HID, DM)):
                sp.dma_start(full[0:NE, at:at + w], A["L0_ffn_" + name]).then_inc(rows_in, 16)
                sp.dma_start(full[NE:NE + 1, at:at + w], A["L0_ffn_s" + name].rearrange("(a n) -> a n", a=1))\
                  .then_inc(rows_in, 16)
            load_x(sp, A, x_in, last_zeroed, nodes_in)
            sp.wait_ge(parts_made, 1)
            sp.dma_start(K.bias_tab, parts[:, :, :]).then_inc(parts_out, 16)
            sp.wait_ge(parts_out, 16)
            sp.wait_ge(nodes_in, 32)

        @block.vector
        def _(dve):
            dve.memset(x_in[:, NT - 1, :], 0.0).then_inc(last_zeroed, 1)
            step = Chain(dve, stepped)
            dve.wait_ge(rows_in, 96)
            step(dve.tensor_copy(parts[:, 0, :], full[:, :]))
            step(dve.tensor_tensor(full[:, :], full[:, :], parts[:, 0, :], ALU.subtract))
            step(dve.tensor_copy(parts[:, 1, :], full[:, :]))
            step(dve.tensor_tensor(full[:, :], full[:, :], parts[:, 1, :], ALU.subtract))
            dve.tensor_copy(parts[:, 2, :], full[:, :]).then_inc(parts_made, 1)


def route(nc, K, A):
    with ExitStack() as ctx:
        def sem(n):
            return ctx.enter_context(stage_semaphore(nc, f"route_{n}"))

        def sb(n, shape, dt):
            return ctx.enter_context(nc.sbuf_tensor(f"route_{n}", shape, dt))
        weights_in, rows_out, turned, xT_made, logits_made, exp_ready, exp_made = (
            sem("weights_in"), sem("rows_out"), sem("turned"), sem("xT_made"), sem("logits_made"), sem("exp_ready"),
            sem("exp_made"))
        stepped, iotas, chosen, counted, zeroed = sem("stepped"), sem("iotas"), sem("chosen"), sem("counted"), sem("zeroed")
        gw = sb("gw", [P, KC, NE], F32)
        rows = sb("rows", [P, 2, NE], F32)
        xT = sb("xT", [P, 2, KC, P], F32)
        lo = sb("lo", [P, NT, NE], F32)
        s = sb("s", [P, NT, NE], F32)
        sc, sel, c1, c2, pos, tot, tok, it = K.sc, K.sel, K.c1, K.c2, K.pos, K.tot, K.tok, K.it
        mx = sb("mx", [P, NT], F32)
        g = sb("g", [P, NT, NGRP], F32)
        cmp_ = K.Wu[:, 2, 0:NT * NE * NE // HID, :].rearrange("p k (u i j) -> p (k u) i j", i=NE, j=NE)
        eq = K.Wu[:, 1, 0:NT * NE * NE // HID, :].rearrange("p k (u i j) -> p (k u) i j", i=NE, j=NE)
        zrow = K.Wd[:, 1, 0:1, :]
        rank = sb("rank", [P, NT, NE], F32)
        tri = sb("tri", [P, NE, NE], F32)
        tri8 = sb("tri8", [P, NGRP, NGRP], F32)
        upper = sb("upper", [P, P], F32)
        valid = sb("valid", [P, NT], F32)
        none = sb("none", [P, TM], I32)
        psT = [ctx.enter_context(nc.psum_tensor(f"route_psT{i}", [P, 2, 512], F32)) for i in range(2)]
        psL = ctx.enter_context(nc.psum_tensor("route_psL", [P, NT * NE], F32))
        psC = [ctx.enter_context(nc.psum_tensor(f"route_psC{i}", [P, NT * NE], F32)) for i in range(2)]
        block = ctx.enter_context(nc.Block())

        @block.sync
        def _(sp):
            sp.dma_start(gw[:, :, :], A["L0_ffn_gate_w"].rearrange("(k p) n -> p k n", p=P)).then_inc(weights_in, 16)
            sp.dma_start(rows[:, 0, :], bcast(A["L0_ffn_gate_b"], P)).then_inc(weights_in, 16)
            sp.dma_start(rows[:, 1, :], bcast(A["L0_ffn_bias"], P)).then_inc(weights_in, 16)
            sp.dma_start(K.xn_tab.rearrange("(t p) d -> p t d", p=P), K.xn[:, :, :]).then_inc(rows_out, 16)
            for w, dram in ((K.Wu, "sWu"), (K.Wg, "sWg"), (K.Wd, "sWd")):
                sp.dma_start(w[:, 0, :, :], A["L0_ffn_" + dram].rearrange("(k p) n -> p k n", p=P))\
                  .then_inc(K.shared_in, 16)
            sp.dma_start(K.br[:, 0, :], K.bias_tab[NE]).then_inc(K.shared_in, 16)
            sp.wait_ge(zeroed, 2)
            sp.dma_start(K.pair_tab.rearrange("(p k) a -> p (k a)", p=P), none[:, :]).then_inc(rows_out, 16)
            sp.dma_start(K.pair_y[2 * SURE * P:, :].rearrange("(t p) d -> p t d", p=P),
                         zrow[:, :, :].broadcast_to([P, TM - 2 * SURE, DM])).then_inc(rows_out, 16)
            sp.wait_ge(rows_out, 48)

        @block.gpsimd
        def _(pool):
            pool.memset(none[:, :], 0).then_inc(zeroed, 1)
            pool.memset(zrow[:, :, :], 0.0).then_inc(zeroed, 1)
            pool.memset(upper[:, :], 1.0).then_inc(iotas, 1)
            pool.memset(tri[:, :, :], 1.0).then_inc(iotas, 1)
            pool.memset(tri8[:, :, :], 1.0).then_inc(iotas, 1)
            pool.wait_ge(iotas, 3)
            pool.affine_select(out=upper[:, :], in_=upper[:, :], compare_op=ALU.is_gt, fill=0.0, base=0,
                               pattern=[[1, P]], channel_multiplier=-1).then_inc(iotas, 1)
            pool.affine_select(out=tri[:, :, :], in_=tri[:, :, :], compare_op=ALU.is_gt, fill=0.0, base=0,
                               pattern=[[1, NE], [-1, NE]], channel_multiplier=0).then_inc(iotas, 1)
            pool.affine_select(out=tri8[:, :, :], in_=tri8[:, :, :], compare_op=ALU.is_gt, fill=0.0, base=0,
                               pattern=[[1, NGRP], [-1, NGRP]], channel_multiplier=0).then_inc(iotas, 1)
            pool.iota(tok[:, :], [[P, NT]], base=0, channel_multiplier=1,
                      allow_small_or_imprecise_dtypes=True).then_inc(iotas, 1)
            pool.iota(it[:, :], [[1, TM]], base=0, channel_multiplier=0,
                      allow_small_or_imprecise_dtypes=True).then_inc(iotas, 1)

        @block.tensor
        def _(pe):
            pe.wait_ge(weights_in, 48)
            def turn(t):
                if t >= 2:
                    pe.wait_ge(xT_made, t - 1)
                for k in range(KC):
                    last = pe.transpose(psT[t % 2][:, k // 3, (k % 3) * P:(k % 3 + 1) * P],
                                        K.xn[:, t, k * P:(k + 1) * P], K.ident[:, :])
                last.then_inc(turned, 1)
            turn(0)
            for t in range(NT):
                if t + 1 < NT:
                    turn(t + 1)
                pe.wait_ge(xT_made, t + 1)
                for k in range(KC):
                    last = pe.matmul(psL[:, t * NE:(t + 1) * NE], xT[:, t % 2, k, :], gw[:, k, :], start=(k == 0),
                                     stop=(k == KC - 1))
                last.then_inc(logits_made, 1)
            pe.wait_ge(chosen, 1)
            selv = sel[:, :, :].rearrange("p t e -> p (t e)")
            pe.matmul(psC[0][:, :], upper[:, :], selv, start=True, stop=True)
            pe.matmul(psC[1][:, :], K.ones[:, :], selv, start=True, stop=True).then_inc(counted, 1)

        @block.scalar
        def _(act):
            for t in range(NT):
                act.wait_ge(turned, t + 1)
                if t >= 2:
                    act.wait_ge(logits_made, t - 1)
                for c in range(2):
                    last = act.activation(xT[:, t % 2, 3 * c:3 * c + 3, :].rearrange("p k n -> p (k n)"),
                                          psT[t % 2][:, c, 0:3 * P], ACT.Copy)
                last.then_inc(xT_made, 1)
            act.wait_ge(exp_ready, 1)
            act.activation(sc[:, :, :], lo[:, :, :], ACT.Exp).then_inc(exp_made, 1)

        @block.vector
        def _(dve):
            step = Chain(dve, stepped)

            def over(x, n):
                return x.rearrange("p (t e) -> p t e", e=1).broadcast_to([P, NT, n])

            dve.wait_ge(logits_made, NT)
            gb = rows[:, 0:1, :].broadcast_to([P, NT, NE])
            step(dve.tensor_tensor(lo[:, :, :], psL[:, :].rearrange("p (t e) -> p t e", e=NE), gb, ALU.add))
            step(dve.tensor_reduce(mx[:, :], lo[:, :, :], AX.X, ALU.max))
            dve.tensor_tensor(lo[:, :, :], lo[:, :, :], over(mx[:, :], NE), ALU.subtract).then_inc(exp_ready, 1)
            dve.wait_ge(exp_made, 1)
            step(dve.tensor_reduce(mx[:, :], sc[:, :, :], AX.X, ALU.add))
            step(dve.reciprocal(mx[:, :], mx[:, :]))
            step(dve.tensor_tensor(sc[:, :, :], sc[:, :, :], over(mx[:, :], NE), ALU.mult))
            step(dve.tensor_tensor(s[:, :, :], sc[:, :, :], rows[:, 1:2, :].broadcast_to([P, NT, NE]), ALU.add))
            s4 = s[:, :, :].rearrange("p t (g a) -> p t g a", a=PER)
            step(dve.tensor_tensor(g[:, :, :], s4[:, :, :, 0], s4[:, :, :, 1], ALU.add))
            dve.wait_ge(iotas, 8)

            def top(x, n, k, low, out):
                for t in range(NT):
                    xj = x[:, t:t + 1, :].broadcast_to([P, n, n])
                    xi = x[:, t, :].rearrange("p (i j) -> p i j", j=1).broadcast_to([P, n, n])
                    dve.tensor_tensor(cmp_[:, t, 0:n, 0:n], xj, xi, ALU.is_gt)
                    last = dve.tensor_tensor(eq[:, t, 0:n, 0:n], xj, xi, ALU.is_equal)
                step(last)
                for t in range(NT):
                    last = dve.tensor_tensor(eq[:, t, 0:n, 0:n], eq[:, t, 0:n, 0:n], low[:, :, :], ALU.mult)
                step(last)
                for t in range(NT):
                    last = dve.tensor_tensor(cmp_[:, t, 0:n, 0:n], cmp_[:, t, 0:n, 0:n], eq[:, t, 0:n, 0:n], ALU.add)
                step(last)
                for t in range(NT):
                    last = dve.tensor_reduce(rank[:, t, 0:n], cmp_[:, t, 0:n, 0:n], AX.X, ALU.add)
                step(last)
                step(dve.tensor_scalar(out, rank[:, :, 0:n], float(k), None, ALU.is_lt))

            top(g, NGRP, TOPG, tri8, c1[:, :, 0:NGRP])
            for a in range(PER):
                step(dve.tensor_scalar(c2[:, :, 0:NGRP], c1[:, :, 0:NGRP], 1.0, BIG, ALU.subtract, ALU.mult))
                step(dve.tensor_tensor(s4[:, :, :, a], s4[:, :, :, a], c1[:, :, 0:NGRP], ALU.mult))
                step(dve.tensor_tensor(s4[:, :, :, a], s4[:, :, :, a], c2[:, :, 0:NGRP], ALU.add))
            top(s, NE, TOPE, tri, sel[:, :, :])
            step(dve.tensor_scalar(valid[:, :], tok[:, :], float(N), None, ALU.is_lt))
            dve.tensor_tensor(sel[:, :, :], sel[:, :, :], over(valid[:, :], NE), ALU.mult).then_inc(chosen, 1)
            dve.wait_ge(chosen, 1)
            src_, n = sel, 1
            for dst_ in (c1, c2, c1, c2):
                dve.tensor_copy(dst_[:, :, 0:n], src_[:, :, 0:n])
                step(dve.tensor_tensor(dst_[:, :, n:NE], src_[:, :, n:NE], src_[:, :, 0:NE - n], ALU.add))
                src_, n = dst_, 2 * n
            dve.wait_ge(counted, 1)
            step(dve.tensor_copy(pos[:, :, :], psC[0][:, :].rearrange("p (t e) -> p t e", e=NE)))
            step(dve.tensor_copy(tot[:, :, :], psC[1][:, :].rearrange("p (t e) -> p t e", e=NE)))


def pair_tables(dve, K, sb, step):
    sc, sel, c1, c2, pos, tot, tok, it = K.sc, K.sel, K.c1, K.c2, K.pos, K.tot, K.tok, K.it
    s = sb("s", [P, NT, NE], F32)
    run = sb("run", [P, NE], F32)
    nt = sb("nt", [P, NE], F32)
    nti = sb("nti", [P, NE], I32)
    zer = sb("zer", [P, NE], F32)
    cum = sb("cum", [P, NE], F32)
    base = sb("base", [P, NE], F32)
    te = sb("te", [P, TM], F32)
    pk = sb("pk", [P, TOPE, NT], F32)
    lane = sb("lane", [P, TOPE, NT], I32)
    new, zt, runs, before, before2, used = (
        sb(x, [P, TM], F32) for x in ("new", "zt", "runs", "before", "before2", "used"))
    lastp = sb("lastp", [P, 1], F32)
    lastp_i = sb("lastp_i", [P, 1], I32)
    step(dve.memset(run[:, :], 0.0))
    for t in range(NT):
        step(dve.tensor_tensor(pos[:, t, :], pos[:, t, :], run[:, :], ALU.add))
        step(dve.tensor_tensor(run[:, :], run[:, :], tot[:, t, :], ALU.add))
    step(dve.tensor_scalar(nti[:, :], run[:, :], float(P - 1), None, ALU.add))
    step(dve.tensor_scalar(nti[:, :], nti[:, :], P.bit_length() - 1, None, ALU.arith_shift_right))
    step(dve.tensor_copy(nt[:, :], nti[:, :]))
    step(dve.memset(zer[:, :], 0.0))
    step(dve.tensor_tensor_scan(cum[:, :], nt[:, :], zer[:, :], 0.0, ALU.add, ALU.add))
    step(dve.tensor_tensor(base[:, :], cum[:, :], nt[:, :], ALU.subtract))
    step(dve.tensor_scalar(base[:, :], base[:, :], float(P), None, ALU.mult))
    step(dve.tensor_tensor(pos[:, :, :], pos[:, :, :],
                           base[:, :].rearrange("p (a e) -> p a e", a=1).broadcast_to([P, NT, NE]), ALU.add))
    step(dve.memset(te[:, :], 0.0))
    for e in range(NE):
        step(dve.scalar_tensor_tensor(out=te[:, :], in0=it[:, :], scalar=cum[:, e:e + 1], in1=te[:, :],
                                      op0=ALU.is_ge, op1=ALU.add))
    step(dve.tensor_scalar(te[:, :], te[:, :], float(NE - 1), None, ALU.min))
    step(dve.tensor_copy(K.tile_expert[:, :], te[:, :]))
    step(dve.memset(new[:, 0:1], 1.0))
    step(dve.tensor_tensor(new[:, 1:TM], te[:, 1:TM], te[:, 0:TM - 1], ALU.not_equal))
    step(dve.memset(zt[:, :], 0.0))
    step(dve.tensor_tensor_scan(runs[:, :], new[:, :], zt[:, :], 0.0, ALU.add, ALU.add))
    step(dve.tensor_tensor(te[:, :], new[:, :], it[:, :], ALU.mult))
    step(dve.tensor_tensor_scan(te[:, :], zt[:, :], te[:, :], 0.0, ALU.add, ALU.max))
    step(dve.memset(before[:, :], 0.0))
    step(dve.tensor_copy(before[:, 1:TM], te[:, 0:TM - 1]))
    step(dve.tensor_tensor(before2[:, :], new[:, :], before[:, :], ALU.mult))
    step(dve.tensor_tensor_scan(before2[:, :], zt[:, :], before2[:, :], 0.0, ALU.add, ALU.max))
    step(dve.memset(before[:, :], 0.0))
    step(dve.tensor_copy(before[:, 1:TM], before2[:, 0:TM - 1]))
    step(dve.tensor_scalar(lastp[:, :], cum[:, NE - 1:NE], 1.0, None, ALU.add))
    step(dve.tensor_copy(lastp_i[:, :], lastp[:, :]))
    step(dve.tensor_scalar(lastp_i[:, :], lastp_i[:, :], 1, None, ALU.arith_shift_right))
    step(dve.tensor_copy(lastp[:, :], lastp_i[:, :]))
    step(dve.tensor_scalar(lastp[:, :], lastp[:, :], 2.0, None, ALU.mult))
    step(dve.tensor_scalar(used[:, :], it[:, :], lastp[:, :], None, ALU.is_lt))
    step(dve.tensor_copy(K.tile_used[:, :], used[:, :]))
    step(dve.tensor_scalar(lastp[:, :], lastp[:, :], 0.5, -1.0, ALU.mult, ALU.add))
    step(dve.tensor_copy(K.last_pair[:, :], lastp[:, :]))
    step(dve.tensor_tensor(new[:, :], new[:, :], used[:, :], ALU.mult))
    step(dve.tensor_copy(K.run_new[:, :], new[:, :]))
    step(dve.tensor_scalar(te[:, :], runs[:, :], float(LOADS), None, ALU.mult))
    step(dve.tensor_copy(K.run_loads[:, :], te[:, :]))
    step(dve.memset(te[:, :], 0.0))
    for r in range(SLOTS, NE + 1, SLOTS):
        step(dve.scalar_tensor_tensor(out=te[:, :], in0=runs[:, :], scalar=float(r), in1=te[:, :],
                                      op0=ALU.is_ge, op1=ALU.add))
    step(dve.scalar_tensor_tensor(out=te[:, :], in0=te[:, :], scalar=-float(SLOTS), in1=runs[:, :],
                                  op0=ALU.mult, op1=ALU.add))
    step(dve.tensor_copy(K.run_slot[:, :], te[:, :]))
    step(dve.tensor_copy(K.run_before[:, :], before[:, :]))
    for q in range(TOPE):
        step(dve.tensor_scalar(c1[:, :, :], c2[:, :, :], float(q + 1), None, ALU.is_equal))
        step(dve.tensor_tensor(c1[:, :, :], c1[:, :, :], sel[:, :, :], ALU.mult))
        step(dve.tensor_tensor(s[:, :, :], c1[:, :, :], pos[:, :, :], ALU.mult))
        step(dve.tensor_reduce(pk[:, q, :], s[:, :, :], AX.X, ALU.add))
        step(dve.tensor_tensor(s[:, :, :], c1[:, :, :], sc[:, :, :], ALU.mult))
        step(dve.tensor_reduce(K.pair_w[:, q, :], s[:, :, :], AX.X, ALU.add))
    step(dve.tensor_scalar(K.pair_w[:, :, :], K.pair_w[:, :, :], SCALE, None, ALU.mult))
    step(dve.tensor_copy(K.pair_row[:, :, :], pk[:, :, :]))
    step(dve.tensor_scalar(lane[:, :, :], K.pair_row[:, :, :], P - 1, None, ALU.bitwise_and))
    step(dve.tensor_scalar(K.pair_at[:, :, :], K.pair_row[:, :, :], P.bit_length() - 1, None,
                           ALU.arith_shift_right))
    step(dve.scalar_tensor_tensor(out=K.pair_at[:, :, :], in0=lane[:, :, :], scalar=float(TM),
                                  in1=K.pair_at[:, :, :], op0=ALU.mult, op1=ALU.add))
    step(dve.tensor_copy(K.token_id[:, :], tok[:, :]))


def load_expert(sp, K, A, n):
    e = sp.value_load(K.tile_expert[0:1, bass.ds(n, 1)], min_val=0, max_val=NE - 1)
    slot = sp.value_load(K.run_slot[0:1, bass.ds(n, 1)], min_val=0, max_val=SLOTS - 1)
    loads = sp.value_load(K.run_loads[0:1, bass.ds(n, 1)], min_val=LOADS, max_val=LOADS * TM)
    sp.wait_ge(K.weights_in, loads)
    sp.nop(nofuse=True)
    for w, dram in ((K.Wu, "Wu"), (K.Wg, "Wg"), (K.Wd, "Wd")):
        sp.dma_start(w[:, bass.ds(slot, 1), :, :].rearrange("p s k n -> p (s k) n"),
                     A["L0_ffn_" + dram][bass.ds(e, 1)].rearrange("e (k p) n -> p (e k) n", p=P))\
          .then_inc(K.weights_in, 16)
    sp.dma_start(K.br[:, bass.ds(slot, 1), :].rearrange("c s n -> c (s n)"),
                 K.bias_tab[bass.ds(e, 1)].rearrange("e c n -> c (e n)")).then_inc(K.weights_in, 16)


def expert_tiles(nc, K, A, name, count, routed):
    C = 2
    with ExitStack() as ctx:
        def sem(n):
            return ctx.enter_context(stage_semaphore(nc, f"{name}_{n}"))

        def sb(n, shape, dt):
            return ctx.enter_context(nc.sbuf_tensor(f"{name}_{n}", shape, dt))
        Wu, Wg, Wd, br = K.Wu, K.Wg, K.Wd, K.br
        weights_in = K.weights_in if routed else K.shared_in
        x_in = [sem(f"x_in{k}") for k in range(2)]
        y_out = [sem(f"y_out{k}") for k in range(2)]
        x_turned, xT_made, up_made, silu_made, act_made, act_turned, actT_made, y_made, y_taken = (
            sem("x_turned"), sem("xT_made"), sem("up_made"), sem("silu_made"), sem("act_made"), sem("act_turned"),
            sem("actT_made"), sem("y_made"), sem("y_taken"))
        scattered, pairs_in, index_set = sem("scattered"), sem("pairs_in"), sem("index_set")
        tables_stepped, tables_made = sem("tables_stepped"), sem("tables_made")
        xe = sb("xe", [P, 2, DM], F32)
        ix = [sb(f"ix{k}", [P, 1], I32) for k in range(2)]
        xT = sb("xT", [P, 2, KC, P], F32)
        su = sb("su", [P, 2, HID], F32)
        aa = sb("aa", [P, 2, HID], F32)
        aT = sb("aT", [P, 2, KH, P], F32)
        y = sb("y", [P, 2, DM], F32)
        psG = [ctx.enter_context(nc.psum_tensor(f"{name}_psG{k}", [P, 512], F32)) for k in range(2)]
        psU = [ctx.enter_context(nc.psum_tensor(f"{name}_psU{k}", [P, 512], F32)) for k in range(2)]
        psX = ctx.enter_context(nc.psum_tensor(f"{name}_psX", [P, 2, 512], F32))
        psY = ctx.enter_context(nc.psum_tensor(f"{name}_psY", [P, 2, 512], F32))
        block = ctx.enter_context(nc.Block())
        half = count // 2
        yrows = K.pair_y if routed else K.shared_y

        @block.sync
        def _(sp):
            def load_x(i):
                for k in range(2):
                    n = 2 * i + k
                    sp.wait_ge(x_turned, n - 1 + C)
                    sp.nop(nofuse=True)
                    sp.dma_start(xe[:, k, :], K.xn_tab[bass.ds(n * P, P), :]).then_inc(x_in[k], 16)

            def load_next_run(n):
                new = sp.value_load(K.run_new[0:1, bass.ds(n, 1)], min_val=0, max_val=1)
                with sp.If(new):
                    before = sp.value_load(K.run_before[0:1, bass.ds(n, 1)], min_val=0, max_val=TM)
                    sp.wait_ge(y_made, before + C)
                    sp.nop(nofuse=True)
                    load_expert(sp, K, A, n)

            if routed:
                with sp.Fori(1, TM) as n:
                    load_next_run(n)
                return
            load_x(0)
            sp.wait_ge(tables_made, 1)
            load_expert(sp, K, A, 0)
            with sp.Fori(1, half) as i:
                load_x(i)

        @block.gpsimd
        def _(pool):
            if not routed:
                pool.wait_ge(tables_made, 1)
                for t in range(NT):
                    m = P if t < NT - 1 else NLAST
                    for q in range(TOPE):
                        pool.indirect_dma_start(K.pair_tab, bass.IndirectOffsetOnAxis(ap=K.pair_at[0:m, q, t:t + 1], axis=0),
                                                K.token_id[0:m, t:t + 1], None).then_inc(scattered, 16)
                pool.wait_ge(scattered, 16 * NT * TOPE)
                pool.dma_start(K.pairs[:, :], K.pair_tab.rearrange("(p k) a -> p (k a)", p=P)).then_inc(pairs_in, 16)
                pool.wait_ge(pairs_in, 16)
                return
            def gather_pair(i):
                for k in range(2):
                    n = 2 * i + k
                    pool.wait_ge(x_turned, n - 1 + C)
                    pool.nop(nofuse=True)
                    pool.tensor_copy(ix[k][:, :], K.pairs[:, bass.ds(n, 1)]).then_inc(index_set, 1)
                    pool.wait_ge(index_set, n + 1)
                    pool.nop(nofuse=True)
                    pool.indirect_dma_start(xe[:, k, :], None, K.xn_tab,
                                            bass.IndirectOffsetOnAxis(ap=ix[k][:, :], axis=0)).then_inc(x_in[k], 16)

            with pool.Fori(0, SURE) as i:
                gather_pair(i)
            with pool.Fori(SURE, half) as i:
                with pool.If(pool.value_load(K.tile_used[0:1, bass.ds(2 * i, 1)], min_val=0, max_val=1)):
                    gather_pair(i)

        def in_pairs(eng, first, step, last):
            def pair(i):
                step(2 * i + 1, 1, i)
                step(2 * i + 2, 0, i + 1)
            first()
            if not routed:
                with eng.Fori(0, half - 1) as i:
                    pair(i)
                last(half - 1)
                return
            with eng.Fori(0, SURE - 1) as i:
                pair(i)
            with eng.Fori(SURE - 1, half - 1) as i:
                with eng.If(eng.value_load(K.tile_used[0:1, bass.ds(2 * i + 2, 1)], min_val=0, max_val=1)):
                    pair(i)
            last(eng.value_load(K.last_pair[0:1, 0:1], min_val=SURE - 1, max_val=half - 1))

        @block.tensor
        def _(pe):
            def turn_x(n, k, it):
                pe.wait_ge(x_in[k], 16 * it + 16)
                pe.nop(nofuse=True)
                for c in range(KC):
                    last = pe.transpose(psX[:, c // 4, (c % 4) * P:(c % 4 + 1) * P], xe[:, k, c * P:(c + 1) * P],
                                        K.ident[:, :])
                last.then_inc(x_turned, 1)

            def slot_of(n):
                if not routed:
                    return 0
                return pe.value_load(K.run_slot[0:1, bass.ds(n, 1)], min_val=0, max_val=SLOTS - 1)

            def product(ps, W, at, k, s):
                pe.matmul(ps[:, :], K.ones3[:, :], br[:, bass.ds(s, 1), at:at + HID], start=True, stop=False)
                for c in range(KC):
                    last = pe.matmul(ps[:, :], xT[:, k, c, :], W[:, bass.ds(s, 1), c, :], start=False,
                                     stop=(c == KC - 1))
                return last

            def gate(n, k, it):
                pe.wait_ge(xT_made, n + 1)
                pe.wait_ge(act_made, n - 1 + C)
                if routed:
                    loads = pe.value_load(K.run_loads[0:1, bass.ds(n, 1)], min_val=LOADS, max_val=LOADS * TM)
                    pe.wait_ge(weights_in, loads + LOADS)
                    pe.nop(nofuse=True)
                s = slot_of(n)
                product(psG[k], Wg, HID, k, s)
                return s

            def up(n, k, s):
                product(psU[k], Wu, 0, k, s).then_inc(up_made, 1)

            def turn_act(n, k):
                pe.wait_ge(act_made, n + 1 + C)
                pe.nop(nofuse=True)
                for c in range(KH):
                    last = pe.transpose(psX[:, 0, c * P:(c + 1) * P], aa[:, k, c * P:(c + 1) * P], K.ident[:, :])
                last.then_inc(act_turned, 1)

            def down(n, k):
                s = slot_of(n)
                pe.wait_ge(actT_made, n + 1)
                pe.wait_ge(y_taken, n + 1)
                pe.nop(nofuse=True)
                for a in range(2):
                    cols = slice(a * HALF, (a + 1) * HALF)
                    pe.matmul(psY[:, a, 0:HALF], K.ones3[:, :], br[:, bass.ds(s, 1), 2 * HID + a * HALF:2 * HID + (a + 1) * HALF],
                              start=True, stop=False)
                    for c in range(KH):
                        last = pe.matmul(psY[:, a, 0:HALF], aT[:, k, c, :], Wd[:, bass.ds(s, 1), c, cols], start=False,
                                         stop=(c == KH - 1))
                last.then_inc(y_made, 1)

            def first():
                turn_x(0, 0, 0)
                if not routed:
                    pe.wait_ge(weights_in, LOADS)
                up(0, 0, gate(0, 0, 0))
                turn_x(1, 1, 0)

            def step(n, k, it):
                s = gate(n, k, it)
                turn_act(n - 1, 1 - k)
                up(n, k, s)
                pe.wait_ge(actT_made, n)
                pe.nop(nofuse=True)
                turn_x(n + 1, 1 - k, it + (1 if k else 0))
                down(n - 1, 1 - k)

            def last(turn):
                n = 2 * turn + 1
                s = gate(n, 1, turn)
                turn_act(n - 1, 0)
                up(n, 1, s)
                down(n - 1, 0)
                turn_act(n, 1)
                down(n, 1)
            in_pairs(pe, first, step, last)

        @block.scalar
        def _(act):
            for k in range(2):
                act.sem_inc(y_out[k], 16)
            act.sem_inc(y_taken, 1)

            def take_x(n, k):
                act.wait_ge(x_turned, n + 1 + C)
                act.nop(nofuse=True)
                act.activation(xT[:, k, 0:4, :].rearrange("p c n -> p (c n)"), psX[:, 0, :], ACT.Copy)
                act.activation(xT[:, k, 4:KC, :].rearrange("p c n -> p (c n)"), psX[:, 1, 0:2 * P], ACT.Copy)\
                   .then_inc(xT_made, 1)

            def silu(n, k):
                act.wait_ge(up_made, n + 1)
                act.nop(nofuse=True)
                act.activation(su[:, k, :], psU[k][:, :], ACT.Silu).then_inc(silu_made, 1)

            def take_y(n, k, it):
                act.wait_ge(y_made, n + 1 + C)
                act.wait_ge(y_out[k], 16 * it + 16)
                act.nop(nofuse=True)
                act.activation(y[:, k, :].rearrange("p (a n) -> p a n", a=2), psY[:, :, 0:HALF], ACT.Copy)\
                   .then_inc(y_taken, 1)
                act.wait_ge(y_taken, n + 2)
                act.nop(nofuse=True)
                act.dma_start(yrows[bass.ds(n * P, P), :], y[:, k, :]).then_inc(y_out[k], 16)

            def first():
                take_x(0, 0)
                silu(0, 0)
                take_x(1, 1)

            def step(n, k, it):
                silu(n, k)
                take_x(n + 1, 1 - k)
                take_y(n - 1, 1 - k, it if k else it - 1)

            def last(turn):
                silu(2 * turn + 1, 1)
                take_y(2 * turn, 0, turn)
                take_y(2 * turn + 1, 1, turn)
                for k in range(2):
                    act.wait_ge(y_out[k], 16 * turn + 32)
                    act.nop(nofuse=True)
            in_pairs(act, first, step, last)

        @block.vector
        def _(dve):
            dve.sem_inc(x_turned, C)
            dve.sem_inc(act_made, C)
            dve.sem_inc(y_made, C)
            if not routed:
                dve.sem_inc(K.weights_in, LOADS)
                step = Chain(dve, tables_stepped)
                pair_tables(dve, K, sb, step)
                dve.engine_nop().then_inc(tables_made, 1)

            def multiply(n, k):
                dve.wait_ge(silu_made, n + 1)
                dve.nop(nofuse=True)
                dve.tensor_tensor(aa[:, k, :], psG[k][:, :], su[:, k, :], ALU.mult).then_inc(act_made, 1)

            def take_act(n, k):
                dve.wait_ge(act_turned, n + 1)
                dve.nop(nofuse=True)
                dve.tensor_copy(aT[:, k, :, :].rearrange("p c n -> p (c n)"), psX[:, 0, :]).then_inc(actT_made, 1)

            def first():
                multiply(0, 0)

            def step(n, k, it):
                take_act(n - 1, 1 - k)
                multiply(n, k)

            def last(turn):
                take_act(2 * turn, 0)
                multiply(2 * turn + 1, 1)
                take_act(2 * turn + 1, 1)
            in_pairs(dve, first, step, last)


def combine(nc, K, A, out):
    D = 4
    with ExitStack() as ctx:
        def sem(n):
            return ctx.enter_context(stage_semaphore(nc, f"comb_{n}"))

        def sb(n, shape, dt):
            return ctx.enter_context(nc.sbuf_tensor(f"comb_{n}", shape, dt))
        gathered = [sem(f"gathered{k}") for k in range(D)]
        shared_in = [sem(f"shared_in{k}") for k in range(D)]
        stepped, tile_made, out_written = sem("stepped"), sem("tile_made"), sem("out_written")
        yq = sb("yq", [P, D, TOPE, DM], F32)
        ys = sb("ys", [P, D, DM], F32)
        block = ctx.enter_context(nc.Block())

        @block.gpsimd
        def _(pool):
            for t in range(NT):
                m = P if t < NT - 1 else NLAST
                if t >= D:
                    pool.wait_ge(tile_made, t - D + 1)
                for q in range(TOPE):
                    pool.indirect_dma_start(yq[0:m, t % D, q, :], None, K.pair_y,
                                            bass.IndirectOffsetOnAxis(ap=K.pair_row[0:m, q, t:t + 1], axis=0))\
                        .then_inc(gathered[t % D], 16)

        @block.sync
        def _(sp):
            for t in range(NT):
                if t >= D:
                    sp.wait_ge(tile_made, t - D + 1)
                sp.dma_start(ys[:, t % D, :], K.shared_y[t * P:(t + 1) * P, :]).then_inc(shared_in[t % D], 16)

        @block.scalar
        def _(act):
            for t in range(NT):
                m = P if t < NT - 1 else NLAST
                act.wait_ge(tile_made, t + 1)
                act.dma_start(out[t * P:t * P + m, :], K.h[0:m, t, :]).then_inc(out_written, 16)
            act.wait_ge(out_written, 16 * NT)

        @block.vector
        def _(dve):
            step = Chain(dve, stepped)
            for t in range(NT):
                m = P if t < NT - 1 else NLAST
                dve.wait_ge(shared_in[t % D], 16 * (t // D + 1))
                dve.wait_ge(gathered[t % D], 16 * TOPE * (t // D + 1))
                acc = ys[0:m, t % D, :]
                for q in range(TOPE):
                    step(dve.scalar_tensor_tensor(out=acc, in0=yq[0:m, t % D, q, :], scalar=K.pair_w[0:m, q, t:t + 1],
                                                  in1=acc, op0=ALU.mult, op1=ALU.add))
                dve.tensor_tensor(K.h[0:m, t, :], K.h[0:m, t, :], acc, ALU.add).then_inc(tile_made, 1)


def ffn(nc, K, A, out):
    K.xn_tab = nc.dram_tensor("xn_table", (NP, DM), F32).ap()
    K.pair_tab = nc.dram_tensor("pair_table", (P * TM, 1), I32).ap()
    K.pair_y = nc.dram_tensor("pair_rows", (TM * P, DM), F32).ap()
    K.shared_y = nc.dram_tensor("shared_rows", (NP, DM), F32).ap()
    with ExitStack() as ctx:
        def sb(n, shape, dt):
            return ctx.enter_context(nc.sbuf_tensor(n, shape, dt))
        K.ones3 = sb("ones3", [3, P], BF16)
        K.tile_expert, K.run_new, K.run_loads, K.run_slot, K.run_before = (
            sb(x, [P, TM], I32) for x in ("tile_expert", "run_new", "run_loads", "run_slot", "run_before"))
        K.sc, K.sel, K.c1, K.c2, K.pos, K.tot = (
            sb(x, [P, NT, NE], F32) for x in ("scores", "chosen", "number_a", "number_b", "places", "totals"))
        K.tok = sb("tokens", [P, NT], F32)
        K.it = sb("tiles", [P, TM], F32)
        K.tile_used = sb("tile_used", [P, TM], I32)
        K.last_pair = sb("last_pair", [P, 1], I32)
        K.pair_w = sb("pair_w", [P, TOPE, NT], F32)
        K.pair_row = sb("pair_row", [P, TOPE, NT], I32)
        K.pair_at = sb("pair_at", [P, TOPE, NT], I32)
        K.token_id = sb("token_id", [P, NT], I32)
        K.pairs = sb("pairs", [P, TM], I32)
        with ExitStack() as c2:
            made = c2.enter_context(stage_semaphore(nc, "ones3_made"))
            block = c2.enter_context(nc.Block())

            @block.vector
            def _(dve):
                dve.memset(K.ones3[:, :], 1.0).then_inc(made, 1)
                dve.wait_ge(made, 1)
        with ExitStack() as c2:
            K.Wu, K.Wg = (c2.enter_context(nc.sbuf_tensor(x, [P, SLOTS, KC, HID], F32)) for x in ("Wu", "Wg"))
            K.Wd = c2.enter_context(nc.sbuf_tensor("Wd", [P, SLOTS, KH, DM], F32))
            K.br = c2.enter_context(nc.sbuf_tensor("bias_rows", [3, SLOTS, BW], BF16))
            K.shared_in = c2.enter_context(stage_semaphore(nc, "shared_weights_in"))
            with ExitStack() as c3:
                K.xn = c3.enter_context(nc.sbuf_tensor("xn", [P, NT, DM], F32))
                norm_block(nc, K, "ln_ffn", K.h, K.xn)
                route(nc, K, A)
            K.weights_in = c2.enter_context(stage_semaphore(nc, "routed_weights_in"))
            expert_tiles(nc, K, A, "shared", NT, False)
            expert_tiles(nc, K, A, "routed", TM, True)
        combine(nc, K, A, out)


def build(nc, A, out):
    RETIRED.clear()
    K = Keep()
    K.srt_src = nc.dram_tensor("sorted_src", (1, ES), I32).ap()
    K.srt_dst = nc.dram_tensor("sorted_dst", (1, ES), I32).ap()
    K.bias_tab = nc.dram_tensor("bias_table", (NE + 1, 3, BW), BF16).ap()
    K.hs_tab = nc.dram_tensor("hs_table", (NP, ROW), F32).ap()
    with ExitStack() as ctx:
        def sb(n, shape, dt):
            return ctx.enter_context(nc.sbuf_tensor(n, shape, dt))
        K.ident = sb("ident", [P, P], F32)
        K.ones = sb("ones", [P, P], F32)
        K.iota_free = sb("iota_free", [P, P], F32)
        K.iota_part = sb("iota_part", [P, 1], F32)
        K.sel_head = sb("sel_head", [P, H], F32)
        K.sel_headT = sb("sel_headT", [H, P], F32)
        K.sel_tile = sb("sel_tile", [P, TPC], F32)
        K.h = sb("h", [P, NT, DM], F32)
        constants(nc, K)
        with ExitStack() as c2:
            x_in = c2.enter_context(nc.sbuf_tensor("x_in", [P, NT, DM], F32))
            first_loads(nc, K, A, x_in)
            norm_block(nc, K, "ln_in", x_in, K.h)
        with ExitStack() as c2:
            K.lnw, K.lnb, K.onw, K.onb = (c2.enter_context(nc.sbuf_tensor(n, [P, DM], F32))
                                          for n in ("ln_w", "ln_b", "on_w", "on_b"))
            gnn(nc, K, A)
            x_again = c2.enter_context(nc.sbuf_tensor("x_again", [P, NT, DM], F32))
            norm_block(nc, K, f"ln{L - 1}", K.h, K.h, K.lnw, K.lnb, also=(K.onw, K.onb, x_again), load=A["x"],
                       load_to=x_again)
        recycle(nc)
        ffn(nc, K, A, out)


_INS = ['x', 'src', 'dst', 'L0_gnn_Wsrc', 'L0_gnn_bsrc', 'L0_gnn_Wdst', 'L0_gnn_bdst', 'L0_gnn_attn', 'L0_gnn_ln_w',
        'L0_gnn_ln_b', 'L0_gnn_on_w', 'L0_gnn_on_b', 'L0_ffn_gate_w', 'L0_ffn_gate_b', 'L0_ffn_bias', 'L0_ffn_Wu',
        'L0_ffn_bu', 'L0_ffn_Wg', 'L0_ffn_bg', 'L0_ffn_Wd', 'L0_ffn_bd', 'L0_ffn_sWu', 'L0_ffn_sbu', 'L0_ffn_sWg',
        'L0_ffn_sbg', 'L0_ffn_sWd', 'L0_ffn_sbd']
_OUTS = [((N, DM), 'float32')]


def kernel(**inputs):
    import numpy as _np
    import concourse.bacc as _bacc
    from concourse import mybir as _mybir
    from concourse.bass_utils import run_bass_kernel_spmd as _run

    nc = _bacc.Bacc("TRN2", target_bir_lowering=False, num_devices=1)
    arrays, args = {}, {}
    for name in _INS:
        a = _np.ascontiguousarray(inputs[name])
        arrays[f"in_{name}_dram"] = a
        args[name] = nc.dram_tensor(f"in_{name}_dram", a.shape, _mybir.dt.from_np(a.dtype), kind="ExternalInput").ap()
    out = nc.dram_tensor("out_0_dram", _OUTS[0][0], _mybir.dt.from_np(_np.dtype(_OUTS[0][1])),
                         kind="ExternalOutput").ap()
    build(nc, args, out)
    r = _run(nc, [arrays], core_ids=[0])
    return r.results[0]["out_0_dram"]
```
